# Optimizing a Trainium2 kernel written in Bass

```python
import numpy as np
import jax
import jax.numpy as jnp

def _softmax(x, axis=-1):
    return jax.nn.softmax(x, axis=axis)

def _gelu(x):
    return jax.nn.gelu(x, approximate=True)

def _silu(x):
    return jax.nn.silu(x)

def _sigmoid(x):
    return jax.nn.sigmoid(x)

def _layernorm(x, axis=-1, eps=1e-05):
    m = jnp.mean(x, axis=axis, keepdims=True)
    v = jnp.var(x, axis=axis, keepdims=True)
    return (x - m) / jnp.sqrt(v + eps)

def _scatter_add(tgt, idx, src, axis=0):
    return tgt.at[idx].add(src)

def _segment_sum(src, seg, n):
    return jax.ops.segment_sum(src, seg, n)
kernel_name = 'mk_decoder_postln_d1_seqx_r4_aa685f'

def setup_inputs(seed: int=0):
    np.random.seed(seed)
    _w = jnp.asarray

    def _rec_inputs():
        import jax
        import jax.numpy as jnp
        _rk = jax.random.key(seed)
        x = -0.0002928 + 1 * jax.random.normal(jax.random.fold_in(_rk, 1), (8, 256, 512), jnp.float32)
        _lenS = 256 - jax.random.randint(jax.random.fold_in(_rk, 7), (8,), 0, max(1, 256 // 4) + 1, jnp.int32)
        _lenS2 = 256 - jax.random.randint(jax.random.fold_in(_rk, 8), (8,), 0, max(1, 256 // 4) + 1, jnp.int32)
        _ctx_2048P = jax.random.normal(jax.random.fold_in(_rk, 11), (8, 16, 512), jnp.float32)
        _ctx_2048c = jax.random.dirichlet(jax.random.fold_in(_rk, 511), 0.3 * jnp.ones((16,), jnp.float32), (8, 256))
        _ctx_2048t = jnp.einsum('bsk,bkd->bsd', _ctx_2048c, _ctx_2048P)
        _ctx_2048t = _ctx_2048t * jax.lax.rsqrt(jnp.mean(jnp.square(_ctx_2048t)) + 1e-12) * 0.953939
        ctx_2048 = -1.39393e-06 + 0.999914 * (_ctx_2048t + 0.3 * jax.random.normal(jax.random.fold_in(_rk, 611), (8, 256, 512), jnp.float32))
        _validS = jnp.arange(256)[None, :] < _lenS[:, None]
        _validS2 = jnp.arange(256)[None, :] < _lenS2[:, None]
        _causal = jnp.tril(jnp.ones((256, 256), dtype=bool))
        mask_Bx1x2048_fk1 = jnp.where(jnp.ones((8, 1, 512), dtype=bool), 1.0, 0.0).astype(jnp.float32)
        return (x, ctx_2048, mask_Bx1x2048_fk1)
    x, ctx_2048, mask_Bx1x2048_fk1 = _rec_inputs()

    def _L0_attn_setup():
        import jax, jax.numpy as jnp
        import numpy as np
        import math
        EMB = 512
        HEADS = 16
        HEAD_DIM = EMB // HEADS
        SCALE = math.sqrt(HEAD_DIM)

        def srms_norm(x, eps_min=1e-12):
            d = x.shape[-1]
            xf = x.astype(jnp.float32)
            norm = jnp.linalg.norm(xf * (1.0 / math.sqrt(d)), axis=-1, keepdims=True)
            norm = jnp.maximum(norm, eps_min)
            return (xf / norm).astype(x.dtype)
        key = jax.random.key(seed)
        ks = jax.random.split(key, 6)
        x = jax.random.normal(ks[0], (4, 1024, EMB), dtype=jnp.float32)
        std = 1.0 / math.sqrt(EMB)
        Wq = jax.random.normal(ks[1], (EMB, EMB), dtype=jnp.float32) * std
        Wk = jax.random.normal(ks[2], (EMB, EMB), dtype=jnp.float32) * std
        Wv = jax.random.normal(ks[3], (EMB, EMB), dtype=jnp.float32) * std
        Wu = jax.random.normal(ks[4], (EMB, EMB), dtype=jnp.float32) * std
        Wo = jax.random.normal(ks[5], (EMB, EMB), dtype=jnp.float32) * std
        return {'x': x, 'Wq': Wq, 'Wk': Wk, 'Wv': Wv, 'Wu': Wu, 'Wo': Wo}
    _L0_attn_all = _L0_attn_setup()
    _L0_attn_in = {k: v for k, v in _L0_attn_all.items() if k in ('Wq', 'Wk', 'Wv', 'Wu', 'Wo')}
    del _L0_attn_all

    def _L0_xattn_setup():
        import math
        import jax, jax.numpy as jnp
        import numpy as np
        SIZE = 256
        HEADS = 16
        HEAD_DIM = SIZE // HEADS
        B, T, S = (2, 512, 512)
        NEG = 1000000.0
        key = jax.random.key(seed)
        ks = jax.random.split(key, 10)
        target = jax.random.normal(ks[0], (B, SIZE, T), dtype=jnp.float32)
        source = jax.random.normal(ks[1], (B, SIZE, S), dtype=jnp.float32)
        target_mask = (jax.random.uniform(ks[2], (B, 1, T)) > 0.1).astype(jnp.float32)
        source_mask = (jax.random.uniform(ks[3], (B, 1, S)) > 0.1).astype(jnp.float32)
        scale = 1.0 / math.sqrt(SIZE)
        Wq = jax.random.normal(ks[4], (SIZE, SIZE), dtype=jnp.float32) * scale
        Wk = jax.random.normal(ks[5], (SIZE, SIZE), dtype=jnp.float32) * scale
        Wv = jax.random.normal(ks[6], (SIZE, SIZE), dtype=jnp.float32) * scale
        bq = jax.random.normal(ks[7], (SIZE,), dtype=jnp.float32) * 0.01
        bk = jax.random.normal(ks[8], (SIZE,), dtype=jnp.float32) * 0.01
        bv = jax.random.normal(ks[9], (SIZE,), dtype=jnp.float32) * 0.01
        return {'target': target, 'source': source, 'target_mask': target_mask, 'source_mask': source_mask, 'Wq': Wq, 'bq': bq, 'Wk': Wk, 'bk': bk, 'Wv': Wv, 'bv': bv}
    _L0_xattn_all = _L0_xattn_setup()
    _L0_xattn_in = {k: v for k, v in _L0_xattn_all.items() if k in ('Wq', 'bq', 'Wk', 'bk', 'Wv', 'bv')}
    del _L0_xattn_all

    def _L0_ffn_setup():
        import jax, jax.numpy as jnp
        import numpy as np
        ALPHA = 1.702
        LIMIT = 7.0
        TOP_K = 4
        B, S, H = (1, 256, 512)
        E, D = (16, 512)
        key = jax.random.key(seed)
        ks = jax.random.split(key, 7)
        s = 0.02
        return {'hidden_states': jax.random.normal(ks[0], (B, S, H), dtype=jnp.float32), 'router_weight': jax.random.normal(ks[1], (E, H), dtype=jnp.float32) * s, 'router_bias': jax.random.normal(ks[2], (E,), dtype=jnp.float32) * s, 'gate_up_proj': jax.random.normal(ks[3], (E, H, 2 * D), dtype=jnp.float32) * s, 'gate_up_proj_bias': jax.random.normal(ks[4], (E, 2 * D), dtype=jnp.float32) * s, 'down_proj': jax.random.normal(ks[5], (E, D, H), dtype=jnp.float32) * s, 'down_proj_bias': jax.random.normal(ks[6], (E, H), dtype=jnp.float32) * s}
    _L0_ffn_all = _L0_ffn_setup()
    _L0_ffn_in = {k: v for k, v in _L0_ffn_all.items() if k in ('router_weight', 'router_bias', 'gate_up_proj', 'gate_up_proj_bias', 'down_proj', 'down_proj_bias')}
    del _L0_ffn_all
    return {'x': x, 'ctx_2048': ctx_2048, 'mask_Bx1x2048_fk1': mask_Bx1x2048_fk1, 'L0_attn_Wq': _L0_attn_in['Wq'], 'L0_attn_Wk': _L0_attn_in['Wk'], 'L0_attn_Wv': _L0_attn_in['Wv'], 'L0_attn_Wu': _L0_attn_in['Wu'], 'L0_attn_Wo': _L0_attn_in['Wo'], 'L0_xattn_Wq': _L0_xattn_in['Wq'], 'L0_xattn_bq': _L0_xattn_in['bq'], 'L0_xattn_Wk': _L0_xattn_in['Wk'], 'L0_xattn_bk': _L0_xattn_in['bk'], 'L0_xattn_Wv': _L0_xattn_in['Wv'], 'L0_xattn_bv': _L0_xattn_in['bv'], 'L0_ffn_router_weight': _L0_ffn_in['router_weight'], 'L0_ffn_router_bias': _L0_ffn_in['router_bias'], 'L0_ffn_gate_up_proj': _L0_ffn_in['gate_up_proj'], 'L0_ffn_gate_up_proj_bias': _L0_ffn_in['gate_up_proj_bias'], 'L0_ffn_down_proj': _L0_ffn_in['down_proj'], 'L0_ffn_down_proj_bias': _L0_ffn_in['down_proj_bias']}

def reference(x, ctx_2048, mask_Bx1x2048_fk1, L0_attn_Wq, L0_attn_Wk, L0_attn_Wv, L0_attn_Wu, L0_attn_Wo, L0_xattn_Wq, L0_xattn_bq, L0_xattn_Wk, L0_xattn_bk, L0_xattn_Wv, L0_xattn_bv, L0_ffn_router_weight, L0_ffn_router_bias, L0_ffn_gate_up_proj, L0_ffn_gate_up_proj_bias, L0_ffn_down_proj, L0_ffn_down_proj_bias):
    import jax
    import jax.numpy as jnp

    def _L0_attn_ref(x, Wq, Wk, Wv, Wu, Wo):
        import jax, jax.numpy as jnp
        import numpy as np
        import math
        EMB = 512
        HEADS = 16
        HEAD_DIM = EMB // HEADS
        SCALE = math.sqrt(HEAD_DIM)

        def srms_norm(x, eps_min=1e-12):
            d = x.shape[-1]
            xf = x.astype(jnp.float32)
            norm = jnp.linalg.norm(xf * (1.0 / math.sqrt(d)), axis=-1, keepdims=True)
            norm = jnp.maximum(norm, eps_min)
            return (xf / norm).astype(x.dtype)
        B, L, D = x.shape
        H, dh = (HEADS, HEAD_DIM)
        q = (x @ Wq).reshape(B, L, H, dh).transpose(0, 2, 1, 3)
        k = (x @ Wk).reshape(B, L, H, dh).transpose(0, 2, 1, 3)
        v = (x @ Wv).reshape(B, L, H, dh).transpose(0, 2, 1, 3)
        u = (x @ Wu).reshape(B, L, H, dh).transpose(0, 2, 1, 3)
        q = jax.nn.relu(q) / SCALE
        k = jax.nn.relu(k) / SCALE
        u = jax.nn.silu(u)
        kv = jnp.einsum('bhlk,bhlv->bhkv', k, v)
        out = jnp.einsum('bhlk,bhkv->bhlv', q, kv)
        out = srms_norm(out) * u
        out = out.transpose(0, 2, 1, 3).reshape(B, L, D)
        return out @ Wo

    def _L0_xattn_ref(target, source, target_mask, source_mask, Wq, bq, Wk, bk, Wv, bv):
        import math
        import jax, jax.numpy as jnp
        import numpy as np
        SIZE = 256
        HEADS = 16
        HEAD_DIM = SIZE // HEADS
        B, T, S = (2, 512, 512)
        NEG = 1000000.0
        b, _, t = target.shape
        s = source.shape[-1]
        q = jnp.einsum('oc,bct->bot', Wq, target) + bq[None, :, None]
        k = jnp.einsum('oc,bcs->bos', Wk, source) + bk[None, :, None]
        v = jnp.einsum('oc,bcs->bos', Wv, source) + bv[None, :, None]
        q = q.reshape(b, HEADS, HEAD_DIM, t)
        k = k.reshape(b, HEADS, HEAD_DIM, s)
        v = v.reshape(b, HEADS, HEAD_DIM, s)
        dot = jnp.einsum('bhdt,bhds->bhts', q, k) / math.sqrt(HEAD_DIM)
        mask = target_mask[:, :, :, None] * source_mask[:, :, None, :]
        dot = mask * dot - (1.0 - mask) * NEG
        amap = jax.nn.softmax(dot, axis=-1) * mask
        out = jnp.einsum('bhts,bhds->bhdt', amap, v)
        return out.reshape(b, HEADS * HEAD_DIM, t)

    def _L0_ffn_ref(hidden_states, router_weight, router_bias, gate_up_proj, gate_up_proj_bias, down_proj, down_proj_bias):
        import jax, jax.numpy as jnp
        import numpy as np
        ALPHA = 1.702
        LIMIT = 7.0
        TOP_K = 4
        B, S, H = (1, 256, 512)
        E, D = (16, 512)
        batch, seq, hdim = hidden_states.shape
        x = hidden_states.reshape(-1, hdim)
        T = x.shape[0]
        logits = x @ router_weight.T + router_bias
        top_val, top_idx = jax.lax.top_k(logits, TOP_K)
        top_val = jax.nn.softmax(top_val, axis=-1)
        router_scores = jnp.zeros_like(logits).at[jnp.arange(T)[:, None], top_idx].set(top_val)
        gate_up = jnp.einsum('th,ehd->etd', x, gate_up_proj) + gate_up_proj_bias[:, None, :]
        gate = gate_up[..., ::2]
        up = gate_up[..., 1::2]
        gate = jnp.minimum(gate, LIMIT)
        up = jnp.clip(up, -LIMIT, LIMIT)
        glu = gate * jax.nn.sigmoid(gate * ALPHA)
        out = jnp.einsum('etd,edh->eth', (up + 1.0) * glu, down_proj) + down_proj_bias[:, None, :]
        out = out * router_scores.T[:, :, None]
        out = out.sum(axis=0)
        return out.reshape(batch, seq, hdim)
    x = _layernorm(x + _L0_attn_ref(x, L0_attn_Wq, L0_attn_Wk, L0_attn_Wv, L0_attn_Wu, L0_attn_Wo), axis=-1)
    x = _layernorm(x + _L0_xattn_ref(x, ctx_2048, mask_Bx1x2048_fk1, mask_Bx1x2048_fk1, L0_xattn_Wq, L0_xattn_bq, L0_xattn_Wk, L0_xattn_bk, L0_xattn_Wv, L0_xattn_bv), axis=-1)
    x = _layernorm(x + _L0_ffn_ref(x, L0_ffn_router_weight, L0_ffn_router_bias, L0_ffn_gate_up_proj, L0_ffn_gate_up_proj_bias, L0_ffn_down_proj, L0_ffn_down_proj_bias), axis=-1)
    return x

_drawn_inputs = setup_inputs


def setup_inputs(seed=0):
    import zlib

    import numpy as np

    out = dict(_drawn_inputs(seed))
    spreads = {}
    factors = {'L0_xattn_bq': 59.405,
     'L0_xattn_bk': 64.0,
     'L0_xattn_bv': 64.0,
     'L0_ffn_router_bias': 5.278,
     'L0_ffn_gate_up_proj_bias': 8.0,
     'L0_ffn_down_proj_bias': 5.504}
    for name, (base, spread) in spreads.items():
        noise = np.random.default_rng([zlib.crc32(name.encode()), seed]).standard_normal(out[name].shape)
        drawn = base * np.exp(spread * noise) if base else spread * noise
        out[name] = jnp.asarray(drawn.astype(out[name].dtype))
    for name, factor in factors.items():
        out[name] = (out[name] * factor).astype(out[name].dtype)
    return out
```

```python
from contextlib import ExitStack

import concourse.bass as bass
from concourse import mybir

F32 = mybir.dt.float32
F32R = mybir.dt.float32r
BF16 = mybir.dt.bfloat16
I32 = mybir.dt.int32
U32 = mybir.dt.uint32
ALU = mybir.AluOpType
ACT = mybir.ActivationFunctionType
AX = mybir.AxisListType

P = 128
B, L, D = 8, 256, 512
TOK = B * L
NT = TOK // P
KC = D // P
LN_EPS = 1e-5
SPLITS = ((0, 0), (0, 1), (1, 0))


def scaled(count, group, offset):
    return group * count + offset


def spare_registers(engine, name, n):
    return [engine.alloc_register(name=f"{name}_{i}") for i in range(n)]


def wait_apart(engine, registers, constant, *waits):
    values = []
    for (_, value), register in zip(waits, registers):
        if not isinstance(value, int):
            engine.reg_mov(register, value)
            value = register
        values.append(value)
    engine.wait_ge(*constant)
    for (semaphore, _), value in zip(waits, values):
        engine.wait_ge(semaphore, value)


def linear_attention(nc, A, x1):
    H, DH = 16, 32
    INV_SCALE = DH ** -0.5
    NG, TPG = 4, 4
    GT = TPG * P
    WQ, WK, WV, WU, WO = range(5)
    with ExitStack() as ctx:
        def sb(name, shape, dt=F32):
            return ctx.enter_context(nc.sbuf_tensor(name, shape, dt))

        def sem(name):
            return ctx.enter_context(nc.semaphore(name))

        w_raw = sb("w_raw", [P, 2, KC, D])
        w_split = sb("w_split", [P, 5, 2, KC, D], F32R)
        xT_raw = sb("xT_raw", [P, KC, GT])
        xT_split = sb("xT_split", [P, 2, KC, GT], F32R)
        x_tok = sb("x_tok", [P, 2, D])
        qT = sb("qT", [P, KC, GT])
        k_sb = sb("k_sb", [P, TPG, D])
        v_sb = sb("v_sb", [P, TPG, D])
        u_sb = sb("u_sb", [P, TPG, D])
        kv_mask = sb("kv_mask", [P, P])
        kv_sb = sb("kv_sb", [P, KC, P])
        ident = sb("ident1", [P, P])
        o_sq = sb("o_sq", [P, D])
        o_ss = sb("o_ss", [P, H])
        o_rn = sb("o_rn", [P, H])
        o_norm = sb("o_norm", [P, D])
        o_sb = sb("o_sb", [P, D])
        oT_split = sb("oT_split", [P, 2, KC, P], F32R)
        y_sb = sb("y_sb", [P, D])
        stats = sb("stats", [P, 6])
        mean_var = sb("mean_var", [P, 2])
        rstd = sb("rstd", [P, 1])
        minus_half = sb("minus_half", [P, H])

        def bank(name):
            return ctx.enter_context(nc.psum_tensor(name, [P, D], F32))

        ps_q0, ps_k, ps_v, ps_u = bank("ps_q0"), bank("ps_k"), bank("ps_v"), bank("ps_u")
        ps_kv, ps_o, ps_t, ps_w = bank("ps_kv"), bank("ps_o"), bank("ps_t"), bank("ps_w")
        q_banks = [ps_k, ps_v, ps_u, ps_q0]

        w_loaded = [sem("w_loaded_even"), sem("w_loaded_odd")]
        consts_loaded = sem("consts_loaded")
        w_hi = sem("w_hi")
        w_lo = sem("w_lo")
        xT_loaded = sem("xT_loaded")
        xT_hi = sem("xT_hi")
        xT_lo = sem("xT_lo")
        x_loaded = [sem("x_loaded_even"), sem("x_loaded_odd")]
        q_made, q_kept = sem("q_made"), sem("q_kept")
        proj_made = sem("proj_made")
        k_kept, v_kept, u_kept = sem("k_kept"), sem("v_kept"), sem("u_kept")
        kv_made, kv_kept = sem("kv_made"), sem("kv_kept")
        o_made, o_squared, o_summed, o_scale, o_normed, o_gated = (
            sem("o_made"), sem("o_squared"), sem("o_summed"), sem("o_scale"), sem("o_normed"), sem("o_gated"))
        t_made, t_hi, t_lo = sem("t_made"), sem("t_hi"), sem("t_lo")
        y_made, y_added, y_stats, y_moments, y_rstd, x1_made = (
            sem("y_made"), sem("y_added"), sem("y_stats"), sem("y_moments"), sem("y_rstd"), sem("x1_made"))
        half_set, pool_step, clamp = sem("half_set"), sem("pool_step"), sem("clamp")

        block = ctx.enter_context(nc.Block())

        @block.sync
        def _(sp):
            sp.dma_start(kv_mask[:], A["kv_mask"]).then_inc(consts_loaded, 16)
            sp.dma_start(ident[:], A["ident"]).then_inc(consts_loaded, 16)

            def load_w(w):
                if w >= 2:
                    sp.wait_ge(w_lo, w - 1)
                sp.dma_start(w_raw[:, w % 2], A["w1"][w]).then_inc(w_loaded[w % 2], 16)

            load_w(WQ)
            load_w(WK)
            sp.dma_start(xT_raw[:], A["xT"][:, :, 0:GT]).then_inc(xT_loaded, 16)
            for w in (WV, WU, WO):
                load_w(w)

            with sp.Fori(1, NG) as g:
                sp.wait_ge(xT_lo, TPG * g)
                sp.dma_start(xT_raw[:], A["xT"][:, :, bass.ds(g * GT, GT)]).then_inc(xT_loaded, 16)

        @block.gpsimd
        def _(pool):
            nc.gpsimd.memset(minus_half[:], -0.5).then_inc(half_set, 1)
            pool.wait_ge(half_set, 1)

            def split_x(g, i):
                pool.wait_ge(xT_hi, TPG * g + i + 1)
                cols = slice(i * P, i * P + P)
                nc.gpsimd.tensor_tensor(xT_split[:, 1, :, cols], xT_raw[:, :, cols],
                                        xT_split[:, 0, :, cols].bitcast(F32), ALU.subtract).then_inc(xT_lo, 1)

            for w in range(5):
                pool.wait_ge(w_hi, w + 1)
                if w == 1:
                    for i in range(TPG):
                        split_x(0, i)
                nc.gpsimd.tensor_tensor(w_split[:, w, 1], w_raw[:, w % 2], w_split[:, w, 0].bitcast(F32),
                                        ALU.subtract).then_inc(w_lo, 1)

            def head_scale(t):
                pool.wait_ge(o_summed, t + 1)
                nc.gpsimd.tensor_tensor(o_rn[:], o_ss[:], minus_half[:], ALU.pow).then_inc(o_scale, 1)

            def gate(t, slot):
                pool.wait_ge(o_normed, t + 1)
                pool.wait_ge(u_kept, t + 1)
                if not (isinstance(t, int) and t < 1):
                    pool.wait_ge(t_made, t)
                nc.gpsimd.tensor_tensor(o_sb[:], o_norm[:], u_sb[:, slot], ALU.mult).then_inc(o_gated, 1)

            def token_rstd(t):
                pool.wait_ge(y_moments, t + 1)
                nc.gpsimd.tensor_tensor(rstd[:], mean_var[:, 1:2], minus_half[:, 0:1], ALU.pow).then_inc(y_rstd, 1)

            def load_x(t, slot):
                if not (isinstance(t, int) and t < 2):
                    pool.wait_ge(y_added, t - 1)
                pool.dma_start(x_tok[:, slot], A["x"][bass.ds(t * P, P), :]).then_inc(x_loaded[slot], 16)

            def group(g, first, last):
                t = TPG * g
                if first:
                    load_x(0, 0)
                    load_x(1, 1)
                else:
                    head_scale(t - 1)
                    gate(t - 1, 3)
                    token_rstd(t - 2)
                    load_x(t, 0)
                    token_rstd(t - 1)
                    load_x(t + 1, 1)
                if not last:
                    split_x(g + 1, 0)
                    split_x(g + 1, 1)
                head_scale(t)
                gate(t, 0)
                head_scale(t + 1)
                if not last:
                    split_x(g + 1, 2)
                gate(t + 1, 1)
                token_rstd(t)
                load_x(t + 2, 0)
                token_rstd(t + 1)
                load_x(t + 3, 1)
                if not last:
                    split_x(g + 1, 3)
                head_scale(t + 2)
                gate(t + 2, 2)

            group(0, True, False)
            with pool.Fori(1, NG - 1) as g:
                group(g, False, False)
            group(NG - 1, False, True)
            head_scale(NT - 1)
            gate(NT - 1, 3)
            token_rstd(NT - 2)
            token_rstd(NT - 1)

        @block.scalar
        def _(act):
            def split_w(w):
                act.wait_ge(w_loaded[w % 2], 16 * (w // 2 + 1))
                nc.scalar.activation(w_split[:, w, 0], w_raw[:, w % 2], ACT.Copy).then_inc(w_hi, 1)

            def split_x(g, i, first=False):
                act.wait_ge(xT_loaded, 16 * g + 16)
                if not first:
                    act.wait_ge(proj_made, 3 * (TPG * (g - 1) + i + 1))
                cols = slice(i * P, i * P + P)
                nc.scalar.activation(xT_split[:, 0, :, cols], xT_raw[:, :, cols], ACT.Copy).then_inc(xT_hi, 1)

            def q_block(g, m):
                act.wait_ge(q_made, KC * g + m + 1)
                nc.scalar.activation(qT[:, m], q_banks[m][:], ACT.Relu, scale=INV_SCALE).then_inc(q_kept, 1)

            def keep_k(t, slot):
                act.wait_ge(proj_made, 3 * t + 1)
                nc.scalar.activation(k_sb[:, slot], ps_k[:], ACT.Relu, scale=INV_SCALE).then_inc(k_kept, 1)

            def keep_u(t, slot):
                act.wait_ge(proj_made, 3 * t + 3)
                nc.scalar.activation(u_sb[:, slot], ps_u[:], ACT.Silu).then_inc(u_kept, 1)

            def square(t, o_bank):
                act.wait_ge(o_made, t + 1)
                if not (isinstance(t, int) and t < 1):
                    act.wait_ge(o_summed, t)
                nc.scalar.activation(o_sq[:], o_bank[:], ACT.Square).then_inc(o_squared, 1)

            def keep_oT(t):
                act.wait_ge(t_made, t + 1)
                if not (isinstance(t, int) and t < 1):
                    act.wait_ge(y_made, t)
                nc.scalar.activation(oT_split[:, 0], ps_t[:].rearrange("p (c t) -> p c t", c=KC),
                                     ACT.Copy).then_inc(t_hi, 1)

            def group(g, first, last):
                t = TPG * g
                if not first:
                    square(t - 1, ps_q0)
                q_block(g, 0)
                q_block(g, 1)
                if not first:
                    keep_oT(t - 2)
                q_block(g, 2)
                if not first:
                    keep_oT(t - 1)
                q_block(g, 3)
                keep_k(t, 0)
                keep_u(t, 0)
                if not last:
                    split_x(g + 1, 0)
                keep_k(t + 1, 1)
                keep_u(t + 1, 1)
                if not last:
                    split_x(g + 1, 1)
                square(t, ps_o)
                keep_k(t + 2, 2)
                square(t + 1, ps_q0)
                keep_u(t + 2, 2)
                if not last:
                    split_x(g + 1, 2)
                keep_oT(t)
                keep_k(t + 3, 3)
                keep_oT(t + 1)
                keep_u(t + 3, 3)
                if not last:
                    split_x(g + 1, 3)
                square(t + 2, ps_o)

            split_w(WQ)
            split_w(WK)
            for i in range(TPG):
                split_x(0, i, True)
            for w in (WV, WU, WO):
                split_w(w)
            group(0, True, False)
            with act.Fori(1, NG - 1) as g:
                group(g, False, False)
            group(NG - 1, False, True)
            square(NT - 1, ps_q0)
            keep_oT(NT - 2)
            keep_oT(NT - 1)

        @block.vector
        def _(dve):
            held = spare_registers(dve, "held1", 1)

            def keep_v(t, slot):
                dve.wait_ge(proj_made, 3 * t + 2)
                nc.vector.tensor_copy(v_sb[:, slot], ps_v[:]).then_inc(v_kept, 1)

            def keep_kv(b):
                dve.wait_ge(kv_made, b + 1)
                if not (isinstance(b, int) and b < 1):
                    dve.wait_ge(o_made, 2 * b)
                nc.vector.tensor_tensor(kv_sb[:], ps_kv[:].rearrange("p (c v) -> p c v", c=KC),
                                        kv_mask[:].unsqueeze(1).to_broadcast([P, KC, P]),
                                        ALU.mult).then_inc(kv_kept, 1)

            def norm(t, o_bank):
                dve.wait_ge(o_squared, t + 1)
                if not (isinstance(t, int) and t < 1):
                    dve.wait_ge(o_scale, t)
                nc.vector.tensor_reduce(o_ss[:], o_sq[:].rearrange("p (h d) -> p h d", h=H), AX.X,
                                        ALU.add).then_inc(clamp, 1)
                dve.wait_ge(clamp, t + 1)
                nc.vector.tensor_scalar(o_ss[:], o_ss[:], 1.0 / DH, 1e-24, ALU.mult, ALU.max).then_inc(o_summed, 1)
                dve.wait_ge(o_scale, t + 1)
                if not (isinstance(t, int) and t < 1):
                    dve.wait_ge(o_gated, t)
                nc.vector.tensor_tensor(o_norm[:].rearrange("p (h d) -> p h d", h=H),
                                        o_bank[:].rearrange("p (h d) -> p h d", h=H),
                                        o_rn[:].unsqueeze(2).to_broadcast([P, H, DH]),
                                        ALU.mult).then_inc(o_normed, 1)

            def keep_oT(t):
                dve.wait_ge(t_hi, t + 1)
                nc.vector.tensor_tensor(oT_split[:, 1], ps_t[:].rearrange("p (c t) -> p c t", c=KC),
                                        oT_split[:, 0].bitcast(F32), ALU.subtract).then_inc(t_lo, 1)

            def layernorm(t, slot):
                dve.wait_ge(y_made, t + 1)
                dve.wait_ge(x_loaded[slot], 8 * (t - slot) + 16)
                nc.vector.tensor_tensor(y_sb[:], ps_w[:], x_tok[:, slot], ALU.add).then_inc(y_added, 1)
                dve.wait_ge(y_added, t + 1)
                nc.vector.bn_stats(stats[:], y_sb[:]).then_inc(y_stats, 1)
                wait_apart(dve, held, (half_set, 1), (y_stats, 3 * t + 1))
                nc.vector.bn_aggr(mean_var[:], stats[:]).then_inc(y_stats, 1)
                dve.wait_ge(y_stats, 3 * t + 2)
                nc.vector.tensor_scalar(mean_var[:, 1:2], mean_var[:, 1:2], LN_EPS, None,
                                        ALU.add).then_inc(y_moments, 1)
                dve.wait_ge(y_rstd, t + 1)
                nc.vector.tensor_scalar(x1[:, bass.ds(t, 1), :].squeeze(1) if not isinstance(t, int) else x1[:, t, :],
                                        y_sb[:], mean_var[:, 0:1], rstd[:, 0:1],
                                        ALU.subtract, ALU.mult).then_inc(y_stats, 1)

            def group(g, first):
                t = TPG * g
                if not first:
                    norm(t - 1, ps_q0)
                    keep_oT(t - 2)
                    layernorm(t - 2, 0)
                    keep_oT(t - 1)
                    layernorm(t - 1, 1)
                keep_v(t, 0)
                keep_v(t + 1, 1)
                keep_kv(2 * g)
                norm(t, ps_o)
                keep_v(t + 2, 2)
                norm(t + 1, ps_q0)
                keep_oT(t)
                layernorm(t, 0)
                keep_v(t + 3, 3)
                keep_oT(t + 1)
                keep_kv(2 * g + 1)
                layernorm(t + 1, 1)
                norm(t + 2, ps_o)

            dve.wait_ge(consts_loaded, 32)
            dve.wait_ge(half_set, 1)
            group(0, True)
            with dve.Fori(1, NG) as g:
                group(g, False)
            keep_oT(NT - 2)
            norm(NT - 1, ps_q0)
            layernorm(NT - 2, 0)
            keep_oT(NT - 1)
            layernorm(NT - 1, 1)

        @block.tensor
        def _(pe):
            def q_block(g, m, first):
                if m == 0:
                    pe.wait_ge(xT_lo, TPG * g + TPG)
                if first:
                    pe.wait_ge(w_lo, 1)
                else:
                    pe.wait_ge([k_kept, v_kept, u_kept, o_normed][m], TPG * g)
                n = 0
                for wi, xi in SPLITS:
                    for c in range(KC):
                        mm = nc.tensor.matmul(q_banks[m][:], w_split[:, WQ, wi, c, m * P:(m + 1) * P],
                                              xT_split[:, xi, c, :], start=(n == 0), stop=(n == 3 * KC - 1))
                        n += 1
                mm.then_inc(q_made, 1)

            def project(g, i, w, first):
                t = TPG * g + i
                if first and i == 0:
                    pe.wait_ge(w_lo, w + 1)
                if w == WK:
                    pe.wait_ge(q_kept, KC * g + 1) if i == 0 else pe.wait_ge(k_kept, t)
                elif w == WV:
                    pe.wait_ge(q_kept, KC * g + 2) if i == 0 else pe.wait_ge(v_kept, t)
                else:
                    pe.wait_ge(q_kept, KC * g + 3) if i == 0 else pe.wait_ge(u_kept, t)
                out = {WK: ps_k, WV: ps_v, WU: ps_u}[w]
                n = 0
                for wi, xi in SPLITS:
                    for c in range(KC):
                        mm = nc.tensor.matmul(out[:], xT_split[:, xi, c, i * P:(i + 1) * P],
                                              w_split[:, w, wi, c, :], start=(n == 0), stop=(n == 3 * KC - 1))
                        n += 1
                mm.then_inc(proj_made, 1)

            def kv(b, slot):
                pe.wait_ge(k_kept, 2 * b + 2)
                pe.wait_ge(v_kept, 2 * b + 2)
                if not (isinstance(b, int) and b < 1):
                    pe.wait_ge(kv_kept, b)
                for c in range(KC):
                    for i in range(2):
                        mm = nc.tensor.matmul(ps_kv[:, c * P:(c + 1) * P], k_sb[:, slot + i, c * P:(c + 1) * P],
                                              v_sb[:, slot + i, c * P:(c + 1) * P], start=(i == 0), stop=(i == 1))
                mm.then_inc(kv_made, 1)

            def attend(g, i, o_bank, first):
                t = TPG * g + i
                if i == 0:
                    pe.wait_ge(q_kept, KC * g + 4)
                    pe.wait_ge(kv_kept, 2 * g + 1)
                if i == 2:
                    pe.wait_ge(kv_kept, 2 * g + 2)
                    pe.wait_ge(o_normed, t - 1)
                elif i == 3:
                    pe.wait_ge(o_normed, t - 1)
                elif i == 0 and not first:
                    pe.wait_ge(o_normed, t - 1)
                for c in range(KC):
                    mm = nc.tensor.matmul(o_bank[:, c * P:(c + 1) * P], qT[:, c, i * P:(i + 1) * P],
                                          kv_sb[:, c, :], start=True, stop=True)
                mm.then_inc(o_made, 1)

            def transpose_o(t):
                pe.wait_ge(o_gated, t + 1)
                if not (isinstance(t, int) and t < 1):
                    pe.wait_ge(t_lo, t)
                for c in range(KC):
                    mm = nc.tensor.transpose(ps_t[:, c * P:(c + 1) * P], o_sb[:, c * P:(c + 1) * P], ident[:])
                mm.then_inc(t_made, 1)

            def project_out(t):
                pe.wait_ge(t_lo, t + 1)
                if isinstance(t, int) and t < 1:
                    pe.wait_ge(w_lo, WO + 1)
                else:
                    pe.wait_ge(y_added, t)
                n = 0
                for wi, oi in SPLITS:
                    for c in range(KC):
                        mm = nc.tensor.matmul(ps_w[:], oT_split[:, oi, c, :], w_split[:, WO, wi, c, :],
                                              start=(n == 0), stop=(n == 3 * KC - 1))
                        n += 1
                mm.then_inc(y_made, 1)

            def group(g, first):
                t = TPG * g
                q_block(g, 0, first)
                q_block(g, 1, first)
                if not first:
                    transpose_o(t - 2)
                q_block(g, 2, first)
                if not first:
                    project_out(t - 2)
                    transpose_o(t - 1)
                q_block(g, 3, first)
                if not first:
                    project_out(t - 1)
                project(g, 0, WK, first)
                project(g, 0, WV, first)
                project(g, 0, WU, first)
                project(g, 1, WK, first)
                project(g, 1, WV, first)
                project(g, 1, WU, first)
                kv(2 * g, 0)
                project(g, 2, WK, first)
                attend(g, 0, ps_o, first)
                attend(g, 1, ps_q0, first)
                project(g, 2, WV, first)
                project(g, 2, WU, first)
                transpose_o(t)
                project(g, 3, WK, first)
                project_out(t)
                project(g, 3, WV, first)
                transpose_o(t + 1)
                kv(2 * g + 1, 2)
                project(g, 3, WU, first)
                project_out(t + 1)
                attend(g, 2, ps_o, first)
                attend(g, 3, ps_q0, first)

            pe.wait_ge(consts_loaded, 32)
            group(0, True)
            with pe.Fori(1, NG) as g:
                group(g, False)
            transpose_o(NT - 2)
            project_out(NT - 2)
            transpose_o(NT - 1)
            project_out(NT - 1)
def cross_attention(nc, A, S, x):
    H, DH, C, T = 16, 16, 2 * P, D
    NQ, HQ, NC = 4, 4, T // P
    PENALTY = 4e6
    ROWS_A, ROWS_B = 6 * DH + 9, 6 * DH + 12
    STEPS = NQ * NC
    MISC0, MISC = 7, 10
    STACK_DMAS = 8
    with ExitStack() as ctx:
        def sb(name, shape, dt=F32):
            return ctx.enter_context(nc.sbuf_tensor(name, shape, dt))

        def sem(name):
            return ctx.enter_context(nc.semaphore(name))

        w2 = sb("w2", [P, 3, 2, C])
        bias_qk = sb("bias_qk", [P, 2, 2])
        bias_v = sb("bias_v", [P, C])
        mask_col = sb("mask_col", [P, B, NC])
        mask_now = sb("mask_now", [P, NC])
        ident = sb("ident2", [P, P])
        m_rows = sb("m_rows", [B, T])
        pen_rows = sb("pen_rows", [B, T])
        rest_rows = sb("rest_rows", [B, T])
        row_parts = sb("row_parts", [B, 7, T], BF16)
        ctx_sb = sb("ctx_sb", [P, 2, T])
        mask_in = sb("mask_in", [P, T])
        mask_out = sb("mask_out", [P, T])
        full = sb("full", [P, 2, T])
        rest = sb("rest", [P, 2, T])
        parts = sb("parts", [P, 2, 3, T], BF16)
        q_stack = sb("q_stack", [P, H, T], BF16)
        k_stack = sb("k_stack", [P, H, T], BF16)
        v_stage = sb("v_stage", [P, NC, C])
        v_aug = sb("v_aug", [P, NC, H, 32])
        probs = sb("probs", [P, 2, HQ, T])
        row_max = sb("row_max", [P, 2, HQ, NC])
        neg_max = sb("neg_max", [HQ * NC, P])
        neg_rest = sb("neg_rest", [HQ * NC, P])
        neg_parts = sb("neg_parts", [HQ * NC, 3, P], BF16)
        o_sb = sb("o_sb2", [P, 2, T])
        den = sb("den", [P, H * T // P])
        inv = sb("inv", [P, H * T // P])
        num_sb = sb("num_sb", [P, 2, T])
        inv_sb = sb("inv_sb", [P, 2, T])
        stats = sb("stats2", [P, 2, 6])
        mean_var = sb("mean_var2", [P, 2, 2])
        rstd = sb("rstd2", [P, 2])
        minus_half = sb("minus_half2", [P, 2])

        ps_a = [ctx.enter_context(nc.psum_tensor(f"ps_a{i}", [P, 2, T], F32)) for i in range(2)]
        ps_b = [ctx.enter_context(nc.psum_tensor(f"ps_b{i}", [P, T], F32)) for i in range(2)]
        ps_pv = ctx.enter_context(nc.psum_tensor("ps_pv", [P, T], F32))
        ps_misc = ctx.enter_context(nc.psum_tensor("ps_misc", [P, T], F32))

        consts_loaded = sem("consts2_loaded")
        mask_step, rows_made, rows_stored = sem("mask_step"), sem("rows_made"), sem("rows_stored")
        consts_set = sem("consts2_set")
        in_loaded = sem("in_loaded")
        misc_made, misc_kept = sem("misc_made"), sem("misc_kept")
        part1, rest1, part2, part3 = sem("part1"), sem("rest1"), sem("part2"), sem("part3")
        parts_stored = [sem("parts_stored_q"), sem("parts_stored_k")]
        stack_loaded = [sem(f"stack_loaded{i}") for i in range(NQ)]
        a_made = [sem("a_made0"), sem("a_made1")]
        a_kept = [sem("a_kept0"), sem("a_kept1")]
        max_step, max_ready = sem("max_step"), sem("max_ready")
        max_stored = sem("max_stored")
        max_loaded = [sem(f"max_loaded{i}") for i in range(NQ)]
        b_made, exp_done = sem("b_made"), sem("exp_done")
        v_staged, v_filled = sem("v_staged"), sem("v_filled")
        mask_now_set = sem("mask_now_set")
        pv_made, o_kept = sem("pv_made"), sem("o_kept")
        o_stored = [sem("o_stored0"), sem("o_stored1")]
        den_loaded, inv_made, inv_stored, out_loaded = (
            sem("den_loaded"), sem("inv_made"), sem("inv_stored"), sem("out_loaded"))
        attn_scaled, attn_masked = sem("attn_scaled"), sem("attn_masked")
        y_added, y_stats, y_moments, y_rstd, x2_made, x2_stored = (
            sem("y2_added"), sem("y2_stats"), sem("y2_moments"), sem("y2_rstd"), sem("x2_made"), sem("x2_stored"))

        block = ctx.enter_context(nc.Block())

        def at(ref, i):
            return ref[i] if isinstance(i, int) else ref[bass.ds(i, 1)].squeeze(0)

        @block.sync
        def _(sp):
            held = spare_registers(sp, "held2", 1)

            def wait(semaphore, value):
                wait_apart(sp, held, (consts_loaded, 96), (semaphore, value))

            sp.dma_start(m_rows[:], A["mask"]).then_inc(consts_loaded, 16)
            sp.dma_start(w2[:], A["w2"].rearrange("w p c o -> p w c o")).then_inc(consts_loaded, 16)
            sp.dma_start(bias_qk[:], A["bias_qk"]).then_inc(consts_loaded, 16)
            sp.dma_start(bias_v[:], A["bias_v"].to_broadcast([P, C])).then_inc(consts_loaded, 16)
            sp.dma_start(mask_col[:], A["mask_col"]).then_inc(consts_loaded, 16)
            sp.dma_start(ident[:], A["ident"]).then_inc(consts_loaded, 16)

            def load_inputs(b):
                sp.dma_start(ctx_sb[:], at(A["ctx"], b)).then_inc(in_loaded, 16)
                sp.dma_start(mask_in[:], at(A["mask"], b).unsqueeze(0).to_broadcast([P, T])).then_inc(in_loaded, 16)

            def store_parts(b, i):
                qk, o = i % 2, i // 2
                wait(part3, 4 * b + i + 1)
                for j in range(3):
                    sp.dma_start(at(S["parts"], b)[qk, j, :, 8 * o:8 * o + 8, :].rearrange("d h t -> h d t"),
                                 parts[:, qk, j]).then_inc(parts_stored[qk], 16)

            def load_stack(b, q, first):
                if not first:
                    wait(b_made, 64 * (b - 1) + 16 * (q + 1))
                heads = slice(HQ * q, HQ * q + HQ)
                for qk, stack in ((0, q_stack), (1, k_stack)):
                    wait(parts_stored[qk], 96 * b + 48 * (q // 2) + 48)
                    src = at(S["parts"], b)[qk, :, :, heads, :].rearrange("j d h t -> j d (h t)")
                    at_row = 0
                    for n in (3, 2, 1):
                        dst = stack[at_row:at_row + n * DH, heads, :].rearrange("r h t -> r (h t)")
                        if qk == 0:
                            one = src[0:n].rearrange("j d t -> (j d) t")
                            sp.dma_start(dst, one).then_inc(stack_loaded[q], 16)
                        else:
                            one = src[3 - n:4 - n].to_broadcast([n, DH, HQ * T])
                            sp.dma_start(dst, one).then_inc(stack_loaded[q], 16)
                        at_row += n * DH
                sp.dma_start(q_stack[6 * DH:ROWS_A, heads, :],
                             at(S["rows_q"], b).unsqueeze(1).to_broadcast([9, HQ, T])).then_inc(stack_loaded[q], 16)
                sp.dma_start(k_stack[6 * DH:ROWS_B, heads, :],
                             at(S["rows_k"], b).unsqueeze(1).to_broadcast([12, HQ, T])).then_inc(stack_loaded[q], 16)

            def move_max(b, q):
                wait(max_ready, 4 * b + q + 1)
                d = at(S["max"], b)[q]
                sp.dma_start(d.rearrange("j (n t) -> n j t", t=P), neg_parts[:]).then_inc(max_stored, 16)
                wait(max_stored, 16 * (4 * b + q + 1))
                sp.dma_start(q_stack[ROWS_A:ROWS_B, HQ * q:HQ * q + HQ, :],
                             d.rearrange("j (h t) -> j h t", h=HQ)).then_inc(max_loaded[q], 16)

            def store_o(b, q):
                wait(o_kept, 4 * b + q + 1)
                sp.dma_start(at(S["heads"], b)[HQ * q:HQ * q + HQ].rearrange("h r t -> (h r) t"),
                             o_sb[:, q % 2, :]).then_inc(o_stored[q % 2], 16)

            def load_den(b, first=False):
                if not first:
                    wait(x2_made, 2 * b)
                wait(o_stored[0], 32 * (b + 1))
                wait(o_stored[1], 32 * (b + 1))
                sp.dma_start(den[:], at(S["heads"], b)[:, DH, :].rearrange("h (a t) -> h a t", a=8)).then_inc(
                    den_loaded, 16)
                for o in range(2):
                    sp.dma_start(num_sb[:, o, :], at(S["heads"], b)[8 * o:8 * o + 8, 0:DH, :]).then_inc(out_loaded, 16)

            def load_out(b):
                wait(inv_made, b + 1)
                sp.dma_start(at(S["inv"], b).rearrange("h (a t) -> (h a) t", a=8), inv[:]).then_inc(inv_stored, 16)
                sp.dma_start(mask_out[:], at(A["mask"], b).unsqueeze(0).to_broadcast([P, T])).then_inc(out_loaded, 16)
                wait(inv_stored, 16 * (b + 1))
                for o in range(2):
                    sp.dma_start(inv_sb[:, o, :], at(S["inv"], b)[8 * o:8 * o + 8].unsqueeze(1).to_broadcast(
                        [8, DH, T])).then_inc(out_loaded, 16)

            def store_x2(b):
                wait(x2_made, 2 * b + 2)
                sp.dma_start(S["x2"][bass.ds(b * L, L), :].rearrange("(i p) d -> p i d", p=P),
                             x[:, bass.ds(b * 2, 2), :]).then_inc(x2_stored, 16)

            load_inputs(0)
            for r, i in enumerate((0, 1, 2, 3, 3, 3, 4, 4, 5)):
                if r == 0:
                    wait(rows_made, 6)
                sp.dma_start(S["rows_q"][:, r, :], row_parts[:, i, :]).then_inc(rows_stored, 16)
            for r, i in enumerate((6, 6, 6, 0, 1, 2, 0, 1, 0, 6, 6, 6)):
                sp.dma_start(S["rows_k"][:, r, :], row_parts[:, i, :]).then_inc(rows_stored, 16)
            wait(rows_stored, 16 * 21)
            for i in range(4):
                store_parts(0, i)
            wait(v_staged, 2)
            load_inputs(1)
            for q in range(NQ):
                load_stack(0, q, True)
            move_max(0, 0)

            def batch(b, first, last, second=False):
                if not first:
                    store_o(b - 1, 3)
                    load_stack(b, 3, False)
                    load_den(b - 1, second)
                move_max(b, 1)
                if not first:
                    load_out(b - 1)
                if not last:
                    store_parts(b + 1, 0)
                    store_parts(b + 1, 1)
                store_o(b, 0)
                if not last:
                    load_stack(b + 1, 0, False)
                move_max(b, 2)
                if not last:
                    store_parts(b + 1, 2)
                    store_parts(b + 1, 3)
                store_o(b, 1)
                if not last:
                    load_stack(b + 1, 1, False)
                move_max(b, 3)
                store_o(b, 2)
                if not last:
                    load_stack(b + 1, 2, False)
                    move_max(b + 1, 0)
                if not first:
                    store_x2(b - 1)

            def inputs_after(b):
                wait(v_staged, 2 * b + 4)
                load_inputs(b + 2)

            batch(0, True, False)
            inputs_after(0)
            batch(1, False, False, True)
            inputs_after(1)
            with sp.Fori(2, B - 2) as b:
                batch(b, False, False)
                inputs_after(b)
            batch(B - 2, False, False)
            batch(B - 1, False, True)
            store_o(B - 1, 3)
            load_den(B - 1)
            load_out(B - 1)
            store_x2(B - 1)
            wait(x2_stored, 16 * B)

        @block.gpsimd
        def _(pool):
            nc.gpsimd.memset(minus_half[:], -0.5).then_inc(consts_set, 1)
            nc.gpsimd.memset(v_aug[:], 1.0).then_inc(consts_set, 1)
            pool.wait_ge(consts_set, 2)

            def split(b, i):
                k, s = 4 * b + i, i % 2
                pool.wait_ge(part1, k + 1)
                nc.gpsimd.tensor_tensor(rest[:, s], full[:, s], parts[:, s, 0], ALU.subtract).then_inc(rest1, 1)
                pool.wait_ge(part2, k + 1)
                nc.gpsimd.tensor_tensor(parts[:, s, 2], rest[:, s], parts[:, s, 1], ALU.subtract).then_inc(part3, 1)

            def finish_heads(b):
                pool.wait_ge(out_loaded, 80 * b + 80)
                nc.gpsimd.tensor_tensor(inv_sb[:], inv_sb[:], mask_out[:].unsqueeze(1).to_broadcast([P, 2, T]),
                                        ALU.mult).then_inc(attn_scaled, 1)
                pool.wait_ge(attn_scaled, b + 1)
                nc.gpsimd.tensor_tensor(num_sb[:], num_sb[:], inv_sb[:], ALU.mult).then_inc(attn_masked, 1)

            def token_rstd(b):
                pool.wait_ge(y_moments, b + 1)
                nc.gpsimd.tensor_tensor(rstd[:], mean_var[:, :, 1], minus_half[:], ALU.pow).then_inc(y_rstd, 1)

            for i in range(4):
                split(0, i)

            def batch(b, first, last):
                if not last:
                    split(b + 1, 0)
                    split(b + 1, 1)
                if not first:
                    finish_heads(b - 1)
                if not last:
                    split(b + 1, 2)
                    split(b + 1, 3)
                if not first:
                    token_rstd(b - 1)

            batch(0, True, False)
            with pool.Fori(1, B - 1) as b:
                batch(b, False, False)
            batch(B - 1, False, True)
            finish_heads(B - 1)
            token_rstd(B - 1)

        @block.scalar
        def _(act):
            def exps(b, q, c, first):
                n = STEPS * b + NC * q + c
                if not (first and NC * q + c < 2):
                    act.wait_ge(pv_made, n - 1)
                for h in range(HQ):
                    act.wait_ge(b_made, 4 * n + h + 1)
                    nc.scalar.activation(probs[:, c % 2, h], ps_b[h % 2][:], ACT.Exp, scale=DH ** -0.5).then_inc(
                        exp_done, 1)

            def keep_o(b, q, first):
                act.wait_ge(pv_made, STEPS * b + NC * q + NC)
                if not (first and q < 2):
                    act.wait_ge(o_stored[q % 2], 32 * b + 16 * (q // 2))
                nc.scalar.activation(o_sb[:, q % 2], ps_pv[:], ACT.Copy).then_inc(o_kept, 1)

            def batch(b, first):
                for q in range(NQ):
                    for c in range(NC):
                        exps(b, q, c, first)
                        if c == 0 and q > 0:
                            keep_o(b, q - 1, first)
                        elif c == 0 and not first:
                            keep_o(b - 1, 3, False)

            batch(0, True)
            with act.Fori(1, B) as b:
                batch(b, False)
            keep_o(B - 1, 3, False)

        @block.vector
        def _(dve):
            held = spare_registers(dve, "held2", 1)

            def row_split(src, j, k):
                nc.vector.tensor_copy(row_parts[:, j], src[:]).then_inc(mask_step, 1)
                dve.wait_ge(mask_step, k + 1)
                nc.vector.tensor_tensor(rest_rows[:], src[:], row_parts[:, j], ALU.subtract).then_inc(mask_step, 1)
                dve.wait_ge(mask_step, k + 2)
                nc.vector.tensor_copy(row_parts[:, j + 1], rest_rows[:]).then_inc(mask_step, 1)
                dve.wait_ge(mask_step, k + 3)
                nc.vector.tensor_tensor(row_parts[:, j + 2], rest_rows[:], row_parts[:, j + 1],
                                        ALU.subtract).then_inc(rows_made, 1)

            dve.wait_ge(consts_loaded, 96)
            nc.vector.memset(row_parts[:, 6], 1.0).then_inc(rows_made, 1)
            nc.vector.tensor_scalar(pen_rows[:], m_rows[:], -1.0, PENALTY, ALU.add, ALU.mult).then_inc(mask_step, 1)
            dve.wait_ge(mask_step, 1)
            row_split(pen_rows, 0, 1)
            dve.wait_ge(rows_made, 2)
            row_split(m_rows, 3, 4)
            dve.wait_ge(rows_made, 3)
            nc.vector.memset(rest_rows[:], 0.0).then_inc(rows_made, 3)
            dve.wait_ge(consts_set, 2)

            def reduces(k, par, c, halves=(0, 1)):
                for i in halves:
                    dve.wait_ge(a_made[i], k + 1)
                    nc.vector.tensor_reduce(row_max[:, par, 2 * i:2 * i + 2, c], ps_a[i][:], AX.X,
                                            ALU.max).then_inc(a_kept[i], 1)

            def keep_max(m):
                dve.wait_ge(misc_made, m + 1)
                nc.vector.tensor_scalar(neg_max[:], ps_misc[0:HQ * NC, 0:P], -1.0, None, ALU.mult).then_inc(misc_kept, 1)

            def cut_max(k, m, first=False):
                dve.wait_ge(misc_kept, m + 1)
                if not first:
                    dve.wait_ge(max_stored, 16 * k)
                nc.vector.tensor_copy(neg_parts[:, 0], neg_max[:]).then_inc(max_step, 1)
                dve.wait_ge(max_step, 3 * k + 1)
                nc.vector.tensor_tensor(neg_rest[:], neg_max[:], neg_parts[:, 0], ALU.subtract).then_inc(max_step, 1)
                dve.wait_ge(max_step, 3 * k + 2)
                nc.vector.tensor_copy(neg_parts[:, 1], neg_rest[:]).then_inc(max_step, 1)
                dve.wait_ge(max_step, 3 * k + 3)
                nc.vector.tensor_tensor(neg_parts[:, 2], neg_rest[:], neg_parts[:, 1],
                                        ALU.subtract).then_inc(max_ready, 1)

            def keep_qk(b, i, m, first=False):
                k, s = 4 * b + i, i % 2
                dve.wait_ge(misc_made, m + 1)
                dve.wait_ge(in_loaded, 32 * b + 32)
                if not (first and i < 2):
                    dve.wait_ge(part3, k - 1)
                    dve.wait_ge(parts_stored[s], 96 * b + 48 * (i // 2))
                nc.vector.scalar_tensor_tensor(full[:, s], ps_misc[:], bias_qk[:, s, i // 2:i // 2 + 1], mask_in[:],
                                               ALU.add, ALU.mult).then_inc(misc_kept, 1)

            def first_part(i, m):
                s = i % 2
                dve.wait_ge(misc_kept, m + 1)
                nc.vector.tensor_copy(parts[:, s, 0], full[:, s]).then_inc(part1, 1)

            def cut(b, i):
                dve.wait_ge(rest1, 4 * b + i + 1)
                nc.vector.tensor_copy(parts[:, i % 2, 1], rest[:, i % 2]).then_inc(part2, 1)

            def stage_v(b, i, m, first=False):
                dve.wait_ge(misc_made, m + 1)
                if not first:
                    dve.wait_ge(v_filled, 4 * b)
                nc.vector.tensor_tensor(v_stage[:, 2 * i:2 * i + 2], ps_misc[:].rearrange("p (s c) -> p s c", s=2),
                                        bias_v[:].unsqueeze(1).to_broadcast([P, 2, C]), ALU.add)\
                    .then_inc(misc_kept, 1)
                dve.wait_ge(misc_kept, m + 1)
                nc.vector.tensor_copy(mask_now[:, 2 * i:2 * i + 2],
                                      mask_col[:, bass.ds(b, 1), 2 * i:2 * i + 2].squeeze(1)).then_inc(v_staged, 1)

            def fill_v(b, first=False):
                dve.wait_ge(v_staged, 2 * b + 2)
                if not first:
                    dve.wait_ge(pv_made, STEPS * b)
                for c in range(NC):
                    nc.vector.tensor_scalar(v_aug[:, c, :, 0:DH], v_stage[:, c].rearrange("p (h d) -> p h d", h=H),
                                            mask_now[:, c:c + 1], None, ALU.mult).then_inc(v_filled, 1)

            def invert(b):
                dve.wait_ge(den_loaded, 16 * (b + 1))
                nc.vector.reciprocal(inv[:], den[:]).then_inc(inv_made, 1)

            def moments(b):
                dve.wait_ge(attn_masked, b + 1)
                nc.vector.tensor_tensor(num_sb[:], num_sb[:], x[:, bass.ds(2 * b, 2), :], ALU.add).then_inc(y_added, 1)
                dve.wait_ge(y_added, b + 1)
                for i in range(2):
                    nc.vector.bn_stats(stats[:, i], num_sb[:, i]).then_inc(y_stats, 1)
                wait_apart(dve, held, (consts_set, 2), (y_stats, 4 * b + 2))
                for i in range(2):
                    nc.vector.bn_aggr(mean_var[:, i], stats[:, i]).then_inc(y_stats, 1)
                dve.wait_ge(y_stats, 4 * b + 4)
                nc.vector.tensor_scalar(mean_var[:, :, 1], mean_var[:, :, 1], LN_EPS, None, ALU.add).then_inc(
                    y_moments, 1)

            def normalize(b):
                dve.wait_ge(y_rstd, b + 1)
                for i in range(2):
                    nc.vector.tensor_scalar(x[:, bass.ds(2 * b + i, 1), :].squeeze(1), num_sb[:, i],
                                            mean_var[:, i, 0:1], rstd[:, i:i + 1], ALU.subtract, ALU.mult)\
                        .then_inc(x2_made, 1)

            for i in range(4):
                keep_qk(0, i, i, True)
                first_part(i, i)
                cut(0, i)
            stage_v(0, 0, 4, True)
            stage_v(0, 1, 5, True)
            for c in range(NC):
                reduces(c, 0, c)
            keep_max(6)
            cut_max(0, 6, True)
            for c in range(NC):
                reduces(NC + c, 1, c)

            def batch(b, first, last):
                m = MISC0 + MISC * b
                for q in range(NQ):
                    for c in range(NC):
                        s = NC * q + c
                        before = q if last else (0, 3, 6, 9)[q]
                        qk = {2: (0, 1), 3: (1, 2), 6: (2, 4), 7: (3, 5)}
                        turned = s in (1, 5, 9) or (s == 13 and not last)
                        if turned:
                            keep_max(m + before)
                        elif not last and s in qk:
                            keep_qk(b + 1, qk[s][0], m + qk[s][1])
                        elif not last and s in (10, 11):
                            stage_v(b + 1, s - 10, m + s - 3)
                        if not (last and q >= 2):
                            reduces(2 * NC + STEPS * b + s, q % 2, c)
                        if s == 0:
                            fill_v(b, first)
                        if turned:
                            cut_max(4 * b + q + 1, m + before)
                        if not last:
                            if s in qk:
                                first_part(qk[s][0], m + qk[s][1])
                            if s in (3, 4, 7, 8):
                                cut(b + 1, (3, 4, 7, 8).index(s))
                        if not first:
                            if s == 3:
                                invert(b - 1)
                            elif s == 12:
                                moments(b - 1)
                            elif s == 14:
                                normalize(b - 1)

            batch(0, True, False)
            with dve.Fori(1, B - 1) as b:
                batch(b, False, False)
            batch(B - 1, False, True)
            invert(B - 1)
            moments(B - 1)
            normalize(B - 1)

        @block.tensor
        def _(pe):
            def scores_max(k, b, q, c, i, first=False):
                if c == 0 and i == 0:
                    pe.wait_ge(stack_loaded[q], 16 * STACK_DMAS * (b + 1))
                if not first:
                    pe.wait_ge(a_kept[i], k)
                for j in range(2):
                    h = HQ * q + 2 * i + j
                    mm = nc.tensor.matmul(ps_a[i][:, j], q_stack[0:ROWS_A, h, c * P:(c + 1) * P],
                                          k_stack[0:ROWS_A, h, :], start=True, stop=True)
                mm.then_inc(a_made[i], 1)

            def scores(b, q, c, h, first):
                e = 64 * b + 16 * q + 4 * c + h
                if c == 0 and h == 0:
                    pe.wait_ge(max_loaded[q], 16 * (b + 1))
                if not (first and 16 * q + 4 * c + h < 2):
                    pe.wait_ge(exp_done, e - 1)
                hh = HQ * q + h
                nc.tensor.matmul(ps_b[h % 2][:], k_stack[0:ROWS_B, hh, c * P:(c + 1) * P],
                                 q_stack[0:ROWS_B, hh, :], start=True, stop=True).then_inc(b_made, 1)

            def values(b, q, c, first):
                n = STEPS * b + NC * q + c
                pe.wait_ge(exp_done, 4 * n + 4)
                if c == 0:
                    if q == 0:
                        pe.wait_ge(v_filled, 4 * b + 4)
                    if not (first and q == 0):
                        pe.wait_ge(o_kept, 4 * b + q)
                for g in range(HQ):
                    mm = nc.tensor.matmul(ps_pv[32 * g:32 * g + 32, :], v_aug[:, c, HQ * q + g, :],
                                          probs[:, c % 2, g], start=(c == 0), stop=(c == NC - 1))
                mm.then_inc(pv_made, 1)

            def free_misc(m, first):
                if not first:
                    pe.wait_ge(misc_kept, m)

            def project_qk(b, i, m, first=False):
                s, o = i % 2, i // 2
                if i < 2:
                    pe.wait_ge(in_loaded, 32 * b + 32)
                free_misc(m, first)
                for c in range(2):
                    rhs = ctx_sb[:, c] if s else x[:, bass.ds(2 * b + c, 1), :].squeeze(1)
                    mm = nc.tensor.matmul(ps_misc[:], w2[:, s, c, o * P:(o + 1) * P], rhs,
                                          start=(c == 0), stop=(c == 1))
                mm.then_inc(misc_made, 1)

            def project_v(b, i, m):
                free_misc(m, False)
                for j in range(2):
                    sc = 2 * i + j
                    for c in range(2):
                        mm = nc.tensor.matmul(ps_misc[:, j * C:(j + 1) * C], ctx_sb[:, c, sc * P:(sc + 1) * P],
                                              w2[:, 2, c, :], start=(c == 0), stop=(c == 1))
                mm.then_inc(misc_made, 1)

            def transpose_max(m, par, k):
                free_misc(m, False)
                for i in range(2):
                    pe.wait_ge(a_kept[i], k)
                nc.tensor.transpose(ps_misc[0:HQ * NC, 0:P], row_max[:, par].rearrange("p h c -> p (h c)"),
                                    ident[:]).then_inc(misc_made, 1)

            pe.wait_ge(consts_loaded, 96)
            for i in range(4):
                project_qk(0, i, i, i == 0)
            project_v(0, 0, 4)
            project_v(0, 1, 5)
            for c in range(NC):
                for i in range(2):
                    scores_max(c, 0, 0, c, i, c == 0)
            transpose_max(6, 0, NC)
            for c in range(NC):
                for i in range(2):
                    scores_max(NC + c, 0, 1, c, i)

            def batch(b, first, last):
                m = MISC0 + MISC * b
                for q in range(NQ):
                    for c in range(NC):
                        s = NC * q + c
                        k = 2 * NC + STEPS * b + s
                        ahead = not (last and q >= 2)
                        b2, q2 = (b, q + 2) if q < 2 else (b + 1, q - 2)
                        if ahead:
                            scores_max(k, b2, q2, c, 0)
                        scores(b, q, c, 0, first)
                        scores(b, q, c, 1, first)
                        if ahead:
                            scores_max(k, b2, q2, c, 1)
                        if s > 0:
                            values(b, (s - 1) // NC, (s - 1) % NC, first)
                        elif not first:
                            values(b - 1, NQ - 1, NC - 1, False)
                        scores(b, q, c, 2, first)
                        scores(b, q, c, 3, first)
                        if c == 0 and not (last and q == 3):
                            before = q if last else (0, 3, 6, 9)[q]
                            transpose_max(m + before, (q + 1) % 2, k)
                        if not last:
                            if s in (1, 2, 5, 6):
                                i = (1, 2, 5, 6).index(s)
                                project_qk(b + 1, i, m + (1, 2, 4, 5)[i])
                            elif s in (9, 10):
                                project_v(b + 1, s - 9, m + s - 2)

            batch(0, True, False)
            with pe.Fori(1, B - 1) as b:
                batch(b, False, False)
            batch(B - 1, False, True)
            values(B - 1, NQ - 1, NC - 1, False)
E_, K_TOP = 16, 4
TILES = TOK * K_TOP // P + E_
DUMMY = TOK


def route(nc, A, S, x, G):
    W = NT * K_TOP
    with ExitStack() as ctx:
        def sb(name, shape, dt=F32):
            return ctx.enter_context(nc.sbuf_tensor(name, shape, dt))

        def sem(name):
            return ctx.enter_context(nc.semaphore(name))

        rw = sb("rw", [P, KC, E_])
        rb = sb("rb", [P, E_])
        ident = sb("ident3", [P, P])
        before = sb("before", [P, P])
        ones = sb("ones3", [P, P])
        iota_p = sb("iota_p", [P, 1])
        iota_f = sb("iota_f", [P, P])
        xT = sb("xT3", [P, 2, KC, P])
        logits = sb("logits", [P, NT, E_])
        top = sb("top", [P, NT, 8])
        top_i = sb("top_i", [P, NT, 8], U32)
        top_f = sb("top_f", [P, W])
        gap = sb("gap", [P, NT, K_TOP])
        share = sb("share", [P, NT, K_TOP])
        total = sb("total", [P, NT])
        chosen = sb("chosen", [P, W, E_])
        picked = sb("picked", [P, W, E_])
        sel = sb("sel", [P, NT, E_])
        sofar = sb("sofar", [P, NT + 1, E_])
        over = sb("over", [P, E_, E_])
        n_tiles = sb("n_tiles", [P, E_])
        tile_end = sb("tile_end", [P, E_])
        base = sb("base", [P, E_])
        place = sb("place", [P, NT, E_])
        slot = sb("slot", [P, W])
        slot_i = sb("slot_i", [P, W], I32)
        hi_i = sb("hi_i", [P, W], I32)
        lo_i = sb("lo_i", [P, W], I32)
        hi_f = sb("hi_f", [P, W])
        lo_f = sb("lo_f", [P, W])
        token1 = sb("token1", [P, NT])
        in_tile = sb("in_tile", [P, 2, K_TOP, P])
        of_tile = sb("of_tile", [P, 2, K_TOP, TILES])
        payload = sb("payload", [P, 2, K_TOP, 2, TILES])
        empty = sb("empty", [P, TILES])
        tok_f = sb("tok_f", [P, TILES])
        past = sb("past", [1, TILES, E_])
        expert_f = sb("expert_f", [1, TILES])
        expert_i = sb("expert_i", [1, TILES], I32)
        zero = sb("zero3", [P, D])

        ps_t = [ctx.enter_context(nc.psum_tensor(f"ps_t{i}", [P, D], F32)) for i in range(2)]
        ps_l = ctx.enter_context(nc.psum_tensor("ps_l", [P, D], F32))
        ps_r = ctx.enter_context(nc.psum_tensor("ps_r", [P, D], F32))
        ps_s = ctx.enter_context(nc.psum_tensor("ps_s", [P, D], F32))

        loaded, set_ = sem("loaded3"), sem("set3")
        x_turned, x_kept, logit_made = sem("x_turned"), sem("x_kept"), sem("logit_made")
        step = sem("route_step")
        gap_made, exp_made = sem("gap_made"), sem("exp_made")
        sel_made, rank_made = sem("sel_made"), sem("rank_made")
        onehot_made, spread_done = sem("onehot_made"), sem("spread_done")
        dummy_stored, acc_stored = sem("dummy_stored"), sem("acc_stored")

        block = ctx.enter_context(nc.Block())

        @block.sync
        def _(sp):
            sp.dma_start(rw[:], A["router_w"]).then_inc(loaded, 16)
            sp.dma_start(rb[:], A["router_b"].to_broadcast([P, E_])).then_inc(loaded, 16)
            sp.dma_start(ident[:], A["ident"]).then_inc(loaded, 16)
            sp.dma_start(before[:], A["before"]).then_inc(loaded, 16)
            sp.dma_start(iota_p[:], A["iota_p"]).then_inc(loaded, 16)
            sp.dma_start(iota_f[:], A["iota_f"]).then_inc(loaded, 16)
            sp.dma_start(S["acc"][0:TOK, :].rearrange("(t p) d -> p t d", p=P), x[:]).then_inc(acc_stored, 16)
            sp.wait_ge(set_, 3)
            sp.dma_start(S["x2"][TOK:TOK + P, :], zero[:]).then_inc(dummy_stored, 16)
            sp.dma_start(S["acc"][TOK:TOK + P, :], zero[:]).then_inc(dummy_stored, 16)
            sp.wait_ge(dummy_stored, 32)
            sp.wait_ge(acc_stored, 16)

        @block.gpsimd
        def _(pool):
            nc.gpsimd.memset(ones[:], 1.0).then_inc(set_, 1)
            nc.gpsimd.memset(zero[:], 0.0).then_inc(set_, 1)
            nc.gpsimd.memset(sofar[:, 0], 0.0).then_inc(set_, 1)

        @block.scalar
        def _(act):
            for t in range(NT):
                act.wait_ge(x_turned, t + 1)
                if t >= 2:
                    act.wait_ge(logit_made, t - 1)
                nc.scalar.activation(xT[:, t % 2], ps_t[t % 2][:].rearrange("p (c t) -> p c t", c=KC),
                                     ACT.Copy).then_inc(x_kept, 1)
            act.wait_ge(gap_made, 1)
            nc.scalar.activation(share[:], gap[:], ACT.Exp).then_inc(exp_made, 1)

        @block.vector
        def _(dve):
            done = [0]

            def chain(instruction):
                done[0] += 1
                instruction.then_inc(step, 1)
                dve.wait_ge(step, done[0])

            dve.wait_ge(loaded, 96)
            dve.wait_ge(set_, 3)
            for t in range(NT):
                dve.wait_ge(logit_made, t + 1)
            chain(nc.vector.tensor_tensor(logits[:], ps_l[:, 0:NT * E_].rearrange("p (t e) -> p t e", t=NT),
                                          rb[:].unsqueeze(1).to_broadcast([P, NT, E_]), ALU.add))
            for t in range(NT):
                last = nc.vector.max(top[:, t], logits[:, t])
            chain(last)
            for t in range(NT):
                last = nc.vector.max_index(top_i[:, t], top[:, t], logits[:, t])
            nc.vector.tensor_tensor(gap[:], top[:, :, 0:K_TOP], top[:, :, 0:1].to_broadcast([P, NT, K_TOP]),
                                    ALU.subtract).then_inc(gap_made, 1)
            chain(last)
            chain(nc.vector.tensor_copy(top_f[:].rearrange("p (t k) -> p t k", t=NT), top_i[:, :, 0:K_TOP]))
            chain(nc.vector.tensor_tensor(chosen[:], iota_f[:, 0:E_].unsqueeze(1).to_broadcast([P, W, E_]),
                                          top_f[:].unsqueeze(2).to_broadcast([P, W, E_]), ALU.is_equal))
            chain(nc.vector.tensor_reduce(sel[:], chosen[:].rearrange("p (t k) e -> p t e k", k=K_TOP), AX.X, ALU.add))
            for t in range(NT):
                chain(nc.vector.tensor_tensor(sofar[:, t + 1], sofar[:, t], sel[:, t], ALU.add))
            nc.vector.tensor_scalar(token1[:], iota_f[:, 0:NT], float(P), iota_p[:, 0:1], ALU.mult,
                                    ALU.add).then_inc(sel_made, 1)
            dve.wait_ge(exp_made, 1)
            chain(nc.vector.tensor_reduce(total[:], share[:], AX.X, ALU.add))
            chain(nc.vector.reciprocal(total[:], total[:]))
            chain(nc.vector.tensor_tensor(share[:], share[:], total[:].unsqueeze(2).to_broadcast([P, NT, K_TOP]),
                                          ALU.mult))
            dve.wait_ge(rank_made, 1)
            chain(nc.vector.tensor_copy(base[:], ps_r[:, NT * E_:(NT + 1) * E_]))
            chain(nc.vector.scalar_tensor_tensor(over[:], iota_f[:, 0:E_].unsqueeze(1).to_broadcast([P, E_, E_]),
                                                 float(P), base[:].unsqueeze(2).to_broadcast([P, E_, E_]),
                                                 ALU.mult, ALU.is_lt))
            chain(nc.vector.tensor_reduce(n_tiles[:], over[:], AX.X, ALU.add))
            chain(nc.vector.tensor_scalar(n_tiles[:], n_tiles[:], 1.0, None, ALU.max))
            chain(nc.vector.tensor_tensor_scan(tile_end[:], ones[:, 0:E_], n_tiles[:], 0.0, ALU.mult, ALU.add))
            chain(nc.vector.tensor_tensor(base[:], tile_end[:], n_tiles[:], ALU.subtract))
            chain(nc.vector.tensor_scalar(base[:], base[:], float(P), None, ALU.mult))
            chain(nc.vector.tensor_tensor(place[:], ps_r[:, 0:NT * E_].rearrange("p (t e) -> p t e", t=NT),
                                          base[:].unsqueeze(1).to_broadcast([P, NT, E_]), ALU.add))
            for t in range(NT):
                last = nc.vector.tensor_tensor(picked[:, K_TOP * t:K_TOP * t + K_TOP],
                                               chosen[:, K_TOP * t:K_TOP * t + K_TOP],
                                               place[:, t].unsqueeze(1).to_broadcast([P, K_TOP, E_]), ALU.mult)
            chain(last)
            chain(nc.vector.tensor_reduce(slot[:], picked[:], AX.X, ALU.add))
            chain(nc.vector.tensor_copy(slot_i[:], slot[:]))
            nc.vector.tensor_scalar(hi_i[:], slot_i[:], 7, None, ALU.logical_shift_right)
            chain(nc.vector.tensor_scalar(lo_i[:], slot_i[:], P - 1, None, ALU.bitwise_and))
            nc.vector.tensor_copy(hi_f[:], hi_i[:])
            chain(nc.vector.tensor_copy(lo_f[:], lo_i[:]))
            chain(nc.vector.tensor_scalar(token1[:], token1[:], 1.0, None, ALU.add))
            for t in range(NT):
                s, kk = t % 2, slice(K_TOP * t, K_TOP * t + K_TOP)
                if t >= 2:
                    dve.wait_ge(spread_done, t - 1)
                nc.vector.tensor_tensor(in_tile[:, s], iota_f[:].unsqueeze(1).to_broadcast([P, K_TOP, P]),
                                        lo_f[:, kk].unsqueeze(2).to_broadcast([P, K_TOP, P]), ALU.is_equal)
                chain(nc.vector.tensor_tensor(of_tile[:, s], iota_f[:, 0:TILES].unsqueeze(1).to_broadcast(
                    [P, K_TOP, TILES]), hi_f[:, kk].unsqueeze(2).to_broadcast([P, K_TOP, TILES]), ALU.is_equal))
                nc.vector.tensor_scalar(payload[:, s, :, 0], of_tile[:, s], token1[:, t:t + 1], None, ALU.mult)
                nc.vector.tensor_tensor(payload[:, s, :, 1], of_tile[:, s], share[:, t].unsqueeze(2).to_broadcast(
                    [P, K_TOP, TILES]), ALU.mult).then_inc(onehot_made, 1)
            chain(nc.vector.tensor_tensor(past[:], tile_end[0:1].unsqueeze(1).to_broadcast([1, TILES, E_]),
                                          iota_f[0:1, 0:TILES].unsqueeze(2).to_broadcast([1, TILES, E_]), ALU.is_le))
            chain(nc.vector.tensor_reduce(expert_f[:], past[:], AX.X, ALU.add))
            chain(nc.vector.tensor_scalar(expert_f[:], expert_f[:], float(E_ - 1), None, ALU.min))
            chain(nc.vector.tensor_copy(G["expert"][:], expert_f[:]))
            chain(nc.vector.tensor_scalar(G["parity"][:], G["expert"][:], 1, None, ALU.bitwise_and))
            chain(nc.vector.tensor_scalar(G["last_tile"][:], tile_end[0:1], -1.0, None, ALU.add))
            dve.wait_ge(spread_done, NT)
            chain(nc.vector.tensor_scalar(empty[:], ps_s[:, 0:TILES], 0.0, None, ALU.is_equal))
            chain(nc.vector.tensor_scalar(iota_p[:], iota_p[:], float(DUMMY + 1), None, ALU.add))
            chain(nc.vector.tensor_scalar(empty[:], empty[:], iota_p[:, 0:1], -1.0, ALU.mult, ALU.add))
            chain(nc.vector.tensor_tensor(tok_f[:], ps_s[:, 0:TILES], empty[:], ALU.add))
            chain(nc.vector.tensor_copy(G["token"][:], tok_f[:]))
            chain(nc.vector.tensor_copy(G["weight"][:], ps_s[:, TILES:2 * TILES]))

        @block.tensor
        def _(pe):
            pe.wait_ge(loaded, 96)

            def turn(t):
                if t >= 2:
                    pe.wait_ge(x_kept, t - 1)
                for c in range(KC):
                    mm = nc.tensor.transpose(ps_t[t % 2][:, c * P:(c + 1) * P], x[:, t, c * P:(c + 1) * P], ident[:])
                mm.then_inc(x_turned, 1)

            turn(0)
            for t in range(NT):
                if t + 1 < NT:
                    turn(t + 1)
                pe.wait_ge(x_kept, t + 1)
                for c in range(KC):
                    mm = nc.tensor.matmul(ps_l[:, t * E_:(t + 1) * E_], xT[:, t % 2, c], rw[:, c, :],
                                          start=(c == 0), stop=(c == KC - 1))
                mm.then_inc(logit_made, 1)
            pe.wait_ge(sel_made, 1)
            nc.tensor.matmul(ps_r[:, 0:NT * E_], before[:], sel[:].rearrange("p t e -> p (t e)"),
                             start=True, stop=False, skip_group_check=True)
            nc.tensor.matmul(ps_r[:, 0:NT * E_], ones[:], sofar[:, 0:NT].rearrange("p t e -> p (t e)"),
                             start=False, stop=True, skip_group_check=True)
            nc.tensor.matmul(ps_r[:, NT * E_:(NT + 1) * E_], ones[:], sofar[:, NT], start=False, stop=True,
                             skip_group_check=True).then_inc(rank_made, 1)
            for t in range(NT):
                pe.wait_ge(onehot_made, t + 1)
                for k in range(K_TOP):
                    mm = nc.tensor.matmul(ps_s[:, 0:2 * TILES], in_tile[:, t % 2, k],
                                          payload[:, t % 2, k].rearrange("p a t -> p (a t)"),
                                          start=(t == 0 and k == 0), stop=(t == NT - 1 and k == K_TOP - 1))
                mm.then_inc(spread_done, 1)


def experts(nc, A, S, G):
    U = 4
    F = 3 * D
    LIMIT, ALPHA = 7.0, 1.702
    with ExitStack() as ctx:
        def sb(name, shape, dt=F32):
            return ctx.enter_context(nc.sbuf_tensor(name, shape, dt))

        def sem(name):
            return ctx.enter_context(nc.semaphore(name))

        ident = sb("ident4", [P, P])
        zero_row = sb("zero_row", [P, 1])
        w = sb("w_expert", [P, 2, 3, KC, D])
        bias = sb("bias_expert", [P, 2, F])
        rows_at = [sb(f"rows_at{i}", [P, 1], U32) for i in range(U)]
        x_rows = [sb(f"x_rows{i}", [P, D]) for i in range(U)]
        xT = sb("xT4", [P, 2, KC, P])
        gate = sb("gate", [P, D])
        up = sb("up", [P, D])
        sig = sb("sig", [P, D])
        h = sb("h", [P, D])
        hT = sb("hT", [P, KC, P])
        y = [sb(f"y{i}", [P, D]) for i in range(U)]

        def bank(name):
            return ctx.enter_context(nc.psum_tensor(name, [P, D], F32))

        ps_g, ps_u, ps_x, ps_h, ps_y = bank("ps_g"), bank("ps_u2"), bank("ps_x"), bank("ps_h"), bank("ps_y")

        w_loaded = [sem("we_loaded0"), sem("we_loaded1")]
        at_set = sem("at_set")
        tables_read = sem("tables_read")
        gathered = [sem(f"gathered{i}") for i in range(U)]
        x_turned, xT_kept = sem("xe_turned"), sem("xeT_kept")
        gu_made, g_kept, u_kept = sem("gu_made"), sem("g_kept"), sem("ue_kept")
        g_cut, u_cut, gated, sig_made, h_made = sem("g_cut"), sem("u_cut"), sem("gated"), sem("sig_made"), sem("h_made")
        h_turned, hT_kept = sem("h_turned"), sem("hT_kept")
        y_made, y_biased, y_ready = sem("ye_made"), sem("y_biased"), sem("y_ready")
        added = sem("added")

        block = ctx.enter_context(nc.Block())

        def loop(engine, body):
            for j in range(U):
                body(j, j, j == 0, False)
            with engine.Fori(1, TILES // U - 1) as r:
                for j in range(U):
                    body(U * r + j, j, False, False)
            for j in range(U):
                body(TILES - U + j, j, False, j == U - 1)

        def pick(table, i):
            return table[:, i:i + 1] if isinstance(i, int) else table[:, bass.ds(i, 1)]

        @block.sync
        def _(sp):
            sp.dma_start(ident[:], A["ident"]).then_inc(w_loaded[1], 16)
            sp.wait_ge(w_loaded[1], 16)

            def load(e, s):
                sp.dma_start(w[:, s], A["w_expert"][e] if isinstance(e, int) else
                             A["w_expert"][bass.ds(e, 1)].squeeze(0)).then_inc(w_loaded[s], 16)
                sp.dma_start(bias[:, s], (A["b_expert"][e:e + 1] if isinstance(e, int) else
                                          A["b_expert"][bass.ds(e, 1)]).to_broadcast([P, F])).then_inc(w_loaded[s], 16)

            load(0, 0)
            load(1, 1)
            with sp.Fori(1, E_ // 2) as r:
                for s in range(2):
                    e = 2 * r + s
                    last = sp.value_load(G["last_tile"][:, bass.ds(e - 2, 1)], min_val=0, max_val=TILES - 1)
                    sp.wait_ge(y_biased, last + 1)
                    load(e, s)

        @block.gpsimd
        def _(pool):
            held = spare_registers(pool, "held4", 2)

            def gather(i, j, first):
                if not first:
                    pool.wait_ge(x_turned, i - U + 1)
                    pool.wait_ge(added, 16 * (i - U + 1))
                nc.gpsimd.tensor_copy(rows_at[j][:], pick(G["token"], i)).then_inc(at_set, 1)
                wait_apart(pool, held, (tables_read, 1), (at_set, i + 1))
                pool.indirect_dma_start(x_rows[j][:], None, S["x2"], bass.IndirectOffsetOnAxis(rows_at[j][:], 0))\
                    .then_inc(gathered[j], 16)

            def scatter(i, j, first):
                waits = [(y_ready, i + 1)] + ([] if first else [(added, 16 * i)])
                wait_apart(pool, held, (tables_read, 1), *waits)
                pool.indirect_dma_start(S["acc"], bass.IndirectOffsetOnAxis(rows_at[j][:], 0), y[j][:], None,
                                        compute_op=ALU.add).then_inc(added, 16)

            nc.gpsimd.memset(zero_row[:], 0.0).then_inc(tables_read, 1)
            for j in range(2):
                gather(j, j, True)

            def body(i, j, first, last):
                if not (isinstance(i, int) and i >= TILES - 2):
                    gather(i + 2, (j + 2) % U, isinstance(i, int) and i + 2 < U)
                if not first:
                    scatter(i - 1, (j - 1) % U, isinstance(i, int) and i == 1)

            loop(pool, body)
            scatter(TILES - 1, U - 1, False)
            pool.wait_ge(added, 16 * TILES)

        @block.scalar
        def _(act):
            def body(i, j, first, last):
                def turn(ii, jj, free):
                    act.wait_ge(x_turned, ii + 1)
                    if not free:
                        act.wait_ge(gu_made, ii - 1)
                    nc.scalar.activation(xT[:, jj % 2], ps_x[:].rearrange("p (c t) -> p c t", c=KC),
                                         ACT.Copy).then_inc(xT_kept, 1)

                if first:
                    turn(0, 0, True)
                if not last:
                    turn(i + 1, j + 1, isinstance(i, int) and i == 0)
                if not first:
                    act.wait_ge(h_turned, i)
                    if not (isinstance(i, int) and i == 1):
                        act.wait_ge(y_made, i - 1)
                    nc.scalar.activation(hT[:], ps_h[:].rearrange("p (c t) -> p c t", c=KC), ACT.Copy)\
                        .then_inc(hT_kept, 1)
                act.wait_ge(g_cut, i + 1)
                if not first:
                    act.wait_ge(h_made, i)
                nc.scalar.activation(sig[:], gate[:], ACT.Sigmoid, scale=ALPHA).then_inc(sig_made, 1)

            loop(act, body)
            act.wait_ge(h_turned, TILES)
            act.wait_ge(y_made, TILES - 1)
            nc.scalar.activation(hT[:], ps_h[:].rearrange("p (c t) -> p c t", c=KC), ACT.Copy).then_inc(hT_kept, 1)

        @block.vector
        def _(dve):
            def biases(i):
                par = dve.value_load(pick(G["parity"], i), min_val=0, max_val=1)
                return lambda k: bias[:, bass.ds(par, 1), k * D:(k + 1) * D].squeeze(1)

            def finish(i, j, first):
                b = biases(i)
                dve.wait_ge(y_made, i + 1)
                if not (isinstance(i, int) and i < U - 1):
                    dve.wait_ge(added, 16 * (i - U + 2))
                nc.vector.tensor_tensor(y[j][:], ps_y[:], b(2), ALU.add).then_inc(y_biased, 1)
                dve.wait_ge(y_biased, i + 1)
                nc.vector.tensor_scalar(y[j][:], y[j][:], pick(G["weight"], i), None, ALU.mult).then_inc(y_ready, 1)

            def body(i, j, first, last):
                b = biases(i)
                dve.wait_ge(gu_made, i + 1)
                if not first:
                    dve.wait_ge(h_made, i)
                nc.vector.tensor_tensor(gate[:], ps_g[:], b(0), ALU.add).then_inc(g_kept, 1)
                nc.vector.tensor_tensor(up[:], ps_u[:], b(1), ALU.add).then_inc(u_kept, 1)
                dve.wait_ge(g_kept, i + 1)
                nc.vector.tensor_scalar(gate[:], gate[:], LIMIT, None, ALU.min).then_inc(g_cut, 1)
                dve.wait_ge(u_kept, i + 1)
                nc.vector.tensor_scalar(up[:], up[:], LIMIT, -LIMIT, ALU.min, ALU.max).then_inc(u_cut, 1)
                dve.wait_ge(u_cut, i + 1)
                nc.vector.scalar_tensor_tensor(up[:], up[:], 1.0, gate[:], ALU.add, ALU.mult).then_inc(gated, 1)
                dve.wait_ge(gated, i + 1)
                dve.wait_ge(sig_made, i + 1)
                if not first:
                    dve.wait_ge(h_turned, i)
                nc.vector.tensor_tensor(h[:], up[:], sig[:], ALU.mult).then_inc(h_made, 1)
                if not first:
                    finish(i - 1, (j - 1) % U, False)

            loop(dve, body)
            finish(TILES - 1, U - 1, False)

        @block.tensor
        def _(pe):
            pe.wait_ge(w_loaded[1], 16)

            def turn(i, j):
                pe.wait_ge(gathered[j], 16 // U * (i - j) + 16)
                if not (isinstance(i, int) and i == 0):
                    pe.wait_ge(xT_kept, i)
                for c in range(KC):
                    mm = nc.tensor.transpose(ps_x[:, c * P:(c + 1) * P], x_rows[j][:, c * P:(c + 1) * P], ident[:])
                mm.then_inc(x_turned, 1)

            def weights(i):
                e = pe.value_load(pick(G["expert"], i), min_val=0, max_val=E_ - 1)
                par = pe.value_load(pick(G["parity"], i), min_val=0, max_val=1)
                return e, par

            def down(i, first):
                pe.wait_ge(h_made, i + 1)
                if not first:
                    pe.wait_ge(hT_kept, i)
                for c in range(KC):
                    mm = nc.tensor.transpose(ps_h[:, c * P:(c + 1) * P], h[:, c * P:(c + 1) * P], ident[:])
                mm.then_inc(h_turned, 1)
                par = pe.value_load(pick(G["parity"], i), min_val=0, max_val=1)
                pe.wait_ge(hT_kept, i + 1)
                if not first:
                    pe.wait_ge(y_biased, i)
                for c in range(KC):
                    mm = nc.tensor.matmul(ps_y[:], hT[:, c], w[:, bass.ds(par, 1), 2, c].squeeze(1),
                                          start=(c == 0), stop=(c == KC - 1))
                mm.then_inc(y_made, 1)

            turn(0, 0)

            def body(i, j, first, last):
                e, par = weights(i)
                pe.wait_ge(w_loaded[0], e // 2 * 32 + 32)
                pe.wait_ge(w_loaded[1], (e + 1) // 2 * 32 + 16)
                pe.wait_ge(xT_kept, i + 1)
                if not first:
                    pe.wait_ge(g_kept, i)
                    pe.wait_ge(u_kept, i)
                for k, out in ((0, ps_g), (1, ps_u)):
                    for c in range(KC):
                        mm = nc.tensor.matmul(out[:], xT[:, j % 2, c], w[:, bass.ds(par, 1), k, c].squeeze(1),
                                              start=(c == 0), stop=(c == KC - 1))
                mm.then_inc(gu_made, 1)
                if not last:
                    turn(i + 1, (j + 1) % U)
                if not first:
                    down(i - 1, isinstance(i, int) and i == 1)

            loop(pe, body)
            down(TILES - 1, False)


def last_norm(nc, S, out):
    with ExitStack() as ctx:
        def sb(name, shape, dt=F32):
            return ctx.enter_context(nc.sbuf_tensor(name, shape, dt))

        def sem(name):
            return ctx.enter_context(nc.semaphore(name))

        G4 = 4
        NG = NT // G4
        acc = sb("acc_sb", [P, NT, D])
        res = sb("res_sb", [P, NT, D])
        stats = sb("stats5", [P, NT, 6])
        mean_var = sb("mean_var5", [P, NT, 2])
        rstd = sb("rstd5", [P, NT])
        minus_half = sb("minus_half5", [P, NT])
        loaded = [sem(f"acc_loaded{i}") for i in range(NG)]
        stats_made, moments, var_eps, rstd_made, normed, stored, half_set = (
            sem("stats5_made"), sem("moments5"), sem("var_eps"), sem("rstd5_made"), sem("normed"), sem("stored"),
            sem("half5_set"))
        block = ctx.enter_context(nc.Block())

        @block.sync
        def _(sp):
            for g in range(NG):
                sp.dma_start(acc[:, G4 * g:G4 * g + G4], S["acc"][G4 * g * P:G4 * (g + 1) * P, :].rearrange(
                    "(t p) d -> p t d", p=P)).then_inc(loaded[g], 16)
            for g in range(NG):
                sp.wait_ge(normed, G4 * (g + 1))
                sp.dma_start(out[G4 * g * P:G4 * (g + 1) * P, :].rearrange("(t p) d -> p t d", p=P),
                             res[:, G4 * g:G4 * g + G4]).then_inc(stored, 16)
            sp.wait_ge(stored, 16 * NG)

        @block.gpsimd
        def _(pool):
            nc.gpsimd.memset(minus_half[:], -0.5).then_inc(half_set, 1)
            pool.wait_ge(half_set, 1)
            for g in range(NG):
                ts = slice(G4 * g, G4 * g + G4)
                pool.wait_ge(var_eps, g + 1)
                nc.gpsimd.tensor_tensor(rstd[:, ts], mean_var[:, ts, 1], minus_half[:, ts], ALU.pow).then_inc(
                    rstd_made, 1)

        @block.vector
        def _(dve):
            def moments_of(g):
                dve.wait_ge(loaded[g], 16)
                for t in range(G4 * g, G4 * g + G4):
                    nc.vector.bn_stats(stats[:, t], acc[:, t]).then_inc(stats_made, 1)
                dve.wait_ge(stats_made, G4 * (g + 1))
                for t in range(G4 * g, G4 * g + G4):
                    nc.vector.bn_aggr(mean_var[:, t], stats[:, t]).then_inc(moments, 1)
                dve.wait_ge(moments, G4 * (g + 1))
                ts = slice(G4 * g, G4 * g + G4)
                nc.vector.tensor_scalar(mean_var[:, ts, 1], mean_var[:, ts, 1], LN_EPS, None, ALU.add).then_inc(
                    var_eps, 1)

            def apply(g):
                dve.wait_ge(rstd_made, g + 1)
                for t in range(G4 * g, G4 * g + G4):
                    nc.vector.tensor_scalar(res[:, t], acc[:, t], mean_var[:, t, 0:1], rstd[:, t:t + 1],
                                            ALU.subtract, ALU.mult).then_inc(normed, 1)

            moments_of(0)
            for g in range(NG):
                if g + 1 < NG:
                    moments_of(g + 1)
                apply(g)


SCRATCH = {
    "parts": ([B, 2, 3, 16, 16, D], BF16),
    "rows_q": ([B, 9, D], BF16),
    "rows_k": ([B, 12, D], BF16),
    "max": ([B, 4, 3, 4 * D], BF16),
    "heads": ([B, 16, 2 * 16, D], F32),
    "inv": ([B, 16, D], F32),
    "x2": ([TOK + P, D], F32),
    "acc": ([TOK + P, D], F32),
}


def decoder_layer(nc, A, out):
    S = {name: nc.dram_tensor(f"scratch_{name}", shape, dt).ap() for name, (shape, dt) in SCRATCH.items()}
    with ExitStack() as ctx:
        def sb(name, shape, dt):
            return ctx.enter_context(nc.sbuf_tensor(name, shape, dt))

        G = {
            "token": sb("slot_token", [P, TILES], U32),
            "weight": sb("slot_weight", [P, TILES], F32),
            "expert": sb("tile_expert", [1, TILES], I32),
            "parity": sb("tile_parity", [1, TILES], I32),
            "last_tile": sb("expert_last", [1, E_], I32),
        }
        with ExitStack() as keep:
            x = keep.enter_context(nc.sbuf_tensor("x_keep", [P, NT, D], F32))
            linear_attention(nc, A, x)
            cross_attention(nc, A, S, x)
            route(nc, A, S, x, G)
        experts(nc, A, S, G)
        last_norm(nc, S, out)


def kernel(x, ctx_2048, mask_Bx1x2048_fk1, L0_attn_Wq, L0_attn_Wk, L0_attn_Wv, L0_attn_Wu, L0_attn_Wo,
           L0_xattn_Wq, L0_xattn_bq, L0_xattn_Wk, L0_xattn_bk, L0_xattn_Wv, L0_xattn_bv,
           L0_ffn_router_weight, L0_ffn_router_bias, L0_ffn_gate_up_proj, L0_ffn_gate_up_proj_bias,
           L0_ffn_down_proj, L0_ffn_down_proj_bias):
    import numpy as np
    import concourse.bacc as bacc
    from concourse.bass_utils import run_bass_kernel_spmd

    def rows_in(w):
        w = np.asarray(w)
        return w.reshape(-1, P, w.shape[-1]).transpose(1, 0, 2)

    tokens = np.asarray(x).reshape(TOK, D)
    mask = np.asarray(mask_Bx1x2048_fk1).reshape(B, D)
    gate_up, down = np.asarray(L0_ffn_gate_up_proj), np.asarray(L0_ffn_down_proj)
    gate_up_b = np.asarray(L0_ffn_gate_up_proj_bias)
    arrays = {
        "x": tokens,
        "xT": rows_in(tokens.T),
        "w1": np.stack([rows_in(w) for w in (L0_attn_Wq, L0_attn_Wk, L0_attn_Wv, L0_attn_Wu, L0_attn_Wo)]),
        "w2": np.stack([rows_in(np.asarray(w).T) for w in (L0_xattn_Wq, L0_xattn_Wk, L0_xattn_Wv)]),
        "bias_qk": np.stack([np.asarray(b).reshape(2, P).T for b in (L0_xattn_bq, L0_xattn_bk)], 1),
        "bias_v": np.asarray(L0_xattn_bv).reshape(1, 2 * P),
        "ctx": np.asarray(ctx_2048).reshape(B, 2, P, D).transpose(0, 2, 1, 3),
        "mask": mask,
        "mask_col": mask.reshape(B, 4, P).transpose(2, 0, 1),
        "router_w": rows_in(np.asarray(L0_ffn_router_weight).T),
        "router_b": np.asarray(L0_ffn_router_bias).reshape(1, E_),
        "w_expert": np.stack([gate_up[:, :, ::2], gate_up[:, :, 1::2], down], 1).reshape(
            E_, 3, KC, P, D).transpose(0, 3, 1, 2, 4),
        "b_expert": np.concatenate([gate_up_b[:, ::2], gate_up_b[:, 1::2], np.asarray(L0_ffn_down_proj_bias)], 1),
        "ident": np.eye(P, dtype=np.float32),
        "kv_mask": np.kron(np.eye(4), np.ones((32, 32))).astype(np.float32),
        "before": np.triu(np.ones((P, P), np.float32), 1),
        "iota_p": np.arange(P, dtype=np.float32).reshape(P, 1),
        "iota_f": np.tile(np.arange(P, dtype=np.float32), (P, 1)),
    }
    nc = bacc.Bacc("TRN2", target_bir_lowering=False, num_devices=1)
    ins, aps = {}, {}
    for name, a in arrays.items():
        ins[f"in_{name}"] = np.ascontiguousarray(a)
        aps[name] = nc.dram_tensor(f"in_{name}", a.shape, F32, kind="ExternalInput").ap()
    out = nc.dram_tensor("out", [TOK, D], F32, kind="ExternalOutput").ap()
    decoder_layer(nc, aps, out)
    r = run_bass_kernel_spmd(nc, [ins], core_ids=[0])
    return r.results[0]["out"].reshape(B, L, D)
```

```python
from contextlib import ExitStack

import concourse.bass as bass
from concourse import mybir

F32 = mybir.dt.float32
F32R = mybir.dt.float32r
BF16 = mybir.dt.bfloat16
I32 = mybir.dt.int32
U32 = mybir.dt.uint32
ALU = mybir.AluOpType
ACT = mybir.ActivationFunctionType
AX = mybir.AxisListType

P = 128
B, L, D = 8, 256, 512
TOK = B * L
NT = TOK // P
KC = D // P
LN_EPS = 1e-5
SPLITS = ((0, 0), (0, 1), (1, 0))


def scaled(count, group, offset):
    return group * count + offset


def spare_registers(engine, name, n):
    return [engine.alloc_register(name=f"{name}_{i}") for i in range(n)]


def wait_apart(engine, registers, constant, *waits):
    values = []
    for (_, value), register in zip(waits, registers):
        if not isinstance(value, int):
            engine.reg_mov(register, value)
            value = register
        values.append(value)
    engine.wait_ge(*constant)
    for (semaphore, _), value in zip(waits, values):
        engine.wait_ge(semaphore, value)


def linear_attention(nc, A, x1):
    H, DH = 16, 32
    INV_SCALE = DH ** -0.5
    NG, TPG = 4, 4
    GT = TPG * P
    WQ, WK, WV, WU, WO = range(5)
    with ExitStack() as ctx:
        def sb(name, shape, dt=F32):
            return ctx.enter_context(nc.sbuf_tensor(name, shape, dt))

        def sem(name):
            return ctx.enter_context(nc.semaphore(name))

        w_raw = sb("w_raw", [P, 2, KC, D])
        w_split = sb("w_split", [P, 5, 2, KC, D], F32R)
        xT_raw = sb("xT_raw", [P, KC, GT])
        xT_split = sb("xT_split", [P, 2, KC, GT], F32R)
        x_tok = sb("x_tok", [P, 2, D])
        qT = sb("qT", [P, KC, GT])
        k_sb = sb("k_sb", [P, TPG, D])
        v_sb = sb("v_sb", [P, TPG, D])
        u_sb = sb("u_sb", [P, TPG, D])
        kv_mask = sb("kv_mask", [P, P])
        kv_sb = sb("kv_sb", [P, KC, P])
        ident = sb("ident1", [P, P])
        o_sq = sb("o_sq", [P, D])
        o_ss = sb("o_ss", [P, H])
        o_rn = sb("o_rn", [P, H])
        o_norm = sb("o_norm", [P, D])
        o_sb = sb("o_sb", [P, D])
        oT_split = sb("oT_split", [P, 2, KC, P], F32R)
        y_sb = sb("y_sb", [P, D])
        stats = sb("stats", [P, 6])
        mean_var = sb("mean_var", [P, 2])
        rstd = sb("rstd", [P, 1])
        minus_half = sb("minus_half", [P, H])

        def bank(name):
            return ctx.enter_context(nc.psum_tensor(name, [P, D], F32))

        ps_q0, ps_k, ps_v, ps_u = bank("ps_q0"), bank("ps_k"), bank("ps_v"), bank("ps_u")
        ps_kv, ps_o, ps_t, ps_w = bank("ps_kv"), bank("ps_o"), bank("ps_t"), bank("ps_w")
        q_banks = [ps_k, ps_v, ps_u, ps_q0]

        w_loaded = [sem("w_loaded_even"), sem("w_loaded_odd")]
        consts_loaded = sem("consts_loaded")
        w_hi = sem("w_hi")
        w_lo = sem("w_lo")
        xT_loaded = sem("xT_loaded")
        xT_hi = sem("xT_hi")
        xT_lo = sem("xT_lo")
        x_loaded = [sem("x_loaded_even"), sem("x_loaded_odd")]
        q_made, q_kept = sem("q_made"), sem("q_kept")
        proj_made = sem("proj_made")
        k_kept, v_kept, u_kept = sem("k_kept"), sem("v_kept"), sem("u_kept")
        kv_made, kv_kept = sem("kv_made"), sem("kv_kept")
        o_made, o_squared, o_summed, o_scale, o_normed, o_gated = (
            sem("o_made"), sem("o_squared"), sem("o_summed"), sem("o_scale"), sem("o_normed"), sem("o_gated"))
        t_made, t_hi, t_lo = sem("t_made"), sem("t_hi"), sem("t_lo")
        y_made, y_added, y_stats, y_moments, y_rstd, x1_made = (
            sem("y_made"), sem("y_added"), sem("y_stats"), sem("y_moments"), sem("y_rstd"), sem("x1_made"))
        half_set, pool_step, clamp = sem("half_set"), sem("pool_step"), sem("clamp")

        block = ctx.enter_context(nc.Block())

        @block.sync
        def _(sp):
            sp.dma_start(kv_mask[:], A["kv_mask"]).then_inc(consts_loaded, 16)
            sp.dma_start(ident[:], A["ident"]).then_inc(consts_loaded, 16)

            def load_w(w):
                if w >= 2:
                    sp.wait_ge(w_lo, w - 1)
                sp.dma_start(w_raw[:, w % 2], A["w1"][w]).then_inc(w_loaded[w % 2], 16)

            load_w(WQ)
            load_w(WK)
            sp.dma_start(xT_raw[:], A["xT"][:, :, 0:GT]).then_inc(xT_loaded, 16)
            for w in (WV, WU, WO):
                load_w(w)

            with sp.Fori(1, NG) as g:
                sp.wait_ge(xT_lo, TPG * g)
                sp.dma_start(xT_raw[:], A["xT"][:, :, bass.ds(g * GT, GT)]).then_inc(xT_loaded, 16)

        @block.gpsimd
        def _(pool):
            nc.gpsimd.memset(minus_half[:], -0.5).then_inc(half_set, 1)
            pool.wait_ge(half_set, 1)

            def split_x(g, i):
                pool.wait_ge(xT_hi, TPG * g + i + 1)
                cols = slice(i * P, i * P + P)
                nc.gpsimd.tensor_tensor(xT_split[:, 1, :, cols], xT_raw[:, :, cols],
                                        xT_split[:, 0, :, cols].bitcast(F32), ALU.subtract).then_inc(xT_lo, 1)

            for w in range(5):
                pool.wait_ge(w_hi, w + 1)
                if w == 1:
                    for i in range(TPG):
                        split_x(0, i)
                nc.gpsimd.tensor_tensor(w_split[:, w, 1], w_raw[:, w % 2], w_split[:, w, 0].bitcast(F32),
                                        ALU.subtract).then_inc(w_lo, 1)

            def head_scale(t):
                pool.wait_ge(o_summed, t + 1)
                nc.gpsimd.tensor_tensor(o_rn[:], o_ss[:], minus_half[:], ALU.pow).then_inc(o_scale, 1)

            def gate(t, slot):
                pool.wait_ge(o_normed, t + 1)
                pool.wait_ge(u_kept, t + 1)
                if not (isinstance(t, int) and t < 1):
                    pool.wait_ge(t_made, t)
                nc.gpsimd.tensor_tensor(o_sb[:], o_norm[:], u_sb[:, slot], ALU.mult).then_inc(o_gated, 1)

            def token_rstd(t):
                pool.wait_ge(y_moments, t + 1)
                nc.gpsimd.tensor_tensor(rstd[:], mean_var[:, 1:2], minus_half[:, 0:1], ALU.pow).then_inc(y_rstd, 1)

            def load_x(t, slot):
                if not (isinstance(t, int) and t < 2):
                    pool.wait_ge(y_added, t - 1)
                pool.dma_start(x_tok[:, slot], A["x"][bass.ds(t * P, P), :]).then_inc(x_loaded[slot], 16)

            def group(g, first, last):
                t = TPG * g
                if first:
                    load_x(0, 0)
                    load_x(1, 1)
                else:
                    head_scale(t - 1)
                    gate(t - 1, 3)
                    token_rstd(t - 2)
                    load_x(t, 0)
                    token_rstd(t - 1)
                    load_x(t + 1, 1)
                if not last:
                    split_x(g + 1, 0)
                    split_x(g + 1, 1)
                head_scale(t)
                gate(t, 0)
                head_scale(t + 1)
                if not last:
                    split_x(g + 1, 2)
                gate(t + 1, 1)
                token_rstd(t)
                load_x(t + 2, 0)
                token_rstd(t + 1)
                load_x(t + 3, 1)
                if not last:
                    split_x(g + 1, 3)
                head_scale(t + 2)
                gate(t + 2, 2)

            group(0, True, False)
            with pool.Fori(1, NG - 1) as g:
                group(g, False, False)
            group(NG - 1, False, True)
            head_scale(NT - 1)
            gate(NT - 1, 3)
            token_rstd(NT - 2)
            token_rstd(NT - 1)

        @block.scalar
        def _(act):
            def split_w(w):
                act.wait_ge(w_loaded[w % 2], 16 * (w // 2 + 1))
                nc.scalar.activation(w_split[:, w, 0], w_raw[:, w % 2], ACT.Copy).then_inc(w_hi, 1)

            def split_x(g, i, first=False):
                act.wait_ge(xT_loaded, 16 * g + 16)
                if not first:
                    act.wait_ge(proj_made, 3 * (TPG * (g - 1) + i + 1))
                cols = slice(i * P, i * P + P)
                nc.scalar.activation(xT_split[:, 0, :, cols], xT_raw[:, :, cols], ACT.Copy).then_inc(xT_hi, 1)

            def q_block(g, m):
                act.wait_ge(q_made, KC * g + m + 1)
                nc.scalar.activation(qT[:, m], q_banks[m][:], ACT.Relu, scale=INV_SCALE).then_inc(q_kept, 1)

            def keep_k(t, slot):
                act.wait_ge(proj_made, 3 * t + 1)
                nc.scalar.activation(k_sb[:, slot], ps_k[:], ACT.Relu, scale=INV_SCALE).then_inc(k_kept, 1)

            def keep_u(t, slot):
                act.wait_ge(proj_made, 3 * t + 3)
                nc.scalar.activation(u_sb[:, slot], ps_u[:], ACT.Silu).then_inc(u_kept, 1)

            def square(t, o_bank):
                act.wait_ge(o_made, t + 1)
                if not (isinstance(t, int) and t < 1):
                    act.wait_ge(o_summed, t)
                nc.scalar.activation(o_sq[:], o_bank[:], ACT.Square).then_inc(o_squared, 1)

            def keep_oT(t):
                act.wait_ge(t_made, t + 1)
                if not (isinstance(t, int) and t < 1):
                    act.wait_ge(y_made, t)
                nc.scalar.activation(oT_split[:, 0], ps_t[:].rearrange("p (c t) -> p c t", c=KC),
                                     ACT.Copy).then_inc(t_hi, 1)

            def group(g, first, last):
                t = TPG * g
                if not first:
                    square(t - 1, ps_q0)
                q_block(g, 0)
                q_block(g, 1)
                if not first:
                    keep_oT(t - 2)
                q_block(g, 2)
                if not first:
                    keep_oT(t - 1)
                q_block(g, 3)
                keep_k(t, 0)
                keep_u(t, 0)
                if not last:
                    split_x(g + 1, 0)
                keep_k(t + 1, 1)
                keep_u(t + 1, 1)
                if not last:
                    split_x(g + 1, 1)
                square(t, ps_o)
                keep_k(t + 2, 2)
                square(t + 1, ps_q0)
                keep_u(t + 2, 2)
                if not last:
                    split_x(g + 1, 2)
                keep_oT(t)
                keep_k(t + 3, 3)
                keep_oT(t + 1)
                keep_u(t + 3, 3)
                if not last:
                    split_x(g + 1, 3)
                square(t + 2, ps_o)

            split_w(WQ)
            split_w(WK)
            for i in range(TPG):
                split_x(0, i, True)
            for w in (WV, WU, WO):
                split_w(w)
            group(0, True, False)
            with act.Fori(1, NG - 1) as g:
                group(g, False, False)
            group(NG - 1, False, True)
            square(NT - 1, ps_q0)
            keep_oT(NT - 2)
            keep_oT(NT - 1)

        @block.vector
        def _(dve):
            held = spare_registers(dve, "held1", 1)

            def keep_v(t, slot):
                dve.wait_ge(proj_made, 3 * t + 2)
                nc.vector.tensor_copy(v_sb[:, slot], ps_v[:]).then_inc(v_kept, 1)

            def keep_kv(b):
                dve.wait_ge(kv_made, b + 1)
                if not (isinstance(b, int) and b < 1):
                    dve.wait_ge(o_made, 2 * b)
                nc.vector.tensor_tensor(kv_sb[:], ps_kv[:].rearrange("p (c v) -> p c v", c=KC),
                                        kv_mask[:].unsqueeze(1).to_broadcast([P, KC, P]),
                                        ALU.mult).then_inc(kv_kept, 1)

            def norm(t, o_bank):
                dve.wait_ge(o_squared, t + 1)
                if not (isinstance(t, int) and t < 1):
                    dve.wait_ge(o_scale, t)
                nc.vector.tensor_reduce(o_ss[:], o_sq[:].rearrange("p (h d) -> p h d", h=H), AX.X,
                                        ALU.add).then_inc(clamp, 1)
                dve.wait_ge(clamp, t + 1)
                nc.vector.tensor_scalar(o_ss[:], o_ss[:], 1.0 / DH, 1e-24, ALU.mult, ALU.max).then_inc(o_summed, 1)
                dve.wait_ge(o_scale, t + 1)
                if not (isinstance(t, int) and t < 1):
                    dve.wait_ge(o_gated, t)
                nc.vector.tensor_tensor(o_norm[:].rearrange("p (h d) -> p h d", h=H),
                                        o_bank[:].rearrange("p (h d) -> p h d", h=H),
                                        o_rn[:].unsqueeze(2).to_broadcast([P, H, DH]),
                                        ALU.mult).then_inc(o_normed, 1)

            def keep_oT(t):
                dve.wait_ge(t_hi, t + 1)
                nc.vector.tensor_tensor(oT_split[:, 1], ps_t[:].rearrange("p (c t) -> p c t", c=KC),
                                        oT_split[:, 0].bitcast(F32), ALU.subtract).then_inc(t_lo, 1)

            def layernorm(t, slot):
                dve.wait_ge(y_made, t + 1)
                dve.wait_ge(x_loaded[slot], 8 * (t - slot) + 16)
                nc.vector.tensor_tensor(y_sb[:], ps_w[:], x_tok[:, slot], ALU.add).then_inc(y_added, 1)
                dve.wait_ge(y_added, t + 1)
                nc.vector.bn_stats(stats[:], y_sb[:]).then_inc(y_stats, 1)
                wait_apart(dve, held, (half_set, 1), (y_stats, 3 * t + 1))
                nc.vector.bn_aggr(mean_var[:], stats[:]).then_inc(y_stats, 1)
                dve.wait_ge(y_stats, 3 * t + 2)
                nc.vector.tensor_scalar(mean_var[:, 1:2], mean_var[:, 1:2], LN_EPS, None,
                                        ALU.add).then_inc(y_moments, 1)
                dve.wait_ge(y_rstd, t + 1)
                nc.vector.tensor_scalar(x1[:, bass.ds(t, 1), :].squeeze(1) if not isinstance(t, int) else x1[:, t, :],
                                        y_sb[:], mean_var[:, 0:1], rstd[:, 0:1],
                                        ALU.subtract, ALU.mult).then_inc(y_stats, 1)

            def group(g, first):
                t = TPG * g
                if not first:
                    norm(t - 1, ps_q0)
                    keep_oT(t - 2)
                    layernorm(t - 2, 0)
                    keep_oT(t - 1)
                    layernorm(t - 1, 1)
                keep_v(t, 0)
                keep_v(t + 1, 1)
                keep_kv(2 * g)
                norm(t, ps_o)
                keep_v(t + 2, 2)
                norm(t + 1, ps_q0)
                keep_oT(t)
                layernorm(t, 0)
                keep_v(t + 3, 3)
                keep_oT(t + 1)
                keep_kv(2 * g + 1)
                layernorm(t + 1, 1)
                norm(t + 2, ps_o)

            dve.wait_ge(consts_loaded, 32)
            dve.wait_ge(half_set, 1)
            group(0, True)
            with dve.Fori(1, NG) as g:
                group(g, False)
            keep_oT(NT - 2)
            norm(NT - 1, ps_q0)
            layernorm(NT - 2, 0)
            keep_oT(NT - 1)
            layernorm(NT - 1, 1)

        @block.tensor
        def _(pe):
            def q_block(g, m, first):
                if m == 0:
                    pe.wait_ge(xT_lo, TPG * g + TPG)
                if first:
                    pe.wait_ge(w_lo, 1)
                else:
                    pe.wait_ge([k_kept, v_kept, u_kept, o_normed][m], TPG * g)
                n = 0
                for wi, xi in SPLITS:
                    for c in range(KC):
                        mm = nc.tensor.matmul(q_banks[m][:], w_split[:, WQ, wi, c, m * P:(m + 1) * P],
                                              xT_split[:, xi, c, :], start=(n == 0), stop=(n == 3 * KC - 1))
                        n += 1
                mm.then_inc(q_made, 1)

            def project(g, i, w, first):
                t = TPG * g + i
                if first and i == 0:
                    pe.wait_ge(w_lo, w + 1)
                if w == WK:
                    pe.wait_ge(q_kept, KC * g + 1) if i == 0 else pe.wait_ge(k_kept, t)
                elif w == WV:
                    pe.wait_ge(q_kept, KC * g + 2) if i == 0 else pe.wait_ge(v_kept, t)
                else:
                    pe.wait_ge(q_kept, KC * g + 3) if i == 0 else pe.wait_ge(u_kept, t)
                out = {WK: ps_k, WV: ps_v, WU: ps_u}[w]
                n = 0
                for wi, xi in SPLITS:
                    for c in range(KC):
                        mm = nc.tensor.matmul(out[:], xT_split[:, xi, c, i * P:(i + 1) * P],
                                              w_split[:, w, wi, c, :], start=(n == 0), stop=(n == 3 * KC - 1))
                        n += 1
                mm.then_inc(proj_made, 1)

            def kv(b, slot):
                pe.wait_ge(k_kept, 2 * b + 2)
                pe.wait_ge(v_kept, 2 * b + 2)
                if not (isinstance(b, int) and b < 1):
                    pe.wait_ge(kv_kept, b)
                for c in range(KC):
                    for i in range(2):
                        mm = nc.tensor.matmul(ps_kv[:, c * P:(c + 1) * P], k_sb[:, slot + i, c * P:(c + 1) * P],
                                              v_sb[:, slot + i, c * P:(c + 1) * P], start=(i == 0), stop=(i == 1))
                mm.then_inc(kv_made, 1)

            def attend(g, i, o_bank, first):
                t = TPG * g + i
                if i == 0:
                    pe.wait_ge(q_kept, KC * g + 4)
                    pe.wait_ge(kv_kept, 2 * g + 1)
                if i == 2:
                    pe.wait_ge(kv_kept, 2 * g + 2)
                    pe.wait_ge(o_normed, t - 1)
                elif i == 3:
                    pe.wait_ge(o_normed, t - 1)
                elif i == 0 and not first:
                    pe.wait_ge(o_normed, t - 1)
                for c in range(KC):
                    mm = nc.tensor.matmul(o_bank[:, c * P:(c + 1) * P], qT[:, c, i * P:(i + 1) * P],
                                          kv_sb[:, c, :], start=True, stop=True)
                mm.then_inc(o_made, 1)

            def transpose_o(t):
                pe.wait_ge(o_gated, t + 1)
                if not (isinstance(t, int) and t < 1):
                    pe.wait_ge(t_lo, t)
                for c in range(KC):
                    mm = nc.tensor.transpose(ps_t[:, c * P:(c + 1) * P], o_sb[:, c * P:(c + 1) * P], ident[:])
                mm.then_inc(t_made, 1)

            def project_out(t):
                pe.wait_ge(t_lo, t + 1)
                if isinstance(t, int) and t < 1:
                    pe.wait_ge(w_lo, WO + 1)
                else:
                    pe.wait_ge(y_added, t)
                n = 0
                for wi, oi in SPLITS:
                    for c in range(KC):
                        mm = nc.tensor.matmul(ps_w[:], oT_split[:, oi, c, :], w_split[:, WO, wi, c, :],
                                              start=(n == 0), stop=(n == 3 * KC - 1))
                        n += 1
                mm.then_inc(y_made, 1)

            def group(g, first):
                t = TPG * g
                q_block(g, 0, first)
                q_block(g, 1, first)
                if not first:
                    transpose_o(t - 2)
                q_block(g, 2, first)
                if not first:
                    project_out(t - 2)
                    transpose_o(t - 1)
                q_block(g, 3, first)
                if not first:
                    project_out(t - 1)
                project(g, 0, WK, first)
                project(g, 0, WV, first)
                project(g, 0, WU, first)
                project(g, 1, WK, first)
                project(g, 1, WV, first)
                project(g, 1, WU, first)
                kv(2 * g, 0)
                project(g, 2, WK, first)
                attend(g, 0, ps_o, first)
                attend(g, 1, ps_q0, first)
                project(g, 2, WV, first)
                project(g, 2, WU, first)
                transpose_o(t)
                project(g, 3, WK, first)
                project_out(t)
                project(g, 3, WV, first)
                transpose_o(t + 1)
                kv(2 * g + 1, 2)
                project(g, 3, WU, first)
                project_out(t + 1)
                attend(g, 2, ps_o, first)
                attend(g, 3, ps_q0, first)

            pe.wait_ge(consts_loaded, 32)
            group(0, True)
            with pe.Fori(1, NG) as g:
                group(g, False)
            transpose_o(NT - 2)
            project_out(NT - 2)
            transpose_o(NT - 1)
            project_out(NT - 1)
def cross_attention(nc, A, S, x):
    H, DH, C, T = 16, 16, 2 * P, D
    NQ, HQ, NC = 4, 4, T // P
    PENALTY = 4e6
    ROWS_A, ROWS_B = 6 * DH + 9, 6 * DH + 12
    STEPS = NQ * NC
    MISC0, MISC = 7, 10
    STACK_DMAS = 8
    with ExitStack() as ctx:
        def sb(name, shape, dt=F32):
            return ctx.enter_context(nc.sbuf_tensor(name, shape, dt))

        def sem(name):
            return ctx.enter_context(nc.semaphore(name))

        w2 = sb("w2", [P, 3, 2, C])
        bias_qk = sb("bias_qk", [P, 2, 2])
        bias_v = sb("bias_v", [P, C])
        mask_col = sb("mask_col", [P, B, NC])
        mask_now = sb("mask_now", [P, NC])
        ident = sb("ident2", [P, P])
        m_rows = sb("m_rows", [B, T])
        pen_rows = sb("pen_rows", [B, T])
        rest_rows = sb("rest_rows", [B, T])
        row_parts = sb("row_parts", [B, 7, T], BF16)
        ctx_sb = sb("ctx_sb", [P, 2, T])
        mask_in = sb("mask_in", [P, T])
        mask_out = sb("mask_out", [P, T])
        full = sb("full", [P, 2, T])
        rest = sb("rest", [P, 2, T])
        parts = sb("parts", [P, 2, 3, T], BF16)
        q_stack = sb("q_stack", [P, H, T], BF16)
        k_stack = sb("k_stack", [P, H, T], BF16)
        v_stage = sb("v_stage", [P, NC, C])
        v_aug = sb("v_aug", [P, NC, H, 32])
        probs = sb("probs", [P, 2, HQ, T])
        row_max = sb("row_max", [P, 2, HQ, NC])
        neg_max = sb("neg_max", [HQ * NC, P])
        neg_rest = sb("neg_rest", [HQ * NC, P])
        neg_parts = sb("neg_parts", [HQ * NC, 3, P], BF16)
        o_sb = sb("o_sb2", [P, 2, T])
        den = sb("den", [P, H * T // P])
        inv = sb("inv", [P, H * T // P])
        num_sb = sb("num_sb", [P, 2, T])
        inv_sb = sb("inv_sb", [P, 2, T])
        stats = sb("stats2", [P, 2, 6])
        mean_var = sb("mean_var2", [P, 2, 2])
        rstd = sb("rstd2", [P, 2])
        minus_half = sb("minus_half2", [P, 2])

        ps_a = [ctx.enter_context(nc.psum_tensor(f"ps_a{i}", [P, 2, T], F32)) for i in range(2)]
        ps_b = [ctx.enter_context(nc.psum_tensor(f"ps_b{i}", [P, T], F32)) for i in range(2)]
        ps_pv = ctx.enter_context(nc.psum_tensor("ps_pv", [P, T], F32))
        ps_misc = ctx.enter_context(nc.psum_tensor("ps_misc", [P, T], F32))

        consts_loaded = sem("consts2_loaded")
        mask_step, rows_made, rows_stored = sem("mask_step"), sem("rows_made"), sem("rows_stored")
        consts_set = sem("consts2_set")
        in_loaded = sem("in_loaded")
        misc_made, misc_kept = sem("misc_made"), sem("misc_kept")
        part1, rest1, part2, part3 = sem("part1"), sem("rest1"), sem("part2"), sem("part3")
        parts_stored = [sem("parts_stored_q"), sem("parts_stored_k")]
        stack_loaded = [sem(f"stack_loaded{i}") for i in range(NQ)]
        a_made = [sem("a_made0"), sem("a_made1")]
        a_kept = [sem("a_kept0"), sem("a_kept1")]
        max_step, max_ready = sem("max_step"), sem("max_ready")
        max_stored = sem("max_stored")
        max_loaded = [sem(f"max_loaded{i}") for i in range(NQ)]
        b_made, exp_done = sem("b_made"), sem("exp_done")
        v_staged, v_filled = sem("v_staged"), sem("v_filled")
        mask_now_set = sem("mask_now_set")
        pv_made, o_kept = sem("pv_made"), sem("o_kept")
        o_stored = [sem("o_stored0"), sem("o_stored1")]
        den_loaded, inv_made, inv_stored, out_loaded = (
            sem("den_loaded"), sem("inv_made"), sem("inv_stored"), sem("out_loaded"))
        attn_scaled, attn_masked = sem("attn_scaled"), sem("attn_masked")
        y_added, y_stats, y_moments, y_rstd, x2_made, x2_stored = (
            sem("y2_added"), sem("y2_stats"), sem("y2_moments"), sem("y2_rstd"), sem("x2_made"), sem("x2_stored"))

        block = ctx.enter_context(nc.Block())

        def at(ref, i):
            return ref[i] if isinstance(i, int) else ref[bass.ds(i, 1)].squeeze(0)

        @block.sync
        def _(sp):
            held = spare_registers(sp, "held2", 1)

            def wait(semaphore, value):
                wait_apart(sp, held, (consts_loaded, 96), (semaphore, value))

            sp.dma_start(m_rows[:], A["mask"]).then_inc(consts_loaded, 16)
            sp.dma_start(w2[:], A["w2"].rearrange("w p c o -> p w c o")).then_inc(consts_loaded, 16)
            sp.dma_start(bias_qk[:], A["bias_qk"]).then_inc(consts_loaded, 16)
            sp.dma_start(bias_v[:], A["bias_v"].to_broadcast([P, C])).then_inc(consts_loaded, 16)
            sp.dma_start(mask_col[:], A["mask_col"]).then_inc(consts_loaded, 16)
            sp.dma_start(ident[:], A["ident"]).then_inc(consts_loaded, 16)

            def load_inputs(b):
                sp.dma_start(ctx_sb[:], at(A["ctx"], b)).then_inc(in_loaded, 16)
                sp.dma_start(mask_in[:], at(A["mask"], b).unsqueeze(0).to_broadcast([P, T])).then_inc(in_loaded, 16)

            def store_parts(b, i):
                qk, o = i % 2, i // 2
                wait(part3, 4 * b + i + 1)
                for j in range(3):
                    sp.dma_start(at(S["parts"], b)[qk, j, :, 8 * o:8 * o + 8, :].rearrange("d h t -> h d t"),
                                 parts[:, qk, j]).then_inc(parts_stored[qk], 16)

            def load_stack(b, q, first):
                if not first:
                    wait(b_made, 64 * (b - 1) + 16 * (q + 1))
                heads = slice(HQ * q, HQ * q + HQ)
                for qk, stack in ((0, q_stack), (1, k_stack)):
                    wait(parts_stored[qk], 96 * b + 48 * (q // 2) + 48)
                    src = at(S["parts"], b)[qk, :, :, heads, :].rearrange("j d h t -> j d (h t)")
                    at_row = 0
                    for n in (3, 2, 1):
                        dst = stack[at_row:at_row + n * DH, heads, :].rearrange("r h t -> r (h t)")
                        if qk == 0:
                            one = src[0:n].rearrange("j d t -> (j d) t")
                            sp.dma_start(dst, one).then_inc(stack_loaded[q], 16)
                        else:
                            one = src[3 - n:4 - n].to_broadcast([n, DH, HQ * T])
                            sp.dma_start(dst, one).then_inc(stack_loaded[q], 16)
                        at_row += n * DH
                sp.dma_start(q_stack[6 * DH:ROWS_A, heads, :],
                             at(S["rows_q"], b).unsqueeze(1).to_broadcast([9, HQ, T])).then_inc(stack_loaded[q], 16)
                sp.dma_start(k_stack[6 * DH:ROWS_B, heads, :],
                             at(S["rows_k"], b).unsqueeze(1).to_broadcast([12, HQ, T])).then_inc(stack_loaded[q], 16)

            def move_max(b, q):
                wait(max_ready, 4 * b + q + 1)
                d = at(S["max"], b)[q]
                sp.dma_start(d.rearrange("j (n t) -> n j t", t=P), neg_parts[:]).then_inc(max_stored, 16)
                wait(max_stored, 16 * (4 * b + q + 1))
                sp.dma_start(q_stack[ROWS_A:ROWS_B, HQ * q:HQ * q + HQ, :],
                             d.rearrange("j (h t) -> j h t", h=HQ)).then_inc(max_loaded[q], 16)

            def store_o(b, q):
                wait(o_kept, 4 * b + q + 1)
                sp.dma_start(at(S["heads"], b)[HQ * q:HQ * q + HQ].rearrange("h r t -> (h r) t"),
                             o_sb[:, q % 2, :]).then_inc(o_stored[q % 2], 16)

            def load_den(b, first=False):
                if not first:
                    wait(x2_made, 2 * b)
                wait(o_stored[0], 32 * (b + 1))
                wait(o_stored[1], 32 * (b + 1))
                sp.dma_start(den[:], at(S["heads"], b)[:, DH, :].rearrange("h (a t) -> h a t", a=8)).then_inc(
                    den_loaded, 16)
                for o in range(2):
                    sp.dma_start(num_sb[:, o, :], at(S["heads"], b)[8 * o:8 * o + 8, 0:DH, :]).then_inc(out_loaded, 16)

            def load_out(b):
                wait(inv_made, b + 1)
                sp.dma_start(at(S["inv"], b).rearrange("h (a t) -> (h a) t", a=8), inv[:]).then_inc(inv_stored, 16)
                sp.dma_start(mask_out[:], at(A["mask"], b).unsqueeze(0).to_broadcast([P, T])).then_inc(out_loaded, 16)
                wait(inv_stored, 16 * (b + 1))
                for o in range(2):
                    sp.dma_start(inv_sb[:, o, :], at(S["inv"], b)[8 * o:8 * o + 8].unsqueeze(1).to_broadcast(
                        [8, DH, T])).then_inc(out_loaded, 16)

            def store_x2(b):
                wait(x2_made, 2 * b + 2)
                sp.dma_start(S["x2"][bass.ds(b * L, L), :].rearrange("(i p) d -> p i d", p=P),
                             x[:, bass.ds(b * 2, 2), :]).then_inc(x2_stored, 16)

            load_inputs(0)
            for r, i in enumerate((0, 1, 2, 3, 3, 3, 4, 4, 5)):
                if r == 0:
                    wait(rows_made, 6)
                sp.dma_start(S["rows_q"][:, r, :], row_parts[:, i, :]).then_inc(rows_stored, 16)
            for r, i in enumerate((6, 6, 6, 0, 1, 2, 0, 1, 0, 6, 6, 6)):
                sp.dma_start(S["rows_k"][:, r, :], row_parts[:, i, :]).then_inc(rows_stored, 16)
            wait(rows_stored, 16 * 21)
            for i in range(4):
                store_parts(0, i)
            wait(v_staged, 2)
            load_inputs(1)
            for q in range(NQ):
                load_stack(0, q, True)
            move_max(0, 0)

            def batch(b, first, last, second=False):
                if not first:
                    store_o(b - 1, 3)
                    load_stack(b, 3, False)
                    load_den(b - 1, second)
                move_max(b, 1)
                if not first:
                    load_out(b - 1)
                if not last:
                    store_parts(b + 1, 0)
                    store_parts(b + 1, 1)
                store_o(b, 0)
                if not last:
                    load_stack(b + 1, 0, False)
                move_max(b, 2)
                if not last:
                    store_parts(b + 1, 2)
                    store_parts(b + 1, 3)
                store_o(b, 1)
                if not last:
                    load_stack(b + 1, 1, False)
                move_max(b, 3)
                store_o(b, 2)
                if not last:
                    load_stack(b + 1, 2, False)
                    move_max(b + 1, 0)
                if not first:
                    store_x2(b - 1)

            def inputs_after(b):
                wait(v_staged, 2 * b + 4)
                load_inputs(b + 2)

            batch(0, True, False)
            inputs_after(0)
            batch(1, False, False, True)
            inputs_after(1)
            with sp.Fori(2, B - 2) as b:
                batch(b, False, False)
                inputs_after(b)
            batch(B - 2, False, False)
            batch(B - 1, False, True)
            store_o(B - 1, 3)
            load_den(B - 1)
            load_out(B - 1)
            store_x2(B - 1)
            wait(x2_stored, 16 * B)

        @block.gpsimd
        def _(pool):
            nc.gpsimd.memset(minus_half[:], -0.5).then_inc(consts_set, 1)
            nc.gpsimd.memset(v_aug[:], 1.0).then_inc(consts_set, 1)
            pool.wait_ge(consts_set, 2)

            def split(b, i):
                k, s = 4 * b + i, i % 2
                pool.wait_ge(part1, k + 1)
                nc.gpsimd.tensor_tensor(rest[:, s], full[:, s], parts[:, s, 0], ALU.subtract).then_inc(rest1, 1)
                pool.wait_ge(part2, k + 1)
                nc.gpsimd.tensor_tensor(parts[:, s, 2], rest[:, s], parts[:, s, 1], ALU.subtract).then_inc(part3, 1)

            def finish_heads(b):
                pool.wait_ge(out_loaded, 80 * b + 80)
                nc.gpsimd.tensor_tensor(inv_sb[:], inv_sb[:], mask_out[:].unsqueeze(1).to_broadcast([P, 2, T]),
                                        ALU.mult).then_inc(attn_scaled, 1)
                pool.wait_ge(attn_scaled, b + 1)
                nc.gpsimd.tensor_tensor(num_sb[:], num_sb[:], inv_sb[:], ALU.mult).then_inc(attn_masked, 1)

            def token_rstd(b):
                pool.wait_ge(y_moments, b + 1)
                nc.gpsimd.tensor_tensor(rstd[:], mean_var[:, :, 1], minus_half[:], ALU.pow).then_inc(y_rstd, 1)

            for i in range(4):
                split(0, i)

            def batch(b, first, last):
                if not last:
                    split(b + 1, 0)
                    split(b + 1, 1)
                if not first:
                    finish_heads(b - 1)
                if not last:
                    split(b + 1, 2)
                    split(b + 1, 3)
                if not first:
                    token_rstd(b - 1)

            batch(0, True, False)
            with pool.Fori(1, B - 1) as b:
                batch(b, False, False)
            batch(B - 1, False, True)
            finish_heads(B - 1)
            token_rstd(B - 1)

        @block.scalar
        def _(act):
            def exps(b, q, c, first):
                n = STEPS * b + NC * q + c
                if not (first and NC * q + c < 2):
                    act.wait_ge(pv_made, n - 1)
                for h in range(HQ):
                    act.wait_ge(b_made, 4 * n + h + 1)
                    nc.scalar.activation(probs[:, c % 2, h], ps_b[h % 2][:], ACT.Exp, scale=DH ** -0.5).then_inc(
                        exp_done, 1)

            def keep_o(b, q, first):
                act.wait_ge(pv_made, STEPS * b + NC * q + NC)
                if not (first and q < 2):
                    act.wait_ge(o_stored[q % 2], 32 * b + 16 * (q // 2))
                nc.scalar.activation(o_sb[:, q % 2], ps_pv[:], ACT.Copy).then_inc(o_kept, 1)

            def batch(b, first):
                for q in range(NQ):
                    for c in range(NC):
                        exps(b, q, c, first)
                        if c == 0 and q > 0:
                            keep_o(b, q - 1, first)
                        elif c == 0 and not first:
                            keep_o(b - 1, 3, False)

            batch(0, True)
            with act.Fori(1, B) as b:
                batch(b, False)
            keep_o(B - 1, 3, False)

        @block.vector
        def _(dve):
            held = spare_registers(dve, "held2", 1)

            def row_split(src, j, k):
                nc.vector.tensor_copy(row_parts[:, j], src[:]).then_inc(mask_step, 1)
                dve.wait_ge(mask_step, k + 1)
                nc.vector.tensor_tensor(rest_rows[:], src[:], row_parts[:, j], ALU.subtract).then_inc(mask_step, 1)
                dve.wait_ge(mask_step, k + 2)
                nc.vector.tensor_copy(row_parts[:, j + 1], rest_rows[:]).then_inc(mask_step, 1)
                dve.wait_ge(mask_step, k + 3)
                nc.vector.tensor_tensor(row_parts[:, j + 2], rest_rows[:], row_parts[:, j + 1],
                                        ALU.subtract).then_inc(rows_made, 1)

            dve.wait_ge(consts_loaded, 96)
            nc.vector.memset(row_parts[:, 6], 1.0).then_inc(rows_made, 1)
            nc.vector.tensor_scalar(pen_rows[:], m_rows[:], -1.0, PENALTY, ALU.add, ALU.mult).then_inc(mask_step, 1)
            dve.wait_ge(mask_step, 1)
            row_split(pen_rows, 0, 1)
            dve.wait_ge(rows_made, 2)
            row_split(m_rows, 3, 4)
            dve.wait_ge(rows_made, 3)
            nc.vector.memset(rest_rows[:], 0.0).then_inc(rows_made, 3)
            dve.wait_ge(consts_set, 2)

            def reduces(k, par, c, halves=(0, 1)):
                for i in halves:
                    dve.wait_ge(a_made[i], k + 1)
                    nc.vector.tensor_reduce(row_max[:, par, 2 * i:2 * i + 2, c], ps_a[i][:], AX.X,
                                            ALU.max).then_inc(a_kept[i], 1)

            def keep_max(m):
                dve.wait_ge(misc_made, m + 1)
                nc.vector.tensor_scalar(neg_max[:], ps_misc[0:HQ * NC, 0:P], -1.0, None, ALU.mult).then_inc(misc_kept, 1)

            def cut_max(k, m, first=False):
                dve.wait_ge(misc_kept, m + 1)
                if not first:
                    dve.wait_ge(max_stored, 16 * k)
                nc.vector.tensor_copy(neg_parts[:, 0], neg_max[:]).then_inc(max_step, 1)
                dve.wait_ge(max_step, 3 * k + 1)
                nc.vector.tensor_tensor(neg_rest[:], neg_max[:], neg_parts[:, 0], ALU.subtract).then_inc(max_step, 1)
                dve.wait_ge(max_step, 3 * k + 2)
                nc.vector.tensor_copy(neg_parts[:, 1], neg_rest[:]).then_inc(max_step, 1)
                dve.wait_ge(max_step, 3 * k + 3)
                nc.vector.tensor_tensor(neg_parts[:, 2], neg_rest[:], neg_parts[:, 1],
                                        ALU.subtract).then_inc(max_ready, 1)

            def keep_qk(b, i, m, first=False):
                k, s = 4 * b + i, i % 2
                dve.wait_ge(misc_made, m + 1)
                dve.wait_ge(in_loaded, 32 * b + 32)
                if not (first and i < 2):
                    dve.wait_ge(part3, k - 1)
                    dve.wait_ge(parts_stored[s], 96 * b + 48 * (i // 2))
                nc.vector.scalar_tensor_tensor(full[:, s], ps_misc[:], bias_qk[:, s, i // 2:i // 2 + 1], mask_in[:],
                                               ALU.add, ALU.mult).then_inc(misc_kept, 1)

            def first_part(i, m):
                s = i % 2
                dve.wait_ge(misc_kept, m + 1)
                nc.vector.tensor_copy(parts[:, s, 0], full[:, s]).then_inc(part1, 1)

            def cut(b, i):
                dve.wait_ge(rest1, 4 * b + i + 1)
                nc.vector.tensor_copy(parts[:, i % 2, 1], rest[:, i % 2]).then_inc(part2, 1)

            def stage_v(b, i, m, first=False):
                dve.wait_ge(misc_made, m + 1)
                if not first:
                    dve.wait_ge(v_filled, 4 * b)
                nc.vector.tensor_tensor(v_stage[:, 2 * i:2 * i + 2], ps_misc[:].rearrange("p (s c) -> p s c", s=2),
                                        bias_v[:].unsqueeze(1).to_broadcast([P, 2, C]), ALU.add)\
                    .then_inc(misc_kept, 1)
                dve.wait_ge(misc_kept, m + 1)
                nc.vector.tensor_copy(mask_now[:, 2 * i:2 * i + 2],
                                      mask_col[:, bass.ds(b, 1), 2 * i:2 * i + 2].squeeze(1)).then_inc(v_staged, 1)

            def fill_v(b, first=False):
                dve.wait_ge(v_staged, 2 * b + 2)
                if not first:
                    dve.wait_ge(pv_made, STEPS * b)
                for c in range(NC):
                    nc.vector.tensor_scalar(v_aug[:, c, :, 0:DH], v_stage[:, c].rearrange("p (h d) -> p h d", h=H),
                                            mask_now[:, c:c + 1], None, ALU.mult).then_inc(v_filled, 1)

            def invert(b):
                dve.wait_ge(den_loaded, 16 * (b + 1))
                nc.vector.reciprocal(inv[:], den[:]).then_inc(inv_made, 1)

            def moments(b):
                dve.wait_ge(attn_masked, b + 1)
                nc.vector.tensor_tensor(num_sb[:], num_sb[:], x[:, bass.ds(2 * b, 2), :], ALU.add).then_inc(y_added, 1)
                dve.wait_ge(y_added, b + 1)
                for i in range(2):
                    nc.vector.bn_stats(stats[:, i], num_sb[:, i]).then_inc(y_stats, 1)
                wait_apart(dve, held, (consts_set, 2), (y_stats, 4 * b + 2))
                for i in range(2):
                    nc.vector.bn_aggr(mean_var[:, i], stats[:, i]).then_inc(y_stats, 1)
                dve.wait_ge(y_stats, 4 * b + 4)
                nc.vector.tensor_scalar(mean_var[:, :, 1], mean_var[:, :, 1], LN_EPS, None, ALU.add).then_inc(
                    y_moments, 1)

            def normalize(b):
                dve.wait_ge(y_rstd, b + 1)
                for i in range(2):
                    nc.vector.tensor_scalar(x[:, bass.ds(2 * b + i, 1), :].squeeze(1), num_sb[:, i],
                                            mean_var[:, i, 0:1], rstd[:, i:i + 1], ALU.subtract, ALU.mult)\
                        .then_inc(x2_made, 1)

            for i in range(4):
                keep_qk(0, i, i, True)
                first_part(i, i)
                cut(0, i)
            stage_v(0, 0, 4, True)
            stage_v(0, 1, 5, True)
            for c in range(NC):
                reduces(c, 0, c)
            keep_max(6)
            cut_max(0, 6, True)
            for c in range(NC):
                reduces(NC + c, 1, c)

            def batch(b, first, last):
                m = MISC0 + MISC * b
                for q in range(NQ):
                    for c in range(NC):
                        s = NC * q + c
                        before = q if last else (0, 3, 6, 9)[q]
                        qk = {2: (0, 1), 3: (1, 2), 6: (2, 4), 7: (3, 5)}
                        turned = s in (1, 5, 9) or (s == 13 and not last)
                        if turned:
                            keep_max(m + before)
                        elif not last and s in qk:
                            keep_qk(b + 1, qk[s][0], m + qk[s][1])
                        elif not last and s in (10, 11):
                            stage_v(b + 1, s - 10, m + s - 3)
                        if not (last and q >= 2):
                            reduces(2 * NC + STEPS * b + s, q % 2, c)
                        if s == 0:
                            fill_v(b, first)
                        if turned:
                            cut_max(4 * b + q + 1, m + before)
                        if not last:
                            if s in qk:
                                first_part(qk[s][0], m + qk[s][1])
                            if s in (3, 4, 7, 8):
                                cut(b + 1, (3, 4, 7, 8).index(s))
                        if not first:
                            if s == 3:
                                invert(b - 1)
                            elif s == 12:
                                moments(b - 1)
                            elif s == 14:
                                normalize(b - 1)

            batch(0, True, False)
            with dve.Fori(1, B - 1) as b:
                batch(b, False, False)
            batch(B - 1, False, True)
            invert(B - 1)
            moments(B - 1)
            normalize(B - 1)

        @block.tensor
        def _(pe):
            def scores_max(k, b, q, c, i, first=False):
                if c == 0 and i == 0:
                    pe.wait_ge(stack_loaded[q], 16 * STACK_DMAS * (b + 1))
                if not first:
                    pe.wait_ge(a_kept[i], k)
                for j in range(2):
                    h = HQ * q + 2 * i + j
                    mm = nc.tensor.matmul(ps_a[i][:, j], q_stack[0:ROWS_A, h, c * P:(c + 1) * P],
                                          k_stack[0:ROWS_A, h, :], start=True, stop=True)
                mm.then_inc(a_made[i], 1)

            def scores(b, q, c, h, first):
                e = 64 * b + 16 * q + 4 * c + h
                if c == 0 and h == 0:
                    pe.wait_ge(max_loaded[q], 16 * (b + 1))
                if not (first and 16 * q + 4 * c + h < 2):
                    pe.wait_ge(exp_done, e - 1)
                hh = HQ * q + h
                nc.tensor.matmul(ps_b[h % 2][:], k_stack[0:ROWS_B, hh, c * P:(c + 1) * P],
                                 q_stack[0:ROWS_B, hh, :], start=True, stop=True).then_inc(b_made, 1)

            def values(b, q, c, first):
                n = STEPS * b + NC * q + c
                pe.wait_ge(exp_done, 4 * n + 4)
                if c == 0:
                    if q == 0:
                        pe.wait_ge(v_filled, 4 * b + 4)
                    if not (first and q == 0):
                        pe.wait_ge(o_kept, 4 * b + q)
                for g in range(HQ):
                    mm = nc.tensor.matmul(ps_pv[32 * g:32 * g + 32, :], v_aug[:, c, HQ * q + g, :],
                                          probs[:, c % 2, g], start=(c == 0), stop=(c == NC - 1))
                mm.then_inc(pv_made, 1)

            def free_misc(m, first):
                if not first:
                    pe.wait_ge(misc_kept, m)

            def project_qk(b, i, m, first=False):
                s, o = i % 2, i // 2
                if i < 2:
                    pe.wait_ge(in_loaded, 32 * b + 32)
                free_misc(m, first)
                for c in range(2):
                    rhs = ctx_sb[:, c] if s else x[:, bass.ds(2 * b + c, 1), :].squeeze(1)
                    mm = nc.tensor.matmul(ps_misc[:], w2[:, s, c, o * P:(o + 1) * P], rhs,
                                          start=(c == 0), stop=(c == 1))
                mm.then_inc(misc_made, 1)

            def project_v(b, i, m):
                free_misc(m, False)
                for j in range(2):
                    sc = 2 * i + j
                    for c in range(2):
                        mm = nc.tensor.matmul(ps_misc[:, j * C:(j + 1) * C], ctx_sb[:, c, sc * P:(sc + 1) * P],
                                              w2[:, 2, c, :], start=(c == 0), stop=(c == 1))
                mm.then_inc(misc_made, 1)

            def transpose_max(m, par, k):
                free_misc(m, False)
                for i in range(2):
                    pe.wait_ge(a_kept[i], k)
                nc.tensor.transpose(ps_misc[0:HQ * NC, 0:P], row_max[:, par].rearrange("p h c -> p (h c)"),
                                    ident[:]).then_inc(misc_made, 1)

            pe.wait_ge(consts_loaded, 96)
            for i in range(4):
                project_qk(0, i, i, i == 0)
            project_v(0, 0, 4)
            project_v(0, 1, 5)
            for c in range(NC):
                for i in range(2):
                    scores_max(c, 0, 0, c, i, c == 0)
            transpose_max(6, 0, NC)
            for c in range(NC):
                for i in range(2):
                    scores_max(NC + c, 0, 1, c, i)

            def batch(b, first, last):
                m = MISC0 + MISC * b
                for q in range(NQ):
                    for c in range(NC):
                        s = NC * q + c
                        k = 2 * NC + STEPS * b + s
                        ahead = not (last and q >= 2)
                        b2, q2 = (b, q + 2) if q < 2 else (b + 1, q - 2)
                        if ahead:
                            scores_max(k, b2, q2, c, 0)
                        scores(b, q, c, 0, first)
                        scores(b, q, c, 1, first)
                        if ahead:
                            scores_max(k, b2, q2, c, 1)
                        if s > 0:
                            values(b, (s - 1) // NC, (s - 1) % NC, first)
                        elif not first:
                            values(b - 1, NQ - 1, NC - 1, False)
                        scores(b, q, c, 2, first)
                        scores(b, q, c, 3, first)
                        if c == 0 and not (last and q == 3):
                            before = q if last else (0, 3, 6, 9)[q]
                            transpose_max(m + before, (q + 1) % 2, k)
                        if not last:
                            if s in (1, 2, 5, 6):
                                i = (1, 2, 5, 6).index(s)
                                project_qk(b + 1, i, m + (1, 2, 4, 5)[i])
                            elif s in (9, 10):
                                project_v(b + 1, s - 9, m + s - 2)

            batch(0, True, False)
            with pe.Fori(1, B - 1) as b:
                batch(b, False, False)
            batch(B - 1, False, True)
            values(B - 1, NQ - 1, NC - 1, False)
E_, K_TOP = 16, 4
TILES = (TOK * K_TOP + E_ * (P - 1)) // P
DUMMY = TOK


def route(nc, A, S, x, G, W):
    NP = NT * K_TOP
    with ExitStack() as ctx:
        def sb(name, shape, dt=F32):
            return ctx.enter_context(nc.sbuf_tensor(name, shape, dt))

        def sem(name):
            return ctx.enter_context(nc.semaphore(name))

        rw = sb("rw", [P, KC, E_])
        rb = sb("rb", [P, E_])
        ident = sb("ident3", [P, P])
        before = sb("before", [P, P])
        ones = sb("ones3", [P, P])
        iota_p = sb("iota_p", [P, 1])
        iota_f = sb("iota_f", [P, P])
        xT = sb("xT3", [P, 2, KC, P])
        logits = sb("logits", [P, NT, E_])
        top = sb("top", [P, NT, 8])
        top_i = sb("top_i", [P, NT, 8], U32)
        top_f = sb("top_f", [P, NP])
        gap = sb("gap", [P, NT, K_TOP])
        share = sb("share", [P, NT, K_TOP])
        total = sb("total", [P, NT])
        chosen = sb("chosen", [P, NP, E_])
        picked = sb("picked", [P, NP, E_])
        sel = sb("sel", [P, NT, E_])
        sofar = sb("sofar", [P, NT + 1, E_])
        over = sb("over", [P, E_, E_])
        n_tiles = sb("n_tiles", [P, E_])
        tile_end = sb("tile_end", [P, E_])
        base = sb("base", [P, E_])
        place = sb("place", [P, NT, E_])
        slot = sb("slot", [P, NP])
        slot_i = sb("slot_i", [P, NP], I32)
        hi_i = sb("hi_i", [P, NP], I32)
        lo_i = sb("lo_i", [P, NP], I32)
        hi_f = sb("hi_f", [P, NP])
        lo_f = sb("lo_f", [P, NP])
        token1 = sb("token1", [P, NT])
        in_tile = sb("in_tile", [P, 2, K_TOP, P])
        of_tile = sb("of_tile", [P, 2, K_TOP, TILES])
        payload = sb("payload", [P, 2, K_TOP, 2, TILES])
        empty = sb("empty", [P, TILES])
        tok_f = sb("tok_f", [P, TILES])
        past = sb("past", [1, TILES, E_])
        expert_f = sb("expert_f", [1, TILES])
        new_f = sb("new_f", [1, TILES])
        zero = sb("zero3", [P, P])

        ps_t = [ctx.enter_context(nc.psum_tensor(f"ps_t{i}", [P, D], F32)) for i in range(2)]
        ps_l = ctx.enter_context(nc.psum_tensor("ps_l", [P, D], F32))
        ps_r = ctx.enter_context(nc.psum_tensor("ps_r", [P, D], F32))
        ps_s = ctx.enter_context(nc.psum_tensor("ps_s", [P, D], F32))

        loaded, set_ = sem("loaded3"), sem("set3")
        x_turned, x_kept, logit_made = sem("x_turned"), sem("x_kept"), sem("logit_made")
        step = sem("route_step")
        gap_made, exp_made = sem("gap_made"), sem("exp_made")
        sel_made, rank_made = sem("sel_made"), sem("rank_made")
        onehot_made, spread_done = sem("onehot_made"), sem("spread_done")
        dummy_stored, acc_stored = sem("dummy_stored"), sem("acc_stored")

        block = ctx.enter_context(nc.Block())

        @block.sync
        def _(sp):
            sp.dma_start(rw[:], A["router_w"]).then_inc(loaded, 16)
            sp.dma_start(rb[:], A["router_b"].to_broadcast([P, E_])).then_inc(loaded, 16)
            sp.dma_start(ident[:], A["ident"]).then_inc(loaded, 16)
            sp.dma_start(before[:], A["before"]).then_inc(loaded, 16)
            sp.dma_start(iota_p[:], A["iota_p"]).then_inc(loaded, 16)
            sp.dma_start(iota_f[:], A["iota_f"]).then_inc(loaded, 16)
            load_weights(sp, A, W, 0)
            load_biases(sp, A, W, 0, 0)
            load_biases(sp, A, W, 1, 1)
            sp.dma_start(W["ident"][:], A["ident"]).then_inc(W["small_loaded"][1], 16)
            sp.dma_start(S["acc"][0:TOK, :].rearrange("(t p) d -> p t d", p=P), x[:]).then_inc(acc_stored, 16)
            sp.wait_ge(set_, 3)
            zeros = zero[:].unsqueeze(1).to_broadcast([P, KC, P])
            sp.dma_start(S["x2"][TOK:TOK + P, :].rearrange("p (c d) -> p c d", c=KC), zeros).then_inc(dummy_stored, 16)
            sp.dma_start(S["acc"][TOK:TOK + P, :].rearrange("p (c d) -> p c d", c=KC), zeros).then_inc(dummy_stored, 16)
            sp.wait_ge(W["hi"], 3)
            sp.wait_ge(W["lo"], 3)
            load_weights(sp, A, W, 1)
            sp.wait_ge(dummy_stored, 32)
            sp.wait_ge(acc_stored, 16)

        @block.gpsimd
        def _(pool):
            nc.gpsimd.memset(ones[:], 1.0).then_inc(set_, 1)
            nc.gpsimd.memset(zero[:], 0.0).then_inc(set_, 1)
            nc.gpsimd.memset(sofar[:, 0], 0.0).then_inc(set_, 1)
            for k in range(3):
                split_lo(nc, pool, W, 0, 0, k)

        @block.scalar
        def _(act):
            for t in range(NT):
                act.wait_ge(x_turned, t + 1)
                if t >= 2:
                    act.wait_ge(logit_made, t - 1)
                nc.scalar.activation(xT[:, t % 2], ps_t[t % 2][:].rearrange("p (c t) -> p c t", c=KC),
                                     ACT.Copy).then_inc(x_kept, 1)
            for k in range(3):
                split_hi(nc, act, W, 0, 0, k)
            act.wait_ge(gap_made, 1)
            nc.scalar.activation(share[:], gap[:], ACT.Exp).then_inc(exp_made, 1)

        @block.vector
        def _(dve):
            done = [0]

            def chain(instruction):
                done[0] += 1
                instruction.then_inc(step, 1)
                dve.wait_ge(step, done[0])

            dve.wait_ge(loaded, 96)
            dve.wait_ge(set_, 3)
            for t in range(NT):
                dve.wait_ge(logit_made, t + 1)
            chain(nc.vector.tensor_tensor(logits[:], ps_l[:, 0:NT * E_].rearrange("p (t e) -> p t e", t=NT),
                                          rb[:].unsqueeze(1).to_broadcast([P, NT, E_]), ALU.add))
            for t in range(NT):
                last = nc.vector.max(top[:, t], logits[:, t])
            chain(last)
            for t in range(NT):
                last = nc.vector.max_index(top_i[:, t], top[:, t], logits[:, t])
            nc.vector.tensor_tensor(gap[:], top[:, :, 0:K_TOP], top[:, :, 0:1].to_broadcast([P, NT, K_TOP]),
                                    ALU.subtract).then_inc(gap_made, 1)
            chain(last)
            chain(nc.vector.tensor_copy(top_f[:].rearrange("p (t k) -> p t k", t=NT), top_i[:, :, 0:K_TOP]))
            chain(nc.vector.tensor_tensor(chosen[:], iota_f[:, 0:E_].unsqueeze(1).to_broadcast([P, NP, E_]),
                                          top_f[:].unsqueeze(2).to_broadcast([P, NP, E_]), ALU.is_equal))
            chain(nc.vector.tensor_reduce(sel[:], chosen[:].rearrange("p (t k) e -> p t e k", k=K_TOP), AX.X, ALU.add))
            for t in range(NT):
                chain(nc.vector.tensor_tensor(sofar[:, t + 1], sofar[:, t], sel[:, t], ALU.add))
            nc.vector.tensor_scalar(token1[:], iota_f[:, 0:NT], float(P), iota_p[:, 0:1], ALU.mult,
                                    ALU.add).then_inc(sel_made, 1)
            dve.wait_ge(exp_made, 1)
            chain(nc.vector.tensor_reduce(total[:], share[:], AX.X, ALU.add))
            chain(nc.vector.reciprocal(total[:], total[:]))
            chain(nc.vector.tensor_tensor(share[:], share[:], total[:].unsqueeze(2).to_broadcast([P, NT, K_TOP]),
                                          ALU.mult))
            dve.wait_ge(rank_made, 1)
            chain(nc.vector.tensor_copy(base[:], ps_r[:, NT * E_:(NT + 1) * E_]))
            chain(nc.vector.scalar_tensor_tensor(over[:], iota_f[:, 0:E_].unsqueeze(1).to_broadcast([P, E_, E_]),
                                                 float(P), base[:].unsqueeze(2).to_broadcast([P, E_, E_]),
                                                 ALU.mult, ALU.is_lt))
            chain(nc.vector.tensor_reduce(n_tiles[:], over[:], AX.X, ALU.add))
            chain(nc.vector.tensor_scalar(n_tiles[:], n_tiles[:], 1.0, None, ALU.max))
            chain(nc.vector.tensor_tensor_scan(tile_end[:], ones[:, 0:E_], n_tiles[:], 0.0, ALU.mult, ALU.add))
            chain(nc.vector.tensor_tensor(base[:], tile_end[:], n_tiles[:], ALU.subtract))
            chain(nc.vector.tensor_scalar(base[:], base[:], float(P), None, ALU.mult))
            chain(nc.vector.tensor_tensor(place[:], ps_r[:, 0:NT * E_].rearrange("p (t e) -> p t e", t=NT),
                                          base[:].unsqueeze(1).to_broadcast([P, NT, E_]), ALU.add))
            for t in range(NT):
                last = nc.vector.tensor_tensor(picked[:, K_TOP * t:K_TOP * t + K_TOP],
                                               chosen[:, K_TOP * t:K_TOP * t + K_TOP],
                                               place[:, t].unsqueeze(1).to_broadcast([P, K_TOP, E_]), ALU.mult)
            chain(last)
            chain(nc.vector.tensor_reduce(slot[:], picked[:], AX.X, ALU.add))
            chain(nc.vector.tensor_copy(slot_i[:], slot[:]))
            nc.vector.tensor_scalar(hi_i[:], slot_i[:], 7, None, ALU.logical_shift_right)
            chain(nc.vector.tensor_scalar(lo_i[:], slot_i[:], P - 1, None, ALU.bitwise_and))
            nc.vector.tensor_copy(hi_f[:], hi_i[:])
            chain(nc.vector.tensor_copy(lo_f[:], lo_i[:]))
            chain(nc.vector.tensor_scalar(token1[:], token1[:], 1.0, None, ALU.add))
            for t in range(NT):
                s, kk = t % 2, slice(K_TOP * t, K_TOP * t + K_TOP)
                if t >= 2:
                    dve.wait_ge(spread_done, t - 1)
                nc.vector.tensor_tensor(in_tile[:, s], iota_f[:].unsqueeze(1).to_broadcast([P, K_TOP, P]),
                                        lo_f[:, kk].unsqueeze(2).to_broadcast([P, K_TOP, P]), ALU.is_equal)
                chain(nc.vector.tensor_tensor(of_tile[:, s], iota_f[:, 0:TILES].unsqueeze(1).to_broadcast(
                    [P, K_TOP, TILES]), hi_f[:, kk].unsqueeze(2).to_broadcast([P, K_TOP, TILES]), ALU.is_equal))
                nc.vector.tensor_scalar(payload[:, s, :, 0], of_tile[:, s], token1[:, t:t + 1], None, ALU.mult)
                nc.vector.tensor_tensor(payload[:, s, :, 1], of_tile[:, s], share[:, t].unsqueeze(2).to_broadcast(
                    [P, K_TOP, TILES]), ALU.mult).then_inc(onehot_made, 1)
            chain(nc.vector.tensor_tensor(past[:], tile_end[0:1].unsqueeze(1).to_broadcast([1, TILES, E_]),
                                          iota_f[0:1, 0:TILES].unsqueeze(2).to_broadcast([1, TILES, E_]), ALU.is_le))
            chain(nc.vector.tensor_reduce(expert_f[:], past[:], AX.X, ALU.add))
            chain(nc.vector.tensor_scalar(expert_f[:], expert_f[:], float(E_ - 1), None, ALU.min))
            chain(nc.vector.tensor_copy(G["expert"][:], expert_f[:]))
            chain(nc.vector.tensor_scalar(G["parity"][:], G["expert"][:], 1, None, ALU.bitwise_and))
            chain(nc.vector.memset(new_f[:], 1.0))
            chain(nc.vector.tensor_tensor(new_f[:, 1:], expert_f[:, 1:], expert_f[:, :-1], ALU.not_equal))
            chain(nc.vector.scalar_tensor_tensor(new_f[:], expert_f[:], float(E_ - 1), new_f[:], ALU.is_lt, ALU.mult))
            chain(nc.vector.tensor_copy(G["new"][:], new_f[:]))
            chain(nc.vector.tensor_scalar(G["last_tile"][:], tile_end[0:1], -1.0, None, ALU.add))
            dve.wait_ge(spread_done, NT)
            chain(nc.vector.tensor_scalar(empty[:], ps_s[:, 0:TILES], 0.0, None, ALU.is_equal))
            chain(nc.vector.tensor_scalar(iota_p[:], iota_p[:], float(DUMMY + 1), None, ALU.add))
            chain(nc.vector.tensor_scalar(empty[:], empty[:], iota_p[:, 0:1], -1.0, ALU.mult, ALU.add))
            chain(nc.vector.tensor_tensor(tok_f[:], ps_s[:, 0:TILES], empty[:], ALU.add))
            chain(nc.vector.tensor_copy(G["token"][:], tok_f[:]))
            chain(nc.vector.tensor_copy(G["weight"][:], ps_s[:, TILES:2 * TILES]))

        @block.tensor
        def _(pe):
            pe.wait_ge(loaded, 96)

            def turn(t):
                if t >= 2:
                    pe.wait_ge(x_kept, t - 1)
                for c in range(KC):
                    mm = nc.tensor.transpose(ps_t[t % 2][:, c * P:(c + 1) * P], x[:, t, c * P:(c + 1) * P], ident[:])
                mm.then_inc(x_turned, 1)

            turn(0)
            for t in range(NT):
                if t + 1 < NT:
                    turn(t + 1)
                pe.wait_ge(x_kept, t + 1)
                for c in range(KC):
                    mm = nc.tensor.matmul(ps_l[:, t * E_:(t + 1) * E_], xT[:, t % 2, c], rw[:, c, :],
                                          start=(c == 0), stop=(c == KC - 1))
                mm.then_inc(logit_made, 1)
            pe.wait_ge(sel_made, 1)
            nc.tensor.matmul(ps_r[:, 0:NT * E_], before[:], sel[:].rearrange("p t e -> p (t e)"),
                             start=True, stop=False, skip_group_check=True)
            nc.tensor.matmul(ps_r[:, 0:NT * E_], ones[:], sofar[:, 0:NT].rearrange("p t e -> p (t e)"),
                             start=False, stop=True, skip_group_check=True)
            nc.tensor.matmul(ps_r[:, NT * E_:(NT + 1) * E_], ones[:], sofar[:, NT], start=False, stop=True,
                             skip_group_check=True).then_inc(rank_made, 1)
            for t in range(NT):
                pe.wait_ge(onehot_made, t + 1)
                for k in range(K_TOP):
                    mm = nc.tensor.matmul(ps_s[:, 0:2 * TILES], in_tile[:, t % 2, k],
                                          payload[:, t % 2, k].rearrange("p a t -> p (a t)"),
                                          start=(t == 0 and k == 0), stop=(t == NT - 1 and k == K_TOP - 1))
                mm.then_inc(spread_done, 1)


def weight_buffers(nc, ctx):
    def sb(name, shape, dt=F32):
        return ctx.enter_context(nc.sbuf_tensor(name, shape, dt))

    def sem(name):
        return ctx.enter_context(nc.semaphore(name))

    return {
        "raw": sb("we_raw", [P, 3, KC, D]),
        "split": sb("we_split", [P, 2, 3, 2, KC, D], F32R),
        "bias": sb("we_bias", [P, 2, 3 * D]),
        "ident": sb("ident4", [P, P]),
        "loaded": sem("we_loaded"), "hi": sem("we_hi"), "lo": sem("we_lo"),
        "small_loaded": [sem("be_loaded0"), sem("be_loaded1")],
    }


def load_weights(sp, A, W, e):
    sp.dma_start(W["raw"][:], A["w_expert"][e] if isinstance(e, int) else
                 A["w_expert"][bass.ds(e, 1)].squeeze(0)).then_inc(W["loaded"], 16)


def load_biases(sp, A, W, e, s):
    sp.dma_start(W["bias"][:, s], (A["b_expert"][e:e + 1] if isinstance(e, int) else
                                   A["b_expert"][bass.ds(e, 1)]).to_broadcast([P, 3 * D])).then_inc(
        W["small_loaded"][s], 16)


def split_hi(nc, act, W, e, slot, k):
    dst = W["split"][:, bass.ds(slot, 1), k, 0].squeeze(1)
    act.wait_ge(W["loaded"], 16 * e + 16)
    nc.scalar.activation(dst, W["raw"][:, k], ACT.Copy).then_inc(W["hi"], 1)


def split_lo(nc, pool, W, e, slot, k, wait=None):
    hi, lo = (W["split"][:, bass.ds(slot, 1), k, part].squeeze(1) for part in range(2))
    (wait or pool.wait_ge)(W["hi"], 3 * e + k + 1)
    nc.gpsimd.tensor_tensor(lo, W["raw"][:, k], hi, ALU.subtract).then_inc(W["lo"], 1)


def experts(nc, A, S, G, W):
    U = 4
    LIMIT, ALPHA = 7.0, 1.702
    GATE, UP, DOWN = range(3)
    with ExitStack() as ctx:
        def sb(name, shape, dt=F32):
            return ctx.enter_context(nc.sbuf_tensor(name, shape, dt))

        def sem(name):
            return ctx.enter_context(nc.semaphore(name))

        ident, w, bias = W["ident"], W["split"], W["bias"]
        zero_row = sb("zero_row", [P, 1])
        from_rows = [sb(f"from_rows{i}", [P, 1], U32) for i in range(U)]
        to_rows = sb("to_rows", [P, 1], U32)
        x_rows = [sb(f"x_rows{i}", [P, D]) for i in range(U)]
        xT = sb("xT4", [P, 2, 2, KC, P], F32R)
        gate = sb("gate", [P, D])
        up = sb("up", [P, D])
        sig = sb("sig", [P, D])
        h = sb("h", [P, D])
        hT = sb("hT", [P, 2, KC, P], F32R)
        y = [sb(f"y{i}", [P, D]) for i in range(U)]

        def bank(name):
            return ctx.enter_context(nc.psum_tensor(name, [P, D], F32))

        ps_g, ps_u, ps_x, ps_h, ps_y = bank("ps_g"), bank("ps_u2"), bank("ps_x"), bank("ps_h"), bank("ps_y")

        from_set, to_set = sem("from_set"), sem("to_set")
        tables_read = sem("tables_read")
        gathered = [sem(f"gathered{i}") for i in range(U)]
        x_turned, xT_hi, xT_lo = sem("xe_turned"), sem("xeT_hi"), sem("xeT_lo")
        g_made, u_made, g_kept, u_kept = sem("g_made"), sem("ue_made"), sem("g_kept"), sem("ue_kept")
        g_cut, u_cut, gated, sig_made, h_made = sem("g_cut"), sem("u_cut"), sem("gated"), sem("sig_made"), sem("h_made")
        h_turned, hT_hi, hT_lo = sem("h_turned"), sem("hT_hi"), sem("hT_lo")
        y_made, y_biased, y_ready = sem("ye_made"), sem("y_biased"), sem("y_ready")
        added = sem("added")

        block = ctx.enter_context(nc.Block())

        def loop(engine, body):
            for j in range(U):
                body(j, j)
            with engine.Fori(1, TILES // U) as r:
                for j in range(U):
                    body(U * r + j, j)
            for i in range(TILES // U * U, TILES):
                body(i, i % U)

        def is_at(i, n):
            return isinstance(i, int) and i == n

        def below(i, n):
            return isinstance(i, int) and i < n

        def pick(table, i):
            return table[:, i:i + 1] if isinstance(i, int) else table[:, bass.ds(i, 1)]

        def four(psum):
            return psum[:].rearrange("p (c t) -> p c t", c=KC)

        @block.sync
        def _(sp):
            def follow(e, s):
                sp.wait_ge(W["hi"], 3 * e)
                sp.wait_ge(W["lo"], 3 * e)
                load_weights(sp, A, W, e)
                last = sp.value_load(G["last_tile"][:, bass.ds(e - 2, 1)], min_val=0, max_val=TILES - 1)
                sp.wait_ge(y_biased, last + 1)
                load_biases(sp, A, W, e, s)

            with sp.Fori(1, E_ // 2) as r:
                for s in range(2):
                    follow(2 * r + s, s)

        @block.gpsimd
        def _(pool):
            held = spare_registers(pool, "held4", 2)

            def gather(i, j):
                if not below(i, U):
                    pool.wait_ge(x_turned, i - U + 1)
                nc.gpsimd.tensor_copy(from_rows[j][:], pick(G["token"], i)).then_inc(from_set, 1)
                wait_apart(pool, held, (tables_read, 1), (from_set, i + 1))
                pool.indirect_dma_start(x_rows[j][:], None, S["x2"], bass.IndirectOffsetOnAxis(from_rows[j][:], 0))\
                    .then_inc(gathered[j], 16)

            def scatter(i, j):
                if not is_at(i, 0):
                    pool.wait_ge(added, 16 * i)
                nc.gpsimd.tensor_copy(to_rows[:], pick(G["token"], i)).then_inc(to_set, 1)
                wait_apart(pool, held, (tables_read, 1), (to_set, i + 1), (y_ready, i + 1))
                pool.indirect_dma_start(S["acc"], bass.IndirectOffsetOnAxis(to_rows[:], 0), y[j][:], None,
                                        compute_op=ALU.add).then_inc(added, 16)

            nc.gpsimd.memset(zero_row[:], 0.0).then_inc(tables_read, 1)
            for j in range(3):
                gather(j, j)

            def body(i, j):
                if not (isinstance(i, int) and i >= TILES - 3):
                    gather(i + 3, (j + 3) % U)
                if not below(i, 2):
                    scatter(i - 2, (j - 2) % U)
                new = pool.value_load(pick(G["new"], i), min_val=0, max_val=1)
                with pool.If(new == 1):
                    e = pool.value_load(pick(G["expert"], i), min_val=0, max_val=E_ - 2)
                    par = pool.value_load(pick(G["parity"], i), min_val=0, max_val=1)
                    for k in range(3):
                        split_lo(nc, pool, W, e + 1, 1 - par, k,
                                 lambda semaphore, value: wait_apart(pool, held, (tables_read, 1), (semaphore, value)))

            loop(pool, body)
            scatter(TILES - 2, (TILES - 2) % U)
            scatter(TILES - 1, (TILES - 1) % U)
            pool.wait_ge(added, 16 * TILES)

        @block.scalar
        def _(act):
            def x_hi(i, j):
                act.wait_ge(x_turned, i + 1)
                if not below(i, 2):
                    act.wait_ge(u_made, i - 1)
                nc.scalar.activation(xT[:, j % 2, 0], four(ps_x), ACT.Copy).then_inc(xT_hi, 1)

            def h_hi(i):
                act.wait_ge(h_turned, i + 1)
                if not is_at(i, 0):
                    act.wait_ge(y_made, i)
                nc.scalar.activation(hT[:, 0], four(ps_h), ACT.Copy).then_inc(hT_hi, 1)

            def split_next(i, new, k):
                with act.If(new == 1):
                    e = act.value_load(pick(G["expert"], i), min_val=0, max_val=E_ - 2)
                    par = act.value_load(pick(G["parity"], i), min_val=0, max_val=1)
                    if not is_at(i, 0):
                        act.wait_ge(y_made if k == DOWN else u_made, i)
                    split_hi(nc, act, W, e + 1, 1 - par, k)

            x_hi(0, 0)

            def body(i, j):
                if not is_at(i, 0):
                    h_hi(i - 1)
                act.wait_ge(g_cut, i + 1)
                if not is_at(i, 0):
                    act.wait_ge(h_made, i)
                nc.scalar.activation(sig[:], gate[:], ACT.Sigmoid, scale=ALPHA).then_inc(sig_made, 1)
                new = act.value_load(pick(G["new"], i), min_val=0, max_val=1)
                split_next(i, new, GATE)
                if not is_at(i, TILES - 1):
                    x_hi(i + 1, j + 1)
                split_next(i, new, UP)
                split_next(i, new, DOWN)

            loop(act, body)
            h_hi(TILES - 1)

        @block.vector
        def _(dve):
            def x_lo(i, j):
                dve.wait_ge(xT_hi, i + 1)
                nc.vector.tensor_tensor(xT[:, j % 2, 1], four(ps_x), xT[:, j % 2, 0], ALU.subtract).then_inc(xT_lo, 1)

            def h_lo(i):
                dve.wait_ge(hT_hi, i + 1)
                nc.vector.tensor_tensor(hT[:, 1], four(ps_h), hT[:, 0], ALU.subtract).then_inc(hT_lo, 1)

            def biases(i):
                par = dve.value_load(pick(G["parity"], i), min_val=0, max_val=1)
                return lambda k: bias[:, bass.ds(par, 1), k * D:(k + 1) * D].squeeze(1)

            def finish(i, j):
                b = biases(i)
                dve.wait_ge(y_made, i + 1)
                if not below(i, U - 1):
                    dve.wait_ge(added, 16 * (i - U + 2))
                nc.vector.tensor_tensor(y[j][:], ps_y[:], b(DOWN), ALU.add).then_inc(y_biased, 1)
                dve.wait_ge(y_biased, i + 1)
                nc.vector.tensor_scalar(y[j][:], y[j][:], pick(G["weight"], i), None, ALU.mult).then_inc(y_ready, 1)

            x_lo(0, 0)

            def body(i, j):
                b = biases(i)
                dve.wait_ge(g_made, i + 1)
                if not is_at(i, 0):
                    dve.wait_ge(h_made, i)
                nc.vector.tensor_tensor(gate[:], ps_g[:], b(GATE), ALU.add).then_inc(g_kept, 1)
                dve.wait_ge(g_kept, i + 1)
                nc.vector.tensor_scalar(gate[:], gate[:], LIMIT, None, ALU.min).then_inc(g_cut, 1)
                if not is_at(i, 0):
                    h_lo(i - 1)
                dve.wait_ge(u_made, i + 1)
                nc.vector.tensor_tensor(up[:], ps_u[:], b(UP), ALU.add).then_inc(u_kept, 1)
                dve.wait_ge(u_kept, i + 1)
                nc.vector.tensor_scalar(up[:], up[:], LIMIT, -LIMIT, ALU.min, ALU.max).then_inc(u_cut, 1)
                if not is_at(i, TILES - 1):
                    x_lo(i + 1, j + 1)
                dve.wait_ge(u_cut, i + 1)
                dve.wait_ge(g_cut, i + 1)
                nc.vector.scalar_tensor_tensor(up[:], up[:], 1.0, gate[:], ALU.add, ALU.mult).then_inc(gated, 1)
                dve.wait_ge(gated, i + 1)
                dve.wait_ge(sig_made, i + 1)
                if not is_at(i, 0):
                    dve.wait_ge(h_turned, i)
                nc.vector.tensor_tensor(h[:], up[:], sig[:], ALU.mult).then_inc(h_made, 1)
                if not is_at(i, 0):
                    finish(i - 1, (j - 1) % U)

            loop(dve, body)
            h_lo(TILES - 1)
            finish(TILES - 1, (TILES - 1) % U)

        @block.tensor
        def _(pe):
            def transposes(out, rows):
                for c in range(KC):
                    mm = nc.tensor.transpose(out[:, c * P:(c + 1) * P], rows[:, c * P:(c + 1) * P], ident[:])
                return mm

            def turn_x(i, j):
                pe.wait_ge(gathered[j], 16 // U * (i - j) + 16)
                if not is_at(i, 0):
                    pe.wait_ge(xT_lo, i)
                transposes(ps_x, x_rows[j]).then_inc(x_turned, 1)

            def turn_h(i):
                pe.wait_ge(h_made, i + 1)
                if not is_at(i, 0):
                    pe.wait_ge(hT_lo, i)
                transposes(ps_h, h).then_inc(h_turned, 1)

            def products(out, left, par, k):
                passes = [(c, a, b) for c in range(KC) for a, b in SPLITS]
                for n, (c, a, b) in enumerate(passes):
                    mm = nc.tensor.matmul(out[:], left[:, a, c], w[:, bass.ds(par, 1), k, b, c].squeeze(1),
                                          start=(n == 0), stop=(n == len(passes) - 1))
                return mm

            def down(i):
                par = pe.value_load(pick(G["parity"], i), min_val=0, max_val=1)
                pe.wait_ge(hT_lo, i + 1)
                if not is_at(i, 0):
                    pe.wait_ge(y_biased, i)
                products(ps_y, hT, par, DOWN).then_inc(y_made, 1)

            pe.wait_ge(W["small_loaded"][0], 16)
            pe.wait_ge(W["small_loaded"][1], 32)
            turn_x(0, 0)

            def body(i, j):
                e = pe.value_load(pick(G["expert"], i), min_val=0, max_val=E_ - 1)
                par = pe.value_load(pick(G["parity"], i), min_val=0, max_val=1)
                pe.wait_ge(W["hi"], 3 * e + 3)
                pe.wait_ge(W["lo"], 3 * e + 3)
                pe.wait_ge(W["small_loaded"][0], e // 2 * 16 + 16)
                pe.wait_ge(W["small_loaded"][1], (e + 1) // 2 * 16 + 16)
                pe.wait_ge(xT_lo, i + 1)
                if not is_at(i, 0):
                    pe.wait_ge(g_kept, i)
                products(ps_g, xT[:, j % 2], par, GATE).then_inc(g_made, 1)
                if not is_at(i, 0):
                    turn_h(i - 1)
                    pe.wait_ge(u_kept, i)
                products(ps_u, xT[:, j % 2], par, UP).then_inc(u_made, 1)
                if not is_at(i, TILES - 1):
                    turn_x(i + 1, (j + 1) % U)
                if not is_at(i, 0):
                    down(i - 1)

            loop(pe, body)
            turn_h(TILES - 1)
            down(TILES - 1)


def last_norm(nc, S, out):
    with ExitStack() as ctx:
        def sb(name, shape, dt=F32):
            return ctx.enter_context(nc.sbuf_tensor(name, shape, dt))

        def sem(name):
            return ctx.enter_context(nc.semaphore(name))

        G4 = 4
        NG = NT // G4
        acc = sb("acc_sb", [P, NT, D])
        res = sb("res_sb", [P, NT, D])
        stats = sb("stats5", [P, NT, 6])
        mean_var = sb("mean_var5", [P, NT, 2])
        rstd = sb("rstd5", [P, NT])
        minus_half = sb("minus_half5", [P, NT])
        loaded = [sem(f"acc_loaded{i}") for i in range(NG)]
        stats_made, moments, var_eps, rstd_made, normed, stored, half_set = (
            sem("stats5_made"), sem("moments5"), sem("var_eps"), sem("rstd5_made"), sem("normed"), sem("stored"),
            sem("half5_set"))
        block = ctx.enter_context(nc.Block())

        @block.sync
        def _(sp):
            for g in range(NG):
                sp.dma_start(acc[:, G4 * g:G4 * g + G4], S["acc"][G4 * g * P:G4 * (g + 1) * P, :].rearrange(
                    "(t p) d -> p t d", p=P)).then_inc(loaded[g], 16)
            for g in range(NG):
                sp.wait_ge(normed, G4 * (g + 1))
                sp.dma_start(out[G4 * g * P:G4 * (g + 1) * P, :].rearrange("(t p) d -> p t d", p=P),
                             res[:, G4 * g:G4 * g + G4]).then_inc(stored, 16)
            sp.wait_ge(stored, 16 * NG)

        @block.gpsimd
        def _(pool):
            nc.gpsimd.memset(minus_half[:], -0.5).then_inc(half_set, 1)
            pool.wait_ge(half_set, 1)
            for g in range(NG):
                ts = slice(G4 * g, G4 * g + G4)
                pool.wait_ge(var_eps, g + 1)
                nc.gpsimd.tensor_tensor(rstd[:, ts], mean_var[:, ts, 1], minus_half[:, ts], ALU.pow).then_inc(
                    rstd_made, 1)

        @block.vector
        def _(dve):
            def moments_of(g):
                dve.wait_ge(loaded[g], 16)
                for t in range(G4 * g, G4 * g + G4):
                    nc.vector.bn_stats(stats[:, t], acc[:, t]).then_inc(stats_made, 1)
                dve.wait_ge(stats_made, G4 * (g + 1))
                for t in range(G4 * g, G4 * g + G4):
                    nc.vector.bn_aggr(mean_var[:, t], stats[:, t]).then_inc(moments, 1)
                dve.wait_ge(moments, G4 * (g + 1))
                ts = slice(G4 * g, G4 * g + G4)
                nc.vector.tensor_scalar(mean_var[:, ts, 1], mean_var[:, ts, 1], LN_EPS, None, ALU.add).then_inc(
                    var_eps, 1)

            def apply(g):
                dve.wait_ge(rstd_made, g + 1)
                for t in range(G4 * g, G4 * g + G4):
                    nc.vector.tensor_scalar(res[:, t], acc[:, t], mean_var[:, t, 0:1], rstd[:, t:t + 1],
                                            ALU.subtract, ALU.mult).then_inc(normed, 1)

            moments_of(0)
            for g in range(NG):
                if g + 1 < NG:
                    moments_of(g + 1)
                apply(g)


SCRATCH = {
    "parts": ([B, 2, 3, 16, 16, D], BF16),
    "rows_q": ([B, 9, D], BF16),
    "rows_k": ([B, 12, D], BF16),
    "max": ([B, 4, 3, 4 * D], BF16),
    "heads": ([B, 16, 2 * 16, D], F32),
    "inv": ([B, 16, D], F32),
    "x2": ([TOK + P, D], F32),
    "acc": ([TOK + P, D], F32),
}


def decoder_layer(nc, A, out):
    S = {name: nc.dram_tensor(f"scratch_{name}", shape, dt).ap() for name, (shape, dt) in SCRATCH.items()}
    with ExitStack() as ctx:
        def sb(name, shape, dt):
            return ctx.enter_context(nc.sbuf_tensor(name, shape, dt))

        G = {
            "token": sb("slot_token", [P, TILES], U32),
            "weight": sb("slot_weight", [P, TILES], F32),
            "expert": sb("tile_expert", [1, TILES], I32),
            "new": sb("tile_new", [1, TILES], I32),
            "parity": sb("tile_parity", [1, TILES], I32),
            "last_tile": sb("expert_last", [1, E_], I32),
        }
        with ExitStack() as keep:
            x = keep.enter_context(nc.sbuf_tensor("x_keep", [P, NT, D], F32))
            linear_attention(nc, A, x)
            cross_attention(nc, A, S, x)
            W = weight_buffers(nc, keep)
            route(nc, A, S, x, G, W)
            experts(nc, A, S, G, W)
        last_norm(nc, S, out)


def kernel(x, ctx_2048, mask_Bx1x2048_fk1, L0_attn_Wq, L0_attn_Wk, L0_attn_Wv, L0_attn_Wu, L0_attn_Wo,
           L0_xattn_Wq, L0_xattn_bq, L0_xattn_Wk, L0_xattn_bk, L0_xattn_Wv, L0_xattn_bv,
           L0_ffn_router_weight, L0_ffn_router_bias, L0_ffn_gate_up_proj, L0_ffn_gate_up_proj_bias,
           L0_ffn_down_proj, L0_ffn_down_proj_bias):
    import numpy as np
    import concourse.bacc as bacc
    from concourse.bass_utils import run_bass_kernel_spmd

    def rows_in(w):
        w = np.asarray(w)
        return w.reshape(-1, P, w.shape[-1]).transpose(1, 0, 2)

    tokens = np.asarray(x).reshape(TOK, D)
    mask = np.asarray(mask_Bx1x2048_fk1).reshape(B, D)
    gate_up, down = np.asarray(L0_ffn_gate_up_proj), np.asarray(L0_ffn_down_proj)
    gate_up_b = np.asarray(L0_ffn_gate_up_proj_bias)
    arrays = {
        "x": tokens,
        "xT": rows_in(tokens.T),
        "w1": np.stack([rows_in(w) for w in (L0_attn_Wq, L0_attn_Wk, L0_attn_Wv, L0_attn_Wu, L0_attn_Wo)]),
        "w2": np.stack([rows_in(np.asarray(w).T) for w in (L0_xattn_Wq, L0_xattn_Wk, L0_xattn_Wv)]),
        "bias_qk": np.stack([np.asarray(b).reshape(2, P).T for b in (L0_xattn_bq, L0_xattn_bk)], 1),
        "bias_v": np.asarray(L0_xattn_bv).reshape(1, 2 * P),
        "ctx": np.asarray(ctx_2048).reshape(B, 2, P, D).transpose(0, 2, 1, 3),
        "mask": mask,
        "mask_col": mask.reshape(B, 4, P).transpose(2, 0, 1),
        "router_w": rows_in(np.asarray(L0_ffn_router_weight).T),
        "router_b": np.asarray(L0_ffn_router_bias).reshape(1, E_),
        "w_expert": np.stack([gate_up[:, :, ::2], gate_up[:, :, 1::2], down], 1).reshape(
            E_, 3, KC, P, D).transpose(0, 3, 1, 2, 4),
        "b_expert": np.concatenate([gate_up_b[:, ::2], gate_up_b[:, 1::2], np.asarray(L0_ffn_down_proj_bias)], 1),
        "ident": np.eye(P, dtype=np.float32),
        "kv_mask": np.kron(np.eye(4), np.ones((32, 32))).astype(np.float32),
        "before": np.triu(np.ones((P, P), np.float32), 1),
        "iota_p": np.arange(P, dtype=np.float32).reshape(P, 1),
        "iota_f": np.tile(np.arange(P, dtype=np.float32), (P, 1)),
    }
    nc = bacc.Bacc("TRN2", target_bir_lowering=False, num_devices=1)
    ins, aps = {}, {}
    for name, a in arrays.items():
        ins[f"in_{name}"] = np.ascontiguousarray(a)
        aps[name] = nc.dram_tensor(f"in_{name}", a.shape, F32, kind="ExternalInput").ap()
    out = nc.dram_tensor("out", [TOK, D], F32, kind="ExternalOutput").ap()
    decoder_layer(nc, aps, out)
    r = run_bass_kernel_spmd(nc, [ins], core_ids=[0])
    return r.results[0]["out"].reshape(B, L, D)
```

```python
from contextlib import ExitStack

import concourse.bass as bass
from concourse import mybir

F32 = mybir.dt.float32
F32R = mybir.dt.float32r
BF16 = mybir.dt.bfloat16
I32 = mybir.dt.int32
U32 = mybir.dt.uint32
ALU = mybir.AluOpType
ACT = mybir.ActivationFunctionType
AX = mybir.AxisListType

P = 128
B, L, D = 8, 256, 512
TOK = B * L
NT = TOK // P
KC = D // P
LN_EPS = 1e-5
E_, K_TOP = 16, 4
SPLITS = ((0, 0), (0, 1), (1, 0))


def spare_registers(engine, name, n):
    return [engine.alloc_register(name=f"{name}_{i}") for i in range(n)]


def wait_apart(engine, registers, constant, *waits):
    values = []
    for (_, value), register in zip(waits, registers):
        if not isinstance(value, int):
            engine.reg_mov(register, value)
            value = register
        values.append(value)
    engine.wait_ge(*constant)
    for (semaphore, _), value in zip(waits, values):
        engine.wait_ge(semaphore, value)


def linear_attention(nc, A, x1, stage, ident, prefetch):
    H, DH = 16, 32
    INV_SCALE = DH ** -0.5
    NG, TPG = 4, 4
    GT = TPG * P
    WQ, WK, WV, WU, WO = range(5)
    with ExitStack() as ctx:
        def sb(name, shape, dt=F32):
            return ctx.enter_context(nc.sbuf_tensor(name, shape, dt))

        def sem(name):
            return ctx.enter_context(nc.semaphore(name))

        w_raw = stage[:].rearrange("p (i c d) -> p i c d", i=2, c=KC)
        w_split = sb("w_split", [P, 5, 2, KC, D], F32R)
        xT_raw = sb("xT_raw", [P, KC, GT])
        xT_split = sb("xT_split", [P, 2, KC, GT], F32R)
        x_tok = sb("x_tok", [P, 2, D])
        qT = sb("qT", [P, KC, GT])
        k_sb = sb("k_sb", [P, TPG, D])
        v_sb = sb("v_sb", [P, TPG, D])
        u_sb = sb("u_sb", [P, TPG, D])
        kv_mask = sb("kv_mask", [P, P])
        kv_sb = sb("kv_sb", [P, KC, P])
        o_sq = sb("o_sq", [P, D])
        o_ss = sb("o_ss", [P, H])
        o_rn = sb("o_rn", [P, H])
        o_norm = sb("o_norm", [P, D])
        o_sb = sb("o_sb", [P, D])
        oT_split = sb("oT_split", [P, 2, KC, P], F32R)
        y_sb = sb("y_sb", [P, D])
        stats = sb("stats", [P, 6])
        mean_var = sb("mean_var", [P, 2])
        rstd = sb("rstd", [P, 1])
        minus_half = sb("minus_half", [P, H])

        def bank(name):
            return ctx.enter_context(nc.psum_tensor(name, [P, D], F32))

        ps_q0, ps_k, ps_v, ps_u = bank("ps_q0"), bank("ps_k"), bank("ps_v"), bank("ps_u")
        ps_kv, ps_o, ps_t, ps_w = bank("ps_kv"), bank("ps_o"), bank("ps_t"), bank("ps_w")
        q_banks = [ps_k, ps_v, ps_u, ps_q0]

        w_loaded = [sem("w_loaded_even"), sem("w_loaded_odd")]
        consts_loaded = sem("consts_loaded")
        w_hi = sem("w_hi")
        w_lo = [sem(f"w_lo{w}") for w in range(5)]
        xT_loaded = sem("xT_loaded")
        xT_hi = sem("xT_hi")
        xT_lo = sem("xT_lo")
        x_loaded = [sem("x_loaded_even"), sem("x_loaded_odd")]
        q_made, q_kept = sem("q_made"), sem("q_kept")
        proj_made = sem("proj_made")
        k_kept, v_kept, u_kept = sem("k_kept"), sem("v_kept"), sem("u_kept")
        kv_made, kv_kept = sem("kv_made"), sem("kv_kept")
        o_made, o_squared, o_summed, o_scale, o_normed, o_gated = (
            sem("o_made"), sem("o_squared"), sem("o_summed"), sem("o_scale"), sem("o_normed"), sem("o_gated"))
        t_made, t_hi, t_lo = sem("t_made"), sem("t_hi"), sem("t_lo")
        y_made, y_added, y_stats, y_moments, y_rstd, x1_made = (
            sem("y_made"), sem("y_added"), sem("y_stats"), sem("y_moments"), sem("y_rstd"), sem("x1_made"))
        half_set, pool_step, clamp = sem("half_set"), sem("pool_step"), sem("clamp")

        block = ctx.enter_context(nc.Block())

        @block.sync
        def _(sp):
            def load_w(w):
                if w >= 2:
                    sp.wait_ge(w_lo[w - 2], 1)
                sp.dma_start(w_raw[:, w % 2], A["w1"][w]).then_inc(w_loaded[w % 2], 16)

            load_w(WQ)
            sp.dma_start(xT_raw[:], A["xT"][:, :, 0:GT]).then_inc(xT_loaded, 16)
            load_w(WK)
            sp.dma_start(kv_mask[:], A["kv_mask"]).then_inc(consts_loaded, 16)
            sp.dma_start(ident[:], A["ident"]).then_inc(consts_loaded, 16)
            load_w(WV)
            load_w(WU)

            def load_xT(g):
                sp.wait_ge(xT_lo, TPG * g)
                sp.dma_start(xT_raw[:], A["xT"][:, :, bass.ds(g * GT, GT)]).then_inc(xT_loaded, 16)

            load_xT(1)
            load_w(WO)

            for w in range(5):
                sp.wait_ge(w_lo[w], 1)
            prefetch(sp)

            with sp.Fori(2, NG) as g:
                load_xT(g)

        @block.gpsimd
        def _(pool):
            nc.gpsimd.memset(minus_half[:], -0.5).then_inc(half_set, 1)
            pool.wait_ge(half_set, 1)

            def split_x(g, i):
                pool.wait_ge(xT_hi, TPG * g + i + 1)
                cols = slice(i * P, i * P + P)
                nc.gpsimd.tensor_tensor(xT_split[:, 1, :, cols], xT_raw[:, :, cols],
                                        xT_split[:, 0, :, cols].bitcast(F32), ALU.subtract).then_inc(xT_lo, 1)

            for w in (WQ, WV, WO):
                pool.wait_ge(w_hi, w + 1)
                nc.gpsimd.tensor_tensor(w_split[:, w, 1], w_raw[:, w % 2], w_split[:, w, 0].bitcast(F32),
                                        ALU.subtract).then_inc(w_lo[w], 1)

            def head_scale(t):
                pool.wait_ge(o_summed, t + 1)
                nc.gpsimd.tensor_tensor(o_rn[:], o_ss[:], minus_half[:], ALU.pow).then_inc(o_scale, 1)

            def gate(t, slot):
                pool.wait_ge(o_normed, t + 1)
                pool.wait_ge(u_kept, t + 1)
                if not (isinstance(t, int) and t < 1):
                    pool.wait_ge(t_made, t)
                nc.gpsimd.tensor_tensor(o_sb[:], o_norm[:], u_sb[:, slot], ALU.mult).then_inc(o_gated, 1)

            def token_rstd(t):
                pool.wait_ge(y_moments, t + 1)
                nc.gpsimd.tensor_tensor(rstd[:], mean_var[:, 1:2], minus_half[:, 0:1], ALU.pow).then_inc(y_rstd, 1)

            def load_x(t, slot):
                if not (isinstance(t, int) and t < 2):
                    pool.wait_ge(y_added, t - 1)
                pool.dma_start(x_tok[:, slot], A["x"][bass.ds(t * P, P), :]).then_inc(x_loaded[slot], 16)

            def group(g, first, last):
                t = TPG * g
                if first:
                    load_x(0, 0)
                    load_x(1, 1)
                else:
                    head_scale(t - 1)
                    gate(t - 1, 3)
                    token_rstd(t - 2)
                    load_x(t, 0)
                    token_rstd(t - 1)
                    load_x(t + 1, 1)
                if not last:
                    split_x(g + 1, 0)
                    split_x(g + 1, 1)
                head_scale(t)
                gate(t, 0)
                head_scale(t + 1)
                if not last:
                    split_x(g + 1, 2)
                gate(t + 1, 1)
                token_rstd(t)
                load_x(t + 2, 0)
                token_rstd(t + 1)
                load_x(t + 3, 1)
                if not last:
                    split_x(g + 1, 3)
                head_scale(t + 2)
                gate(t + 2, 2)

            group(0, True, False)
            with pool.Fori(1, NG - 1) as g:
                group(g, False, False)
            group(NG - 1, False, True)
            head_scale(NT - 1)
            gate(NT - 1, 3)
            token_rstd(NT - 2)
            token_rstd(NT - 1)

        @block.scalar
        def _(act):
            def split_w(w):
                act.wait_ge(w_loaded[w % 2], 16 * (w // 2 + 1))
                nc.scalar.activation(w_split[:, w, 0], w_raw[:, w % 2], ACT.Copy).then_inc(w_hi, 1)

            def split_x(g, i, first=False):
                act.wait_ge(xT_loaded, 16 * g + 16)
                if not first:
                    act.wait_ge(proj_made, 3 * (TPG * (g - 1) + i + 1))
                cols = slice(i * P, i * P + P)
                nc.scalar.activation(xT_split[:, 0, :, cols], xT_raw[:, :, cols], ACT.Copy).then_inc(xT_hi, 1)

            def q_block(g, m):
                act.wait_ge(q_made, KC * g + m + 1)
                nc.scalar.activation(qT[:, m], q_banks[m][:], ACT.Relu, scale=INV_SCALE).then_inc(q_kept, 1)

            def keep_k(t, slot):
                act.wait_ge(proj_made, 3 * t + 1)
                nc.scalar.activation(k_sb[:, slot], ps_k[:], ACT.Relu, scale=INV_SCALE).then_inc(k_kept, 1)

            def keep_u(t, slot):
                act.wait_ge(proj_made, 3 * t + 3)
                nc.scalar.activation(u_sb[:, slot], ps_u[:], ACT.Silu).then_inc(u_kept, 1)

            def square(t, o_bank):
                act.wait_ge(o_made, t + 1)
                if not (isinstance(t, int) and t < 1):
                    act.wait_ge(o_summed, t)
                nc.scalar.activation(o_sq[:], o_bank[:], ACT.Square).then_inc(o_squared, 1)

            def keep_oT(t):
                act.wait_ge(t_made, t + 1)
                if not (isinstance(t, int) and t < 1):
                    act.wait_ge(y_made, t)
                nc.scalar.activation(oT_split[:, 0], ps_t[:].rearrange("p (c t) -> p c t", c=KC),
                                     ACT.Copy).then_inc(t_hi, 1)

            def group(g, first, last):
                t = TPG * g
                if not first:
                    square(t - 1, ps_q0)
                q_block(g, 0)
                q_block(g, 1)
                if not first:
                    keep_oT(t - 2)
                q_block(g, 2)
                if not first:
                    keep_oT(t - 1)
                q_block(g, 3)
                if first:
                    split_w(WO)
                keep_k(t, 0)
                keep_u(t, 0)
                if not last:
                    split_x(g + 1, 0)
                keep_k(t + 1, 1)
                keep_u(t + 1, 1)
                if not last:
                    split_x(g + 1, 1)
                square(t, ps_o)
                keep_k(t + 2, 2)
                square(t + 1, ps_q0)
                keep_u(t + 2, 2)
                if not last:
                    split_x(g + 1, 2)
                keep_oT(t)
                keep_k(t + 3, 3)
                keep_oT(t + 1)
                if not last:
                    split_x(g + 1, 3)
                keep_u(t + 3, 3)
                square(t + 2, ps_o)

            split_w(WQ)
            for i in range(TPG):
                split_x(0, i, True)
            for w in (WK, WV, WU):
                split_w(w)
            group(0, True, False)
            with act.Fori(1, NG - 1) as g:
                group(g, False, False)
            group(NG - 1, False, True)
            square(NT - 1, ps_q0)
            keep_oT(NT - 2)
            keep_oT(NT - 1)

        @block.vector
        def _(dve):
            held = spare_registers(dve, "held1", 1)

            def keep_v(t, slot):
                dve.wait_ge(proj_made, 3 * t + 2)
                nc.vector.tensor_copy(v_sb[:, slot], ps_v[:]).then_inc(v_kept, 1)

            def keep_kv(b):
                dve.wait_ge(kv_made, b + 1)
                if not (isinstance(b, int) and b < 1):
                    dve.wait_ge(o_made, 2 * b)
                nc.vector.tensor_tensor(kv_sb[:], ps_kv[:].rearrange("p (c v) -> p c v", c=KC),
                                        kv_mask[:].unsqueeze(1).to_broadcast([P, KC, P]),
                                        ALU.mult).then_inc(kv_kept, 1)

            def norm(t, o_bank):
                dve.wait_ge(o_squared, t + 1)
                if not (isinstance(t, int) and t < 1):
                    dve.wait_ge(o_scale, t)
                nc.vector.tensor_reduce(o_ss[:], o_sq[:].rearrange("p (h d) -> p h d", h=H), AX.X,
                                        ALU.add).then_inc(clamp, 1)
                dve.wait_ge(clamp, t + 1)
                nc.vector.tensor_scalar(o_ss[:], o_ss[:], 1.0 / DH, 1e-24, ALU.mult, ALU.max).then_inc(o_summed, 1)
                dve.wait_ge(o_scale, t + 1)
                if not (isinstance(t, int) and t < 1):
                    dve.wait_ge(o_gated, t)
                nc.vector.tensor_tensor(o_norm[:].rearrange("p (h d) -> p h d", h=H),
                                        o_bank[:].rearrange("p (h d) -> p h d", h=H),
                                        o_rn[:].unsqueeze(2).to_broadcast([P, H, DH]),
                                        ALU.mult).then_inc(o_normed, 1)

            def keep_oT(t):
                dve.wait_ge(t_hi, t + 1)
                nc.vector.tensor_tensor(oT_split[:, 1], ps_t[:].rearrange("p (c t) -> p c t", c=KC),
                                        oT_split[:, 0].bitcast(F32), ALU.subtract).then_inc(t_lo, 1)

            def layernorm(t, slot):
                dve.wait_ge(y_made, t + 1)
                dve.wait_ge(x_loaded[slot], 8 * (t - slot) + 16)
                nc.vector.tensor_tensor(y_sb[:], ps_w[:], x_tok[:, slot], ALU.add).then_inc(y_added, 1)
                dve.wait_ge(y_added, t + 1)
                nc.vector.bn_stats(stats[:], y_sb[:]).then_inc(y_stats, 1)
                wait_apart(dve, held, (half_set, 1), (y_stats, 3 * t + 1))
                nc.vector.bn_aggr(mean_var[:], stats[:]).then_inc(y_stats, 1)
                dve.wait_ge(y_stats, 3 * t + 2)
                nc.vector.tensor_scalar(mean_var[:, 1:2], mean_var[:, 1:2], LN_EPS, None,
                                        ALU.add).then_inc(y_moments, 1)
                dve.wait_ge(y_rstd, t + 1)
                nc.vector.tensor_scalar(x1[:, bass.ds(t, 1), :].squeeze(1) if not isinstance(t, int) else x1[:, t, :],
                                        y_sb[:], mean_var[:, 0:1], rstd[:, 0:1],
                                        ALU.subtract, ALU.mult).then_inc(y_stats, 1)

            def group(g, first):
                t = TPG * g
                if not first:
                    norm(t - 1, ps_q0)
                    keep_oT(t - 2)
                    layernorm(t - 2, 0)
                    keep_oT(t - 1)
                    layernorm(t - 1, 1)
                keep_v(t, 0)
                keep_v(t + 1, 1)
                keep_kv(2 * g)
                norm(t, ps_o)
                keep_v(t + 2, 2)
                norm(t + 1, ps_q0)
                keep_oT(t)
                layernorm(t, 0)
                keep_v(t + 3, 3)
                keep_oT(t + 1)
                keep_kv(2 * g + 1)
                layernorm(t + 1, 1)
                norm(t + 2, ps_o)

            for i in range(TPG):
                dve.wait_ge(xT_hi, i + 1)
                cols = slice(i * P, i * P + P)
                nc.vector.tensor_tensor(xT_split[:, 1, :, cols], xT_raw[:, :, cols],
                                        xT_split[:, 0, :, cols].bitcast(F32), ALU.subtract).then_inc(xT_lo, 1)
            for w in (WK, WU):
                dve.wait_ge(w_hi, w + 1)
                nc.vector.tensor_tensor(w_split[:, w, 1], w_raw[:, w % 2], w_split[:, w, 0].bitcast(F32),
                                        ALU.subtract).then_inc(w_lo[w], 1)
            dve.wait_ge(consts_loaded, 32)
            dve.wait_ge(half_set, 1)
            group(0, True)
            with dve.Fori(1, NG) as g:
                group(g, False)
            keep_oT(NT - 2)
            norm(NT - 1, ps_q0)
            layernorm(NT - 2, 0)
            keep_oT(NT - 1)
            layernorm(NT - 1, 1)

        @block.tensor
        def _(pe):
            def q_block(g, m, first):
                if first and m == 0:
                    pe.wait_ge(w_hi, WQ + 1)
                if m == 0:
                    pe.wait_ge(xT_hi, TPG * g + TPG)
                if not first:
                    pe.wait_ge([k_kept, v_kept, u_kept, o_normed][m], TPG * g)
                n = 0
                for wi, xi in SPLITS:
                    if m == 0 and xi:
                        pe.wait_ge(xT_lo, TPG * g + TPG)
                    if first and m == 0 and wi:
                        pe.wait_ge(w_lo[WQ], 1)
                    for c in range(KC):
                        mm = nc.tensor.matmul(q_banks[m][:], w_split[:, WQ, wi, c, m * P:(m + 1) * P],
                                              xT_split[:, xi, c, :], start=(n == 0), stop=(n == 3 * KC - 1))
                        n += 1
                mm.then_inc(q_made, 1)

            def project(g, i, w, first):
                t = TPG * g + i
                if first and i == 0:
                    pe.wait_ge(w_lo[w], 1)
                if w == WK:
                    pe.wait_ge(q_kept, KC * g + 1) if i == 0 else pe.wait_ge(k_kept, t)
                elif w == WV:
                    pe.wait_ge(q_kept, KC * g + 2) if i == 0 else pe.wait_ge(v_kept, t)
                else:
                    pe.wait_ge(q_kept, KC * g + 3) if i == 0 else pe.wait_ge(u_kept, t)
                out = {WK: ps_k, WV: ps_v, WU: ps_u}[w]
                n = 0
                for wi, xi in SPLITS:
                    for c in range(KC):
                        mm = nc.tensor.matmul(out[:], xT_split[:, xi, c, i * P:(i + 1) * P],
                                              w_split[:, w, wi, c, :], start=(n == 0), stop=(n == 3 * KC - 1))
                        n += 1
                mm.then_inc(proj_made, 1)

            def kv(b, slot):
                pe.wait_ge(k_kept, 2 * b + 2)
                pe.wait_ge(v_kept, 2 * b + 2)
                if not (isinstance(b, int) and b < 1):
                    pe.wait_ge(kv_kept, b)
                for c in range(KC):
                    for i in range(2):
                        mm = nc.tensor.matmul(ps_kv[:, c * P:(c + 1) * P], k_sb[:, slot + i, c * P:(c + 1) * P],
                                              v_sb[:, slot + i, c * P:(c + 1) * P], start=(i == 0), stop=(i == 1))
                mm.then_inc(kv_made, 1)

            def attend(g, i, o_bank, first):
                t = TPG * g + i
                if i == 0:
                    pe.wait_ge(q_kept, KC * g + 4)
                    pe.wait_ge(kv_kept, 2 * g + 1)
                if i == 2:
                    pe.wait_ge(kv_kept, 2 * g + 2)
                    pe.wait_ge(o_normed, t - 1)
                elif i == 3:
                    pe.wait_ge(o_normed, t - 1)
                elif i == 0 and not first:
                    pe.wait_ge(o_normed, t - 1)
                for c in range(KC):
                    mm = nc.tensor.matmul(o_bank[:, c * P:(c + 1) * P], qT[:, c, i * P:(i + 1) * P],
                                          kv_sb[:, c, :], start=True, stop=True)
                mm.then_inc(o_made, 1)

            def transpose_o(t):
                pe.wait_ge(o_gated, t + 1)
                if isinstance(t, int) and t < 1:
                    pe.wait_ge(consts_loaded, 32)
                else:
                    pe.wait_ge(t_lo, t)
                for c in range(KC):
                    mm = nc.tensor.transpose(ps_t[:, c * P:(c + 1) * P], o_sb[:, c * P:(c + 1) * P], ident[:])
                mm.then_inc(t_made, 1)

            def project_out(t):
                pe.wait_ge(t_lo, t + 1)
                if isinstance(t, int) and t < 1:
                    pe.wait_ge(w_lo[WO], 1)
                else:
                    pe.wait_ge(y_added, t)
                n = 0
                for wi, oi in SPLITS:
                    for c in range(KC):
                        mm = nc.tensor.matmul(ps_w[:], oT_split[:, oi, c, :], w_split[:, WO, wi, c, :],
                                              start=(n == 0), stop=(n == 3 * KC - 1))
                        n += 1
                mm.then_inc(y_made, 1)

            def group(g, first):
                t = TPG * g
                q_block(g, 0, first)
                q_block(g, 1, first)
                if not first:
                    transpose_o(t - 2)
                q_block(g, 2, first)
                if not first:
                    project_out(t - 2)
                    transpose_o(t - 1)
                q_block(g, 3, first)
                if not first:
                    project_out(t - 1)
                project(g, 0, WK, first)
                project(g, 0, WV, first)
                project(g, 0, WU, first)
                project(g, 1, WK, first)
                project(g, 1, WV, first)
                project(g, 1, WU, first)
                kv(2 * g, 0)
                project(g, 2, WK, first)
                attend(g, 0, ps_o, first)
                attend(g, 1, ps_q0, first)
                project(g, 2, WV, first)
                project(g, 2, WU, first)
                transpose_o(t)
                project(g, 3, WK, first)
                project_out(t)
                project(g, 3, WV, first)
                transpose_o(t + 1)
                kv(2 * g + 1, 2)
                project(g, 3, WU, first)
                project_out(t + 1)
                attend(g, 2, ps_o, first)
                attend(g, 3, ps_q0, first)

            group(0, True)
            with pe.Fori(1, NG) as g:
                group(g, False)
            transpose_o(NT - 2)
            project_out(NT - 2)
            transpose_o(NT - 1)
            project_out(NT - 1)
def attention_inputs(stage):
    at, views = 0, {}
    for name, shape in (("w2", (3, 2, 2 * P)), ("ctx", (2, D)), ("mask", (D,)), ("m_rows", (D,)),
                        ("bias_v", (2 * P,)), ("bias_qk", (2, 2)), ("mask_col", (B, D // P))):
        size = 1
        for n in shape:
            size *= n
        view = stage[:, at:at + size]
        if len(shape) == 3:
            view = view.rearrange("p (a b c) -> p a b c", a=shape[0], b=shape[1])
        elif len(shape) == 2:
            view = view.rearrange("p (a b) -> p a b", a=shape[0])
        views[name] = view
        at += size
    return views


def load_attention_inputs(sp, A, V, loaded, in_loaded):
    sp.dma_start(V["m_rows"][0:B], A["mask"]).then_inc(loaded, 16)
    sp.dma_start(V["w2"], A["w2"].rearrange("w p c o -> p w c o")).then_inc(loaded, 16)
    sp.dma_start(V["bias_qk"], A["bias_qk"]).then_inc(loaded, 16)
    sp.dma_start(V["bias_v"], A["bias_v"].to_broadcast([P, 2 * P])).then_inc(loaded, 16)
    sp.dma_start(V["mask_col"], A["mask_col"]).then_inc(loaded, 16)
    sp.dma_start(V["ctx"], A["ctx"][0]).then_inc(in_loaded, 16)
    sp.dma_start(V["mask"], A["mask"][0:1].to_broadcast([P, D])).then_inc(in_loaded, 16)


def cross_attention(nc, A, S, x, R, V, ident, consts_loaded, in_loaded):
    H, DH, C, T = 16, 16, 2 * P, D
    NQ, HQ, NC = 4, 4, T // P
    PENALTY = 4e6
    ROWS_A, ROWS_B = 6 * DH + 9, 6 * DH + 12
    STEPS = NQ * NC
    MISC0, MISC = 9, 10
    STACK_DMAS = 8
    with ExitStack() as ctx:
        def sb(name, shape, dt=F32):
            return ctx.enter_context(nc.sbuf_tensor(name, shape, dt))

        def sem(name):
            return ctx.enter_context(nc.semaphore(name))

        w2, bias_qk, bias_v, mask_col, m_rows = (
            V["w2"], V["bias_qk"], V["bias_v"], V["mask_col"], V["m_rows"][0:B])
        ctx_sb, mask_in = V["ctx"], V["mask"]
        mask_now = sb("mask_now", [P, NC])
        pen_rows = sb("pen_rows", [B, T])
        rest_rows = sb("rest_rows", [B, T])
        row_parts = sb("row_parts", [B, 7, T], BF16)
        mask_out = sb("mask_out", [P, T])
        full = sb("full", [P, 4, T])
        rest = sb("rest", [P, 4, T])
        parts = sb("parts", [P, 4, 3, T], BF16)
        q_stack = sb("q_stack", [P, H, T], BF16)
        k_stack = sb("k_stack", [P, H, T], BF16)
        v_stage = sb("v_stage", [P, NC, C])
        v_aug = sb("v_aug", [P, NC, H, 32])
        probs = sb("probs", [P, 2, HQ, T])
        row_max = sb("row_max", [P, 2, HQ, NC])
        neg_max = sb("neg_max", [HQ * NC, P])
        neg_rest = sb("neg_rest", [HQ * NC, P])
        neg_parts = sb("neg_parts", [HQ * NC, 3, P], BF16)
        o_sb = sb("o_sb2", [P, 2, T])
        den = sb("den", [P, H * T // P])
        inv = sb("inv", [P, H * T // P])
        num_sb = sb("num_sb", [P, 2, T])
        inv_sb = sb("inv_sb", [P, 2, T])
        stats = sb("stats2", [P, 2, 6])
        mean_var = sb("mean_var2", [P, 2, 2])
        rstd = sb("rstd2", [P, 2])
        minus_half = sb("minus_half2", [P, 2])

        ps_a = [ctx.enter_context(nc.psum_tensor(f"ps_a{i}", [P, 2, T], F32)) for i in range(2)]
        ps_b = [ctx.enter_context(nc.psum_tensor(f"ps_b{i}", [P, T], F32)) for i in range(2)]
        ps_pv = ctx.enter_context(nc.psum_tensor("ps_pv", [P, T], F32))
        ps_misc = ctx.enter_context(nc.psum_tensor("ps_misc", [P, T], F32))

        mask_step, rows_made, rows_stored = sem("mask_step"), sem("rows_made"), sem("rows_stored")
        consts_set = sem("consts2_set")
        misc_made, misc_kept = sem("misc_made"), sem("misc_kept")
        part1, rest1, part2, part3 = sem("part1"), sem("rest1"), sem("part2"), sem("part3")
        parts_stored = [sem("parts_stored_q"), sem("parts_stored_k")]
        stack_loaded = [sem(f"stack_loaded{i}") for i in range(NQ)]
        a_made = [sem("a_made0"), sem("a_made1")]
        a_kept = [sem("a_kept0"), sem("a_kept1")]
        max_step, max_ready = sem("max_step"), sem("max_ready")
        max_stored = sem("max_stored")
        max_loaded = [sem(f"max_loaded{i}") for i in range(NQ)]
        b_made, exp_done = sem("b_made"), sem("exp_done")
        v_staged, v_filled = sem("v_staged"), sem("v_filled")
        mask_now_set = sem("mask_now_set")
        pv_made, o_kept = sem("pv_made"), sem("o_kept")
        o_stored = [sem("o_stored0"), sem("o_stored1")]
        den_loaded, inv_made, inv_stored, out_loaded = (
            sem("den_loaded"), sem("inv_made"), sem("inv_stored"), sem("out_loaded"))
        attn_scaled, attn_masked = sem("attn_scaled"), sem("attn_masked")
        y_added, y_stats, y_moments, y_rstd, x2_made, x2_stored = (
            sem("y2_added"), sem("y2_stats"), sem("y2_moments"), sem("y2_rstd"), sem("x2_made"), sem("x2_stored"))

        first_banks = [ps_misc[:], ps_b[0][:], ps_b[1][:], ps_pv[:], ps_a[0][:, 0], ps_a[0][:, 1]]
        groups = [range(0, 4), range(4, 8), range(8, 12), range(12, 14), range(14, 16)]
        xT = sb("xT_router", [P, 2, KC, T])
        logitT = sb("logitT", [E_, 2, T])
        xT_made, xT_kept, logitT_made, logitT_kept, logits_made, logits_kept = (
            sem("rx_made"), sem("rx_kept"), sem("logitT_made"), sem("logitT_kept"), sem("logits_made"),
            sem("logits_kept"))

        block = ctx.enter_context(nc.Block())

        def at(ref, i):
            return ref[i] if isinstance(i, int) else ref[bass.ds(i, 1)].squeeze(0)

        @block.sync
        def _(sp):
            held = spare_registers(sp, "held2", 1)

            def wait(semaphore, value):
                wait_apart(sp, held, (consts_loaded, 80), (semaphore, value))

            def load_inputs(b):
                sp.dma_start(ctx_sb, at(A["ctx"], b)).then_inc(in_loaded, 16)
                sp.dma_start(mask_in, at(A["mask"], b).unsqueeze(0).to_broadcast([P, T])).then_inc(in_loaded, 16)

            def store_parts(b, i):
                qk, o = i % 2, i // 2
                wait(part3, 4 * b + i + 1)
                for j in range(3):
                    sp.dma_start(at(S["parts"], b)[qk, j, :, 8 * o:8 * o + 8, :].rearrange("d h t -> h d t"),
                                 parts[:, i, j]).then_inc(parts_stored[qk], 16)

            def load_stack(b, q, first, halves=(0, 1)):
                if not first:
                    wait(b_made, 64 * (b - 1) + 16 * (q + 1))
                heads = slice(HQ * q, HQ * q + HQ)
                for qk in halves:
                    stack = (q_stack, k_stack)[qk]
                    wait(parts_stored[qk], 96 * b + 48 * (q // 2) + 48)
                    src = at(S["parts"], b)[qk, :, :, heads, :].rearrange("j d h t -> j d (h t)")
                    at_row = 0
                    for n in (3, 2, 1):
                        dst = stack[at_row:at_row + n * DH, heads, :].rearrange("r h t -> r (h t)")
                        if qk == 0:
                            one = src[0:n].rearrange("j d t -> (j d) t")
                            sp.dma_start(dst, one).then_inc(stack_loaded[q], 16)
                        else:
                            one = src[3 - n:4 - n].to_broadcast([n, DH, HQ * T])
                            sp.dma_start(dst, one).then_inc(stack_loaded[q], 16)
                        at_row += n * DH
                    n, rows = ((9, S["rows_q"]), (12, S["rows_k"]))[qk]
                    sp.dma_start(stack[6 * DH:6 * DH + n, heads, :],
                                 at(rows, b).unsqueeze(1).to_broadcast([n, HQ, T])).then_inc(stack_loaded[q], 16)

            def store_max(b, q):
                wait(max_ready, 4 * b + q + 1)
                sp.dma_start(at(S["max"], b)[q].rearrange("j (n t) -> n j t", t=P), neg_parts[:]).then_inc(
                    max_stored, 16)

            def load_max(b, q):
                wait(max_stored, 16 * (4 * b + q + 1))
                d = at(S["max"], b)[q]
                sp.dma_start(q_stack[ROWS_A:ROWS_B, HQ * q:HQ * q + HQ, :],
                             d.rearrange("j (h t) -> j h t", h=HQ)).then_inc(max_loaded[q], 16)

            def store_o(b, q):
                wait(o_kept, 4 * b + q + 1)
                sp.dma_start(at(S["heads"], b)[HQ * q:HQ * q + HQ].rearrange("h r t -> (h r) t"),
                             o_sb[:, q % 2, :]).then_inc(o_stored[q % 2], 16)

            def store_x2(b):
                wait(x2_made, 2 * b + 2)
                sp.dma_start(S["x2"][bass.ds(b * L, L), :].rearrange("(i p) d -> p i d", p=P),
                             x[:, bass.ds(b * 2, 2), :]).then_inc(x2_stored, 16)

            load_router(sp, A, R)
            for i in range(2):
                store_parts(0, i)
            wait(rows_stored, 16 * 9)
            load_stack(0, 0, True)
            load_stack(0, 1, True)
            for i in range(2, 4):
                store_parts(0, i)
            wait(v_staged, 2)
            load_inputs(1)
            load_stack(0, 2, True)
            load_stack(0, 3, True)
            store_max(0, 0)
            load_max(0, 0)

            def batch(b, first, last, before_last=False):
                if not first:
                    store_o(b - 1, 3)
                store_max(b, 1)
                if not first:
                    load_stack(b, 3, False, (0,))
                load_max(b, 1)
                if not first:
                    load_stack(b, 3, False, (1,))
                if not last:
                    store_parts(b + 1, 0)
                    store_parts(b + 1, 1)
                store_max(b, 2)
                if not last:
                    load_stack(b + 1, 0, False, (0,))
                load_max(b, 2)
                if not last:
                    load_stack(b + 1, 0, False, (1,))
                store_o(b, 0)
                if not (last or before_last):
                    wait(v_staged, 2 * b + 4)
                    load_inputs(b + 2)
                store_o(b, 1)
                store_max(b, 3)
                if not last:
                    load_stack(b + 1, 1, False, (0,))
                load_max(b, 3)
                if not last:
                    load_stack(b + 1, 1, False, (1,))
                    store_parts(b + 1, 2)
                    store_parts(b + 1, 3)
                store_o(b, 2)
                if not last:
                    store_max(b + 1, 0)
                    load_stack(b + 1, 2, False, (0,))
                    load_max(b + 1, 0)
                    load_stack(b + 1, 2, False, (1,))
                if not first:
                    store_x2(b - 1)

            batch(0, True, False)
            with sp.Fori(1, B - 2) as b:
                batch(b, False, False)
            batch(B - 2, False, False, True)
            batch(B - 1, False, True)
            store_o(B - 1, 3)
            store_x2(B - 1)
            wait(x2_stored, 16 * B)

        @block.gpsimd
        def _(pool):
            nc.gpsimd.memset(minus_half[:], -0.5).then_inc(consts_set, 1)
            nc.gpsimd.memset(v_aug[:], 1.0).then_inc(consts_set, 1)
            pool.wait_ge(consts_set, 2)

            def split(b, i):
                k, s = 4 * b + i, i
                pool.wait_ge(part1, k + 1)
                nc.gpsimd.tensor_tensor(rest[:, s], full[:, s], parts[:, s, 0], ALU.subtract).then_inc(rest1, 1)
                pool.wait_ge(part2, k + 1)
                nc.gpsimd.tensor_tensor(parts[:, s, 2], rest[:, s], parts[:, s, 1], ALU.subtract).then_inc(part3, 1)

            held = spare_registers(pool, "held2", 1)

            def wait(semaphore, value):
                wait_apart(pool, held, (consts_set, 2), (semaphore, value))

            def load_den(b, first=False):
                if not first:
                    wait(x2_made, 2 * b)
                wait(o_stored[0], 32 * (b + 1))
                wait(o_stored[1], 32 * (b + 1))
                pool.dma_start(den[:], at(S["heads"], b)[:, DH, :].rearrange("h (a t) -> h a t", a=8)).then_inc(
                    den_loaded, 16)
                for o in range(2):
                    pool.dma_start(num_sb[:, o, :], at(S["heads"], b)[8 * o:8 * o + 8, 0:DH, :]).then_inc(out_loaded, 16)

            def load_out(b):
                wait(inv_made, b + 1)
                pool.dma_start(at(S["inv"], b).rearrange("h (a t) -> (h a) t", a=8), inv[:]).then_inc(inv_stored, 16)
                pool.dma_start(mask_out[:], at(A["mask"], b).unsqueeze(0).to_broadcast([P, T])).then_inc(out_loaded, 16)
                wait(inv_stored, 16 * (b + 1))
                for o in range(2):
                    pool.dma_start(inv_sb[:, o, :], at(S["inv"], b)[8 * o:8 * o + 8].unsqueeze(1).to_broadcast(
                        [8, DH, T])).then_inc(out_loaded, 16)

            def finish_heads(b):
                pool.wait_ge(out_loaded, 80 * b + 80)
                nc.gpsimd.tensor_tensor(inv_sb[:], inv_sb[:], mask_out[:].unsqueeze(1).to_broadcast([P, 2, T]),
                                        ALU.mult).then_inc(attn_scaled, 1)
                pool.wait_ge(attn_scaled, b + 1)
                nc.gpsimd.tensor_tensor(num_sb[:], num_sb[:], inv_sb[:], ALU.mult).then_inc(attn_masked, 1)
                pool.wait_ge(attn_masked, b + 1)
                nc.gpsimd.tensor_tensor(num_sb[:], num_sb[:], x[:, bass.ds(2 * b, 2), :], ALU.add).then_inc(y_added, 1)

            def token_rstd(b):
                pool.wait_ge(y_moments, b + 1)
                nc.gpsimd.tensor_tensor(rstd[:], mean_var[:, :, 1], minus_half[:], ALU.pow).then_inc(y_rstd, 1)

            for i in range(4):
                split(0, i)
            for i in range(2):
                split(1, i)

            def batch(b, first, last, before_last=False, second=False):
                if not first:
                    load_den(b - 1, second)
                if not last:
                    split(b + 1, 2)
                    split(b + 1, 3)
                if not first:
                    load_out(b - 1)
                    finish_heads(b - 1)
                    token_rstd(b - 1)
                if not (last or before_last):
                    split(b + 2, 0)
                    split(b + 2, 1)

            batch(0, True, False)
            batch(1, False, False, False, True)
            with pool.Fori(2, B - 2) as b:
                batch(b, False, False)
            batch(B - 2, False, False, True)
            batch(B - 1, False, True)
            load_den(B - 1)
            load_out(B - 1)
            finish_heads(B - 1)
            token_rstd(B - 1)

        @block.scalar
        def _(act):
            def exps(b, q, c, first):
                n = STEPS * b + NC * q + c
                if not (first and NC * q + c < 2):
                    act.wait_ge(pv_made, n - 1)
                for h in range(HQ):
                    act.wait_ge(b_made, 4 * n + h + 1)
                    nc.scalar.activation(probs[:, c % 2, h], ps_b[h % 2][:], ACT.Exp, scale=DH ** -0.5).then_inc(
                        exp_done, 1)

            def keep_o(b, q, first):
                act.wait_ge(pv_made, STEPS * b + NC * q + NC)
                if not (first and q < 2):
                    act.wait_ge(o_stored[q % 2], 32 * b + 16 * (q // 2))
                nc.scalar.activation(o_sb[:, q % 2], ps_pv[:], ACT.Copy).then_inc(o_kept, 1)

            def batch(b, first):
                for q in range(NQ):
                    for c in range(NC):
                        exps(b, q, c, first)
                        if c == 0 and q > 0:
                            keep_o(b, q - 1, first)
                        elif c == 0 and not first:
                            keep_o(b - 1, 3, False)

            act.wait_ge(rows_made, 6)
            for rows, first_row, n, part, repeat in (
                    ("rows_q", 0, 3, 0, False), ("rows_q", 3, 3, 3, True), ("rows_q", 6, 2, 4, True),
                    ("rows_q", 8, 1, 5, False), ("rows_k", 0, 3, 6, True), ("rows_k", 3, 3, 0, False),
                    ("rows_k", 6, 2, 0, False), ("rows_k", 8, 1, 0, False), ("rows_k", 9, 3, 6, True)):
                src = (row_parts[:, part:part + 1].to_broadcast([B, n, T]) if repeat
                       else row_parts[:, part:part + n])
                act.dma_start(S[rows][:, first_row:first_row + n, :], src).then_inc(rows_stored, 16)

            batch(0, True)
            with act.Fori(1, B) as b:
                batch(b, False)
            keep_o(B - 1, 3, False)

            for g, tiles in enumerate(groups):
                for n, t in enumerate(tiles):
                    act.wait_ge(xT_made, t + 1)
                    if g >= 2:
                        act.wait_ge(logitT_made, g - 1)
                    nc.scalar.activation(xT[:, g % 2, :, n * P:(n + 1) * P],
                                         ps_a[t // 2 % 2][:, t % 2].rearrange("p (c t) -> p c t", c=KC),
                                         ACT.Copy).then_inc(xT_kept, 1)
                act.wait_ge(logitT_made, g + 1)
                if g >= 2:
                    act.wait_ge(logits_made, g - 1)
                n = len(tiles) * P
                nc.scalar.activation(logitT[:, g % 2, 0:n], ps_b[g % 2][0:E_, 0:n], ACT.Copy).then_inc(logitT_kept, 1)

        @block.vector
        def _(dve):
            held = spare_registers(dve, "held2", 1)

            def row_split(src, j, k):
                nc.vector.tensor_copy(row_parts[:, j], src).then_inc(mask_step, 1)
                dve.wait_ge(mask_step, k + 1)
                nc.vector.tensor_tensor(rest_rows[:], src, row_parts[:, j], ALU.subtract).then_inc(mask_step, 1)
                dve.wait_ge(mask_step, k + 2)
                nc.vector.tensor_copy(row_parts[:, j + 1], rest_rows[:]).then_inc(mask_step, 1)
                dve.wait_ge(mask_step, k + 3)
                nc.vector.tensor_tensor(row_parts[:, j + 2], rest_rows[:], row_parts[:, j + 1],
                                        ALU.subtract).then_inc(rows_made, 1)

            def reduces(k, par, c, halves=(0, 1)):
                for i in halves:
                    dve.wait_ge(a_made[i], k + 1)
                    nc.vector.tensor_reduce(row_max[:, par, 2 * i:2 * i + 2, c], ps_a[i][:], AX.X,
                                            ALU.max).then_inc(a_kept[i], 1)

            def keep_max(m):
                dve.wait_ge(misc_made, m + 1)
                nc.vector.tensor_scalar(neg_max[:], ps_misc[0:HQ * NC, 0:P], -1.0, None, ALU.mult).then_inc(misc_kept, 1)

            def cut_max(k, m, first=False):
                dve.wait_ge(misc_kept, m + 1)
                if not first:
                    dve.wait_ge(max_stored, 16 * k)
                nc.vector.tensor_copy(neg_parts[:, 0], neg_max[:]).then_inc(max_step, 1)
                dve.wait_ge(max_step, 3 * k + 1)
                nc.vector.tensor_tensor(neg_rest[:], neg_max[:], neg_parts[:, 0], ALU.subtract).then_inc(max_step, 1)
                dve.wait_ge(max_step, 3 * k + 2)
                nc.vector.tensor_copy(neg_parts[:, 1], neg_rest[:]).then_inc(max_step, 1)
                dve.wait_ge(max_step, 3 * k + 3)
                nc.vector.tensor_tensor(neg_parts[:, 2], neg_rest[:], neg_parts[:, 1],
                                        ALU.subtract).then_inc(max_ready, 1)

            def keep_qk(b, i, m, first=False):
                dve.wait_ge(misc_made, m + 1)
                dve.wait_ge(in_loaded, 32 * b + 32)
                if not first:
                    dve.wait_ge(part3, 4 * b + i - 3)
                    dve.wait_ge(parts_stored[i % 2], 96 * b + 48 * (i // 2) - 48)
                bank = first_banks[i] if first else ps_misc[:]
                nc.vector.scalar_tensor_tensor(full[:, i], bank, bias_qk[:, i % 2, i // 2:i // 2 + 1], mask_in,
                                               ALU.add, ALU.mult).then_inc(misc_kept, 1)

            def first_part(i, m):
                dve.wait_ge(misc_kept, m + 1)
                nc.vector.tensor_copy(parts[:, i, 0], full[:, i]).then_inc(part1, 1)

            def cut(b, i):
                dve.wait_ge(rest1, 4 * b + i + 1)
                nc.vector.tensor_copy(parts[:, i, 1], rest[:, i]).then_inc(part2, 1)

            def stage_v(b, i, m, first=False):
                dve.wait_ge(misc_made, m + 1)
                if not first:
                    dve.wait_ge(v_filled, 4 * b)
                bank = first_banks[4 + i] if first else ps_misc[:]
                nc.vector.tensor_tensor(v_stage[:, 2 * i:2 * i + 2], bank.rearrange("p (s c) -> p s c", s=2),
                                        bias_v.unsqueeze(1).to_broadcast([P, 2, C]), ALU.add)\
                    .then_inc(misc_kept, 1)
                dve.wait_ge(misc_kept, m + 1)
                nc.vector.tensor_copy(mask_now[:, 2 * i:2 * i + 2],
                                      mask_col[:, bass.ds(b, 1), 2 * i:2 * i + 2].squeeze(1)).then_inc(v_staged, 1)

            def fill_v(b, first=False):
                dve.wait_ge(v_staged, 2 * b + 2)
                if not first:
                    dve.wait_ge(pv_made, STEPS * b)
                for c in range(NC):
                    nc.vector.tensor_scalar(v_aug[:, c, :, 0:DH], v_stage[:, c].rearrange("p (h d) -> p h d", h=H),
                                            mask_now[:, c:c + 1], None, ALU.mult).then_inc(v_filled, 1)

            def invert(b):
                dve.wait_ge(den_loaded, 16 * (b + 1))
                nc.vector.reciprocal(inv[:], den[:]).then_inc(inv_made, 1)

            def moments(b):
                dve.wait_ge(y_added, b + 1)
                for i in range(2):
                    nc.vector.bn_stats(stats[:, i], num_sb[:, i]).then_inc(y_stats, 1)
                wait_apart(dve, held, (consts_set, 2), (y_stats, 4 * b + 2))
                for i in range(2):
                    nc.vector.bn_aggr(mean_var[:, i], stats[:, i]).then_inc(y_stats, 1)
                dve.wait_ge(y_stats, 4 * b + 4)
                nc.vector.tensor_scalar(mean_var[:, :, 1], mean_var[:, :, 1], LN_EPS, None, ALU.add).then_inc(
                    y_moments, 1)

            def normalize(b):
                dve.wait_ge(y_rstd, b + 1)
                for i in range(2):
                    nc.vector.tensor_scalar(x[:, bass.ds(2 * b + i, 1), :].squeeze(1), num_sb[:, i],
                                            mean_var[:, i, 0:1], rstd[:, i:i + 1], ALU.subtract, ALU.mult)\
                        .then_inc(x2_made, 1)

            dve.wait_ge(consts_loaded, 80)
            nc.vector.memset(row_parts[:, 6], 1.0).then_inc(rows_made, 1)
            nc.vector.tensor_scalar(pen_rows[:], m_rows, -1.0, PENALTY, ALU.add, ALU.mult).then_inc(mask_step, 1)
            dve.wait_ge(mask_step, 1)
            row_split(pen_rows[:], 0, 1)
            dve.wait_ge(rows_made, 2)
            row_split(m_rows, 3, 4)
            dve.wait_ge(rows_made, 3)
            nc.vector.memset(rest_rows[:], 0.0).then_inc(rows_made, 3)
            for i in range(2):
                keep_qk(0, i, i, True)
                first_part(i, i)
            for i in range(2):
                cut(0, i)
            for i in range(2, 4):
                keep_qk(0, i, i, True)
                first_part(i, i)
            for i in range(2, 4):
                cut(0, i)
            dve.wait_ge(consts_set, 2)
            stage_v(0, 0, 4, True)
            stage_v(0, 1, 5, True)
            for c in range(NC):
                reduces(c, 0, c)
            keep_max(6)
            cut_max(0, 6, True)
            for i in range(2):
                keep_qk(1, i, 7 + i)
                first_part(i, 7 + i)
            for i in range(2):
                cut(1, i)
            for c in range(NC):
                reduces(NC + c, 1, c)

            def batch(b, first, last, before_last=False):
                m = MISC0 + MISC * b - (2 if last else 0)
                for q in range(NQ):
                    for c in range(NC):
                        s = NC * q + c
                        turned = c == 0 and not (last and q == 3)
                        qk = None
                        if s in (2, 3) and not last:
                            qk = b + 1, s, m + s - 1
                        elif s in (14, 15) and not (last or before_last):
                            qk = b + 2, s - 14, m + s - 6
                        if qk:
                            keep_qk(*qk)
                        elif not last and s in (6, 7):
                            stage_v(b + 1, s - 6, m + s - 2)
                        if not (last and q >= 2):
                            reduces(2 * NC + STEPS * b + s, q % 2, c)
                        if s == 0:
                            fill_v(b, first)
                        if turned:
                            before = m + (q if last else (0, 3, 6, 7)[q])
                            keep_max(before)
                            cut_max(4 * b + q + 1, before)
                        if qk:
                            first_part(qk[1], qk[2])
                        if not last and s in (3, 4):
                            cut(b + 1, s - 1)
                        elif s == 15 and not (last or before_last):
                            cut(b + 2, 0)
                        elif s == 0 and not (first or last):
                            cut(b + 1, 1)
                        if not first:
                            if s == 4:
                                invert(b - 1)
                            elif s == 10:
                                moments(b - 1)
                            elif s == 12:
                                normalize(b - 1)

            batch(0, True, False)
            with dve.Fori(1, B - 2) as b:
                batch(b, False, False)
            batch(B - 2, False, False, True)
            batch(B - 1, False, True)
            invert(B - 1)
            moments(B - 1)
            normalize(B - 1)
            dve.wait_ge(R["loaded"], 80)
            for g in range(len(groups)):
                dve.wait_ge(logits_made, g + 1)
            nc.vector.tensor_tensor(R["logits"][:], ps_misc[:, 0:NT * E_].rearrange("p (t e) -> p t e", t=NT),
                                    R["b"][:].unsqueeze(1).to_broadcast([P, NT, E_]), ALU.add).then_inc(logits_kept, 1)
            dve.wait_ge(logits_kept, 1)

        @block.tensor
        def _(pe):
            def scores_max(k, b, q, c, i, first=False):
                if c == 0 and i == 0:
                    pe.wait_ge(stack_loaded[q], 16 * STACK_DMAS * (b + 1))
                if not first:
                    pe.wait_ge(a_kept[i], k)
                for j in range(2):
                    h = HQ * q + 2 * i + j
                    mm = nc.tensor.matmul(ps_a[i][:, j], q_stack[0:ROWS_A, h, c * P:(c + 1) * P],
                                          k_stack[0:ROWS_A, h, :], start=True, stop=True)
                mm.then_inc(a_made[i], 1)

            def scores(b, q, c, h, first):
                e = 64 * b + 16 * q + 4 * c + h
                if c == 0 and h == 0:
                    pe.wait_ge(max_loaded[q], 16 * (b + 1))
                if not (first and 16 * q + 4 * c + h < 2):
                    pe.wait_ge(exp_done, e - 1)
                hh = HQ * q + h
                nc.tensor.matmul(ps_b[h % 2][:], k_stack[0:ROWS_B, hh, c * P:(c + 1) * P],
                                 q_stack[0:ROWS_B, hh, :], start=True, stop=True).then_inc(b_made, 1)

            def values(b, q, c, first):
                n = STEPS * b + NC * q + c
                pe.wait_ge(exp_done, 4 * n + 4)
                if c == 0:
                    if q == 0:
                        pe.wait_ge(v_filled, 4 * b + 4)
                    if not (first and q == 0):
                        pe.wait_ge(o_kept, 4 * b + q)
                for g in range(HQ):
                    mm = nc.tensor.matmul(ps_pv[32 * g:32 * g + 32, :], v_aug[:, c, HQ * q + g, :],
                                          probs[:, c % 2, g], start=(c == 0), stop=(c == NC - 1))
                mm.then_inc(pv_made, 1)

            def free_misc(m, first):
                if not first:
                    pe.wait_ge(misc_kept, m)

            def project_qk(b, i, m, first=False):
                s, o = i % 2, i // 2
                if i < 2:
                    pe.wait_ge(in_loaded, 32 * b + 32)
                if not first:
                    free_misc(m, False)
                bank = first_banks[i] if first else ps_misc[:]
                for c in range(2):
                    rhs = ctx_sb[:, c] if s else x[:, bass.ds(2 * b + c, 1), :].squeeze(1)
                    mm = nc.tensor.matmul(bank, w2[:, s, c, o * P:(o + 1) * P], rhs,
                                          start=(c == 0), stop=(c == 1))
                mm.then_inc(misc_made, 1)

            def project_v(b, i, m, first=False):
                if not first:
                    free_misc(m, False)
                bank = first_banks[4 + i] if first else ps_misc[:]
                for j in range(2):
                    sc = 2 * i + j
                    for c in range(2):
                        mm = nc.tensor.matmul(bank[:, j * C:(j + 1) * C], ctx_sb[:, c, sc * P:(sc + 1) * P],
                                              w2[:, 2, c, :], start=(c == 0), stop=(c == 1))
                mm.then_inc(misc_made, 1)

            def transpose_max(m, par, k):
                free_misc(m, False)
                for i in range(2):
                    pe.wait_ge(a_kept[i], k)
                nc.tensor.transpose(ps_misc[0:HQ * NC, 0:P], row_max[:, par].rearrange("p h c -> p (h c)"),
                                    ident[:]).then_inc(misc_made, 1)

            pe.wait_ge(consts_loaded, 80)
            for i in range(4):
                project_qk(0, i, i, True)
            project_v(0, 0, 4, True)
            project_v(0, 1, 5, True)
            pe.wait_ge(misc_kept, 6)
            for c in range(NC):
                for i in range(2):
                    scores_max(c, 0, 0, c, i, c == 0)
            transpose_max(6, 0, NC)
            for i in range(2):
                project_qk(1, i, 7 + i)
            for c in range(NC):
                for i in range(2):
                    scores_max(NC + c, 0, 1, c, i)

            def batch(b, first, last, before_last=False):
                m = MISC0 + MISC * b - (2 if last else 0)
                for q in range(NQ):
                    for c in range(NC):
                        s = NC * q + c
                        k = 2 * NC + STEPS * b + s
                        ahead = not (last and q >= 2)
                        b2, q2 = (b, q + 2) if q < 2 else (b + 1, q - 2)
                        if ahead:
                            scores_max(k, b2, q2, c, 0)
                            scores_max(k, b2, q2, c, 1)
                        scores(b, q, c, 0, first)
                        scores(b, q, c, 1, first)
                        if c == 0 and not (last and q == 3):
                            before = q if last else (0, 3, 6, 7)[q]
                            transpose_max(m + before, (q + 1) % 2, k)
                        if s > 0:
                            values(b, (s - 1) // NC, (s - 1) % NC, first)
                        elif not first:
                            values(b - 1, NQ - 1, NC - 1, False)
                        scores(b, q, c, 2, first)
                        scores(b, q, c, 3, first)
                        if not last:
                            if s in (1, 2):
                                project_qk(b + 1, s + 1, m + s)
                            elif s in (5, 6):
                                project_v(b + 1, s - 5, m + s - 1)
                            elif s in (13, 14) and not before_last:
                                project_qk(b + 2, s - 13, m + s - 5)

            batch(0, True, False)
            with pe.Fori(1, B - 2) as b:
                batch(b, False, False)
            batch(B - 2, False, False, True)
            batch(B - 1, False, True)
            values(B - 1, NQ - 1, NC - 1, False)

            def turn_back(g):
                pe.wait_ge(logitT_kept, g + 1)
                for n, t in enumerate(groups[g]):
                    mm = nc.tensor.transpose(ps_misc[:, t * E_:(t + 1) * E_], logitT[:, g % 2, n * P:(n + 1) * P],
                                             ident[0:E_, 0:E_])
                mm.then_inc(logits_made, 1)

            pe.wait_ge(R["loaded"], 80)
            pe.wait_ge(misc_kept, MISC0 + MISC * (B - 1) - 2 + NQ - 1)
            for i in range(2):
                pe.wait_ge(a_kept[i], 2 * NC + STEPS * B - 2 * NC)
            pe.wait_ge(exp_done, 64 * B)
            for g, tiles in enumerate(groups):
                for t in tiles:
                    pe.wait_ge(x2_made, t + 1)
                    if t >= 4:
                        pe.wait_ge(xT_kept, t - 3)
                    for c in range(KC):
                        mm = nc.tensor.transpose(ps_a[t // 2 % 2][:, t % 2, c * P:(c + 1) * P],
                                                 x[:, t, c * P:(c + 1) * P], ident[:])
                    mm.then_inc(xT_made, 1)
                if g >= 1:
                    turn_back(g - 1)
                pe.wait_ge(xT_kept, tiles[-1] + 1)
                if g >= 2:
                    pe.wait_ge(logitT_kept, g - 1)
                n = len(tiles) * P
                for c in range(KC):
                    mm = nc.tensor.matmul(ps_b[g % 2][0:E_, 0:n], R["w"][:, c, :], xT[:, g % 2, c, 0:n],
                                          start=(c == 0), stop=(c == KC - 1))
                mm.then_inc(logitT_made, 1)
            turn_back(len(groups) - 1)
TILES = (TOK * K_TOP + E_ * (P - 1)) // P
DUMMY = TOK


def router_buffers(nc, ctx):
    def sb(name, shape, dt=F32):
        return ctx.enter_context(nc.sbuf_tensor(name, shape, dt))

    return {
        "w": sb("rw", [P, KC, E_]), "b": sb("rb", [P, E_]),
        "before": sb("before", [P, P]), "iota_p": sb("iota_p", [P, 1]), "iota_f": sb("iota_f", [P, P]),
        "logits": sb("logits", [P, NT, E_]),
        "loaded": ctx.enter_context(nc.semaphore("router_loaded")),
    }


def load_router(sp, A, R):
    for dst, src in (("w", A["router_w"]), ("b", A["router_b"].to_broadcast([P, E_])), ("before", A["before"]),
                     ("iota_p", A["iota_p"]), ("iota_f", A["iota_f"])):
        sp.dma_start(R[dst][:], src).then_inc(R["loaded"], 16)


def route(nc, A, S, x, G, W, R):
    NP = NT * K_TOP
    with ExitStack() as ctx:
        def sb(name, shape, dt=F32):
            return ctx.enter_context(nc.sbuf_tensor(name, shape, dt))

        def sem(name):
            return ctx.enter_context(nc.semaphore(name))

        before, iota_p, iota_f, logits = R["before"], R["iota_p"], R["iota_f"], R["logits"]
        ones = sb("ones3", [P, P])
        again = sb("again", [P, E_, NT])
        top = sb("top", [P, NT, 8])
        top_i = sb("top_i", [P, NT, 8], U32)
        top_f = sb("top_f", [P, NP])
        gap = sb("gap", [P, NT, K_TOP])
        share = sb("share", [P, NT, K_TOP])
        total = sb("total", [P, NT])
        chosen = sb("chosen", [P, NP, E_])
        picked = sb("picked", [P, NP, E_])
        sel = sb("sel", [P, E_, NT])
        through = sb("through", [P, E_, NT])
        sofar = sb("sofar", [P, E_, NT])
        over = sb("over", [P, E_, E_])
        n_tiles = sb("n_tiles", [P, E_])
        tile_end = sb("tile_end", [P, E_])
        base = sb("base", [P, E_])
        place = sb("place", [P, NT, E_])
        slot = sb("slot", [P, NP])
        slot_i = sb("slot_i", [P, NP], I32)
        hi_i = sb("hi_i", [P, NP], I32)
        lo_i = sb("lo_i", [P, NP], I32)
        hi_f = sb("hi_f", [P, NP])
        lo_f = sb("lo_f", [P, NP])
        token1 = sb("token1", [P, NT])
        in_tile = sb("in_tile", [P, 2, K_TOP, P])
        of_tile = sb("of_tile", [P, 2, K_TOP, TILES])
        payload = sb("payload", [P, 2, K_TOP, 2, TILES])
        empty = sb("empty", [P, TILES])
        tok_f = sb("tok_f", [P, TILES])
        past = sb("past", [1, TILES, E_])
        expert_f = sb("expert_f", [1, TILES])
        new_f = sb("new_f", [1, TILES])
        zero = sb("zero3", [P, P])

        ps_r = ctx.enter_context(nc.psum_tensor("ps_r", [P, D], F32))
        ps_s = ctx.enter_context(nc.psum_tensor("ps_s", [P, D], F32))

        set_ = sem("set3")
        step = sem("route_step")
        gap_made, exp_made = sem("gap_made"), sem("exp_made")
        sel_made, rank_made = sem("sel_made"), sem("rank_made")
        of_tile_made, tokens_made, weights_made, spread_done = (
            sem("of_tile_made"), sem("tokens_made"), sem("weights_made"), sem("spread_done"))
        dummy_stored, acc_stored = sem("dummy_stored"), sem("acc_stored")

        block = ctx.enter_context(nc.Block())

        @block.sync
        def _(sp):
            load_weights(sp, A, W, 0)
            load_biases(sp, A, W, 0, 0)
            load_biases(sp, A, W, 1, 1)
            sp.dma_start(W["ident"][:], A["ident"]).then_inc(W["small_loaded"][1], 16)
            sp.dma_start(S["acc"][0:TOK, :].rearrange("(t p) d -> p t d", p=P), x[:]).then_inc(acc_stored, 16)
            sp.wait_ge(set_, 2)
            zeros = zero[:].unsqueeze(1).to_broadcast([P, KC, P])
            sp.dma_start(S["x2"][TOK:TOK + P, :].rearrange("p (c d) -> p c d", c=KC), zeros).then_inc(dummy_stored, 16)
            sp.dma_start(S["acc"][TOK:TOK + P, :].rearrange("p (c d) -> p c d", c=KC), zeros).then_inc(dummy_stored, 16)
            sp.wait_ge(W["hi"], 3)
            sp.wait_ge(W["lo"], 3)
            load_weights(sp, A, W, 1)
            sp.wait_ge(dummy_stored, 32)
            sp.wait_ge(acc_stored, 16)

        @block.gpsimd
        def _(pool):
            nc.gpsimd.memset(ones[:], 1.0).then_inc(set_, 1)
            nc.gpsimd.memset(zero[:], 0.0).then_inc(set_, 1)
            for k in range(3):
                split_lo(nc, pool, W, 0, 0, k)

        @block.scalar
        def _(act):
            act.wait_ge(gap_made, 1)
            nc.scalar.activation(share[:], gap[:], ACT.Exp).then_inc(exp_made, 1)
            for k in range(3):
                split_hi(nc, act, W, 0, 0, k)
            for t in range(NT):
                act.wait_ge(of_tile_made, t + 1)
                if t >= 2:
                    act.wait_ge(spread_done, t - 1)
                nc.scalar.activation(payload[:, t % 2, :, 0], of_tile[:, t % 2], ACT.Copy,
                                     scale=token1[:, t:t + 1]).then_inc(tokens_made, 1)

        @block.vector
        def _(dve):
            done = [0]

            def chain(instruction):
                done[0] += 1
                instruction.then_inc(step, 1)
                dve.wait_ge(step, done[0])

            dve.wait_ge(set_, 2)
            chain(nc.vector.memset(again[:], 1.0))
            nc.vector.memset(again[:, :, 0:1], 0.0)
            for t in range(NT):
                last = nc.vector.max(top[:, t], logits[:, t])
            chain(last)
            for t in range(NT):
                last = nc.vector.max_index(top_i[:, t], top[:, t], logits[:, t])
            nc.vector.tensor_tensor(gap[:], top[:, :, 0:K_TOP], top[:, :, 0:1].to_broadcast([P, NT, K_TOP]),
                                    ALU.subtract).then_inc(gap_made, 1)
            chain(last)
            chain(nc.vector.tensor_copy(top_f[:].rearrange("p (t k) -> p t k", t=NT), top_i[:, :, 0:K_TOP]))
            chain(nc.vector.tensor_tensor(chosen[:], iota_f[:, 0:E_].unsqueeze(1).to_broadcast([P, NP, E_]),
                                          top_f[:].unsqueeze(2).to_broadcast([P, NP, E_]), ALU.is_equal))
            chain(nc.vector.tensor_reduce(sel[:].rearrange("p e t -> p t e"),
                                          chosen[:].rearrange("p (t k) e -> p t e k", k=K_TOP), AX.X, ALU.add))
            chain(nc.vector.tensor_tensor_scan(through[:].rearrange("p e t -> p (e t)"),
                                               again[:].rearrange("p e t -> p (e t)"),
                                               sel[:].rearrange("p e t -> p (e t)"), 0.0, ALU.mult, ALU.add))
            nc.vector.tensor_tensor(sofar[:], through[:], sel[:], ALU.subtract).then_inc(sel_made, 1)
            chain(nc.vector.tensor_scalar(token1[:], iota_f[:, 0:NT], float(P), iota_p[:, 0:1], ALU.mult, ALU.add))
            chain(nc.vector.tensor_scalar(token1[:], token1[:], 1.0, None, ALU.add))
            dve.wait_ge(exp_made, 1)
            chain(nc.vector.tensor_reduce(total[:], share[:], AX.X, ALU.add))
            chain(nc.vector.reciprocal(total[:], total[:]))
            chain(nc.vector.tensor_tensor(share[:], share[:], total[:].unsqueeze(2).to_broadcast([P, NT, K_TOP]),
                                          ALU.mult))
            dve.wait_ge(rank_made, 1)
            chain(nc.vector.tensor_copy(base[:], ps_r[:, NT * E_:(NT + 1) * E_]))
            chain(nc.vector.scalar_tensor_tensor(over[:], iota_f[:, 0:E_].unsqueeze(1).to_broadcast([P, E_, E_]),
                                                 float(P), base[:].unsqueeze(2).to_broadcast([P, E_, E_]),
                                                 ALU.mult, ALU.is_lt))
            chain(nc.vector.tensor_reduce(n_tiles[:], over[:], AX.X, ALU.add))
            chain(nc.vector.tensor_scalar(n_tiles[:], n_tiles[:], 1.0, None, ALU.max))
            chain(nc.vector.tensor_tensor_scan(tile_end[:], ones[:, 0:E_], n_tiles[:], 0.0, ALU.mult, ALU.add))
            chain(nc.vector.tensor_tensor(base[:], tile_end[:], n_tiles[:], ALU.subtract))
            chain(nc.vector.tensor_scalar(base[:], base[:], float(P), None, ALU.mult))
            chain(nc.vector.tensor_tensor(place[:], ps_r[:, 0:NT * E_].rearrange("p (e t) -> p t e", t=NT),
                                          base[:].unsqueeze(1).to_broadcast([P, NT, E_]), ALU.add))
            chain(nc.vector.tensor_tensor(picked[:].rearrange("p (t k) e -> p t k e", k=K_TOP),
                                          chosen[:].rearrange("p (t k) e -> p t k e", k=K_TOP),
                                          place[:].unsqueeze(2).to_broadcast([P, NT, K_TOP, E_]), ALU.mult))
            chain(nc.vector.tensor_reduce(slot[:], picked[:], AX.X, ALU.add))
            chain(nc.vector.tensor_copy(slot_i[:], slot[:]))
            nc.vector.tensor_scalar(hi_i[:], slot_i[:], 7, None, ALU.logical_shift_right)
            chain(nc.vector.tensor_scalar(lo_i[:], slot_i[:], P - 1, None, ALU.bitwise_and))
            nc.vector.tensor_copy(hi_f[:], hi_i[:])
            chain(nc.vector.tensor_copy(lo_f[:], lo_i[:]))
            for t in range(NT):
                s, kk = t % 2, slice(K_TOP * t, K_TOP * t + K_TOP)
                if t >= 2:
                    dve.wait_ge(spread_done, t - 1)
                    dve.wait_ge(tokens_made, t - 1)
                nc.vector.tensor_tensor(of_tile[:, s], iota_f[:, 0:TILES].unsqueeze(1).to_broadcast(
                    [P, K_TOP, TILES]), hi_f[:, kk].unsqueeze(2).to_broadcast([P, K_TOP, TILES]),
                    ALU.is_equal).then_inc(of_tile_made, 1)
                nc.vector.tensor_tensor(in_tile[:, s], iota_f[:].unsqueeze(1).to_broadcast([P, K_TOP, P]),
                                        lo_f[:, kk].unsqueeze(2).to_broadcast([P, K_TOP, P]), ALU.is_equal)
                dve.wait_ge(of_tile_made, t + 1)
                nc.vector.tensor_tensor(payload[:, s, :, 1], of_tile[:, s], share[:, t].unsqueeze(2).to_broadcast(
                    [P, K_TOP, TILES]), ALU.mult).then_inc(weights_made, 1)
            chain(nc.vector.tensor_tensor(past[:], tile_end[0:1].unsqueeze(1).to_broadcast([1, TILES, E_]),
                                          iota_f[0:1, 0:TILES].unsqueeze(2).to_broadcast([1, TILES, E_]), ALU.is_le))
            chain(nc.vector.tensor_reduce(expert_f[:], past[:], AX.X, ALU.add))
            chain(nc.vector.tensor_scalar(new_f[:], expert_f[:], float(E_), None, ALU.is_lt))
            chain(nc.vector.tensor_copy(G["active"][:], new_f[:]))
            chain(nc.vector.tensor_scalar(expert_f[:], expert_f[:], float(E_ - 1), None, ALU.min))
            chain(nc.vector.tensor_copy(G["expert"][:], expert_f[:]))
            chain(nc.vector.tensor_scalar(G["parity"][:], G["expert"][:], 1, None, ALU.bitwise_and))
            chain(nc.vector.memset(new_f[:], 1.0))
            chain(nc.vector.tensor_tensor(new_f[:, 1:], expert_f[:, 1:], expert_f[:, :-1], ALU.not_equal))
            chain(nc.vector.scalar_tensor_tensor(new_f[:], expert_f[:], float(E_ - 1), new_f[:], ALU.is_lt, ALU.mult))
            chain(nc.vector.tensor_copy(G["new"][:], new_f[:]))
            chain(nc.vector.tensor_scalar(G["last_tile"][:], tile_end[0:1], -1.0, None, ALU.add))
            dve.wait_ge(spread_done, NT)
            chain(nc.vector.tensor_scalar(empty[:], ps_s[:, 0:TILES], 0.0, None, ALU.is_equal))
            chain(nc.vector.tensor_scalar(iota_p[:], iota_p[:], float(DUMMY + 1), None, ALU.add))
            chain(nc.vector.tensor_scalar(empty[:], empty[:], iota_p[:, 0:1], -1.0, ALU.mult, ALU.add))
            chain(nc.vector.tensor_tensor(tok_f[:], ps_s[:, 0:TILES], empty[:], ALU.add))
            chain(nc.vector.tensor_copy(G["token"][:], tok_f[:]))
            chain(nc.vector.tensor_copy(G["weight"][:], ps_s[:, TILES:2 * TILES]))

        @block.tensor
        def _(pe):
            pe.wait_ge(sel_made, 1)
            nc.tensor.matmul(ps_r[:, 0:NT * E_], before[:], sel[:].rearrange("p e t -> p (e t)"),
                             start=True, stop=False, skip_group_check=True)
            nc.tensor.matmul(ps_r[:, 0:NT * E_], ones[:], sofar[:].rearrange("p e t -> p (e t)"),
                             start=False, stop=True, skip_group_check=True)
            nc.tensor.matmul(ps_r[:, NT * E_:(NT + 1) * E_], ones[:], through[:, :, NT - 1], start=False, stop=True,
                             skip_group_check=True).then_inc(rank_made, 1)
            for t in range(NT):
                pe.wait_ge(tokens_made, t + 1)
                pe.wait_ge(weights_made, t + 1)
                for k in range(K_TOP):
                    mm = nc.tensor.matmul(ps_s[:, 0:2 * TILES], in_tile[:, t % 2, k],
                                          payload[:, t % 2, k].rearrange("p a t -> p (a t)"),
                                          start=(t == 0 and k == 0), stop=(t == NT - 1 and k == K_TOP - 1))
                mm.then_inc(spread_done, 1)


def weight_buffers(nc, ctx):
    def sb(name, shape, dt=F32):
        return ctx.enter_context(nc.sbuf_tensor(name, shape, dt))

    def sem(name):
        return ctx.enter_context(nc.semaphore(name))

    return {
        "raw": sb("we_raw", [P, 3, KC, D]),
        "split": sb("we_split", [P, 2, 3, 2, KC, D], F32R),
        "bias": sb("we_bias", [P, 2, 3 * D]),
        "ident": sb("ident4", [P, P]),
        "loaded": sem("we_loaded"), "hi": sem("we_hi"), "lo": sem("we_lo"),
        "small_loaded": [sem("be_loaded0"), sem("be_loaded1")],
    }


def load_weights(sp, A, W, e):
    sp.dma_start(W["raw"][:], A["w_expert"][e] if isinstance(e, int) else
                 A["w_expert"][bass.ds(e, 1)].squeeze(0)).then_inc(W["loaded"], 16)


def load_biases(sp, A, W, e, s):
    sp.dma_start(W["bias"][:, s], (A["b_expert"][e:e + 1] if isinstance(e, int) else
                                   A["b_expert"][bass.ds(e, 1)]).to_broadcast([P, 3 * D])).then_inc(
        W["small_loaded"][s], 16)


def split_hi(nc, act, W, e, slot, k):
    dst = W["split"][:, bass.ds(slot, 1), k, 0].squeeze(1)
    act.wait_ge(W["loaded"], 16 * e + 16)
    nc.scalar.activation(dst, W["raw"][:, k], ACT.Copy).then_inc(W["hi"], 1)


def split_lo(nc, pool, W, e, slot, k, wait=None):
    hi, lo = (W["split"][:, bass.ds(slot, 1), k, part].squeeze(1) for part in range(2))
    (wait or pool.wait_ge)(W["hi"], 3 * e + k + 1)
    nc.gpsimd.tensor_tensor(lo, W["raw"][:, k], hi, ALU.subtract).then_inc(W["lo"], 1)


def experts(nc, A, S, G, W):
    U = 4
    ROUNDS = TILES // U * U
    LIMIT, ALPHA = 7.0, 1.702
    GATE, UP, DOWN = range(3)
    with ExitStack() as ctx:
        def sb(name, shape, dt=F32):
            return ctx.enter_context(nc.sbuf_tensor(name, shape, dt))

        def sem(name):
            return ctx.enter_context(nc.semaphore(name))

        ident, w, bias = W["ident"], W["split"], W["bias"]
        zero_row = sb("zero_row", [P, 1])
        from_rows = [sb(f"from_rows{i}", [P, 1], U32) for i in range(U)]
        to_rows = sb("to_rows", [P, 1], U32)
        x_rows = [sb(f"x_rows{i}", [P, D]) for i in range(U)]
        xT = sb("xT4", [P, 2, 2, KC, P], F32R)
        gate = sb("gate", [P, D])
        up = sb("up", [P, D])
        sig = sb("sig", [P, D])
        h = sb("h", [P, D])
        hT = sb("hT", [P, 2, KC, P], F32R)
        y = [sb(f"y{i}", [P, D]) for i in range(U)]

        def bank(name):
            return ctx.enter_context(nc.psum_tensor(name, [P, D], F32))

        ps_g, ps_u, ps_x, ps_h, ps_y = bank("ps_g"), bank("ps_u2"), bank("ps_x"), bank("ps_h"), bank("ps_y")

        from_set, to_set = sem("from_set"), sem("to_set")
        tables_read = sem("tables_read")
        gathered = [sem(f"gathered{i}") for i in range(U)]
        x_turned, xT_hi, xT_lo = sem("xe_turned"), sem("xeT_hi"), sem("xeT_lo")
        g_made, u_made, g_kept, u_kept = sem("g_made"), sem("ue_made"), sem("g_kept"), sem("ue_kept")
        g_cut, u_cut, gated, sig_made, h_made = sem("g_cut"), sem("u_cut"), sem("gated"), sem("sig_made"), sem("h_made")
        h_turned, hT_hi, hT_lo = sem("h_turned"), sem("hT_hi"), sem("hT_lo")
        y_made, y_biased, y_ready = sem("ye_made"), sem("y_biased"), sem("y_ready")
        added = sem("added")

        block = ctx.enter_context(nc.Block())

        def loop(engine, body, end):
            for j in range(U):
                body(j, j)
            with engine.Fori(1, TILES // U) as r:
                for j in range(U):
                    body(U * r + j, j)
            more = engine.value_load(G["active"][:, ROUNDS:ROUNDS + 1], min_val=0, max_val=1)
            with engine.If(more == 1):
                for i in range(ROUNDS, TILES):
                    body(i, i % U)
                end(TILES - 1)
            with engine.If(more == 0):
                end(ROUNDS - 1)

        def is_at(i, n):
            return isinstance(i, int) and i == n

        def below(i, n):
            return isinstance(i, int) and i < n

        def pick(table, i):
            return table[:, i:i + 1] if isinstance(i, int) else table[:, bass.ds(i, 1)]

        def four(psum):
            return psum[:].rearrange("p (c t) -> p c t", c=KC)

        @block.sync
        def _(sp):
            def follow(e, s):
                sp.wait_ge(W["hi"], 3 * e)
                sp.wait_ge(W["lo"], 3 * e)
                load_weights(sp, A, W, e)
                last = sp.value_load(G["last_tile"][:, bass.ds(e - 2, 1)], min_val=0, max_val=TILES - 1)
                sp.wait_ge(y_biased, last + 1)
                load_biases(sp, A, W, e, s)

            with sp.Fori(1, E_ // 2) as r:
                for s in range(2):
                    follow(2 * r + s, s)

        @block.gpsimd
        def _(pool):
            held = spare_registers(pool, "held4", 2)

            def gather(i, j):
                if not below(i, U):
                    pool.wait_ge(x_turned, i - U + 1)
                nc.gpsimd.tensor_copy(from_rows[j][:], pick(G["token"], i)).then_inc(from_set, 1)
                wait_apart(pool, held, (tables_read, 1), (from_set, i + 1))
                pool.indirect_dma_start(x_rows[j][:], None, S["x2"], bass.IndirectOffsetOnAxis(from_rows[j][:], 0))\
                    .then_inc(gathered[j], 16)

            def scatter(i, j):
                if not is_at(i, 0):
                    pool.wait_ge(added, 16 * i)
                nc.gpsimd.tensor_copy(to_rows[:], pick(G["token"], i)).then_inc(to_set, 1)
                wait_apart(pool, held, (tables_read, 1), (to_set, i + 1), (y_ready, i + 1))
                pool.indirect_dma_start(S["acc"], bass.IndirectOffsetOnAxis(to_rows[:], 0), y[j][:], None,
                                        compute_op=ALU.add).then_inc(added, 16)

            def split_next(i, kinds):
                new = pool.value_load(pick(G["new"], i), min_val=0, max_val=1)
                with pool.If(new == 1):
                    e = pool.value_load(pick(G["expert"], i), min_val=0, max_val=E_ - 2)
                    par = pool.value_load(pick(G["parity"], i), min_val=0, max_val=1)
                    for k in kinds:
                        split_lo(nc, pool, W, e + 1, 1 - par, k,
                                 lambda semaphore, value: wait_apart(pool, held, (tables_read, 1), (semaphore, value)))

            nc.gpsimd.memset(zero_row[:], 0.0).then_inc(tables_read, 1)
            for j in range(3):
                gather(j, j)

            def body(i, j):
                if not (isinstance(i, int) and i >= TILES - 3):
                    gather(i + 3, (j + 3) % U)
                if not below(i, 2):
                    scatter(i - 2, (j - 2) % U)
                if not is_at(i, 0):
                    split_next(i - 1, (DOWN,))
                split_next(i, (GATE, UP))

            def end(i):
                scatter(i - 1, (i - 1) % U)
                scatter(i, i % U)
                pool.wait_ge(added, 16 * i + 16)

            loop(pool, body, end)
            for j in range(U):
                pool.wait_ge(gathered[j], 16 * len(range(j, TILES, U)))

        @block.scalar
        def _(act):
            def x_hi(i, j):
                act.wait_ge(x_turned, i + 1)
                if not below(i, 2):
                    act.wait_ge(u_made, i - 1)
                nc.scalar.activation(xT[:, j % 2, 0], four(ps_x), ACT.Copy).then_inc(xT_hi, 1)

            def h_hi(i):
                act.wait_ge(h_turned, i + 1)
                if not is_at(i, 0):
                    act.wait_ge(y_made, i)
                nc.scalar.activation(hT[:, 0], four(ps_h), ACT.Copy).then_inc(hT_hi, 1)

            def split_next(i):
                new = act.value_load(pick(G["new"], i), min_val=0, max_val=1)
                with act.If(new == 1):
                    e = act.value_load(pick(G["expert"], i), min_val=0, max_val=E_ - 2)
                    par = act.value_load(pick(G["parity"], i), min_val=0, max_val=1)
                    for k in (GATE, UP, DOWN):
                        if not is_at(i, 0):
                            act.wait_ge(y_made if k == DOWN else u_made, i)
                        split_hi(nc, act, W, e + 1, 1 - par, k)

            x_hi(0, 0)

            def body(i, j):
                if not is_at(i, 0):
                    h_hi(i - 1)
                act.wait_ge(g_cut, i + 1)
                if not is_at(i, 0):
                    act.wait_ge(h_made, i)
                nc.scalar.activation(sig[:], gate[:], ACT.Sigmoid, scale=ALPHA).then_inc(sig_made, 1)
                if not is_at(i, TILES - 1):
                    x_hi(i + 1, j + 1)
                split_next(i)

            loop(act, body, h_hi)

        @block.vector
        def _(dve):
            def x_lo(i, j):
                dve.wait_ge(xT_hi, i + 1)
                nc.vector.tensor_tensor(xT[:, j % 2, 1], four(ps_x), xT[:, j % 2, 0], ALU.subtract).then_inc(xT_lo, 1)

            def h_lo(i):
                dve.wait_ge(hT_hi, i + 1)
                nc.vector.tensor_tensor(hT[:, 1], four(ps_h), hT[:, 0], ALU.subtract).then_inc(hT_lo, 1)

            def biases(i):
                par = dve.value_load(pick(G["parity"], i), min_val=0, max_val=1)
                return lambda k: bias[:, bass.ds(par, 1), k * D:(k + 1) * D].squeeze(1)

            def finish(i, j):
                b = biases(i)
                dve.wait_ge(y_made, i + 1)
                if not below(i, U - 1):
                    dve.wait_ge(added, 16 * (i - U + 2))
                nc.vector.tensor_tensor(y[j][:], ps_y[:], b(DOWN), ALU.add).then_inc(y_biased, 1)
                dve.wait_ge(y_biased, i + 1)
                nc.vector.tensor_scalar(y[j][:], y[j][:], pick(G["weight"], i), None, ALU.mult).then_inc(y_ready, 1)

            x_lo(0, 0)

            def body(i, j):
                b = biases(i)
                dve.wait_ge(g_made, i + 1)
                if not is_at(i, 0):
                    dve.wait_ge(h_made, i)
                nc.vector.tensor_tensor(gate[:], ps_g[:], b(GATE), ALU.add).then_inc(g_kept, 1)
                dve.wait_ge(g_kept, i + 1)
                nc.vector.tensor_scalar(gate[:], gate[:], LIMIT, None, ALU.min).then_inc(g_cut, 1)
                if not is_at(i, 0):
                    h_lo(i - 1)
                dve.wait_ge(u_made, i + 1)
                nc.vector.tensor_tensor(up[:], ps_u[:], b(UP), ALU.add).then_inc(u_kept, 1)
                dve.wait_ge(u_kept, i + 1)
                nc.vector.tensor_scalar(up[:], up[:], LIMIT, -LIMIT, ALU.min, ALU.max).then_inc(u_cut, 1)
                if not is_at(i, TILES - 1):
                    x_lo(i + 1, j + 1)
                dve.wait_ge(u_cut, i + 1)
                dve.wait_ge(g_cut, i + 1)
                nc.vector.scalar_tensor_tensor(up[:], up[:], 1.0, gate[:], ALU.add, ALU.mult).then_inc(gated, 1)
                dve.wait_ge(gated, i + 1)
                dve.wait_ge(sig_made, i + 1)
                if not is_at(i, 0):
                    dve.wait_ge(h_turned, i)
                nc.vector.tensor_tensor(h[:], up[:], sig[:], ALU.mult).then_inc(h_made, 1)
                if not is_at(i, 0):
                    finish(i - 1, (j - 1) % U)

            def end(i):
                h_lo(i)
                finish(i, i % U)

            loop(dve, body, end)

        @block.tensor
        def _(pe):
            def transposes(out, rows):
                for c in range(KC):
                    mm = nc.tensor.transpose(out[:, c * P:(c + 1) * P], rows[:, c * P:(c + 1) * P], ident[:])
                return mm

            def turn_x(i, j):
                pe.wait_ge(gathered[j], 16 // U * (i - j) + 16)
                if not is_at(i, 0):
                    pe.wait_ge(xT_lo, i)
                transposes(ps_x, x_rows[j]).then_inc(x_turned, 1)

            def turn_h(i):
                pe.wait_ge(h_made, i + 1)
                if not is_at(i, 0):
                    pe.wait_ge(hT_lo, i)
                transposes(ps_h, h).then_inc(h_turned, 1)

            def products(out, left, par, k):
                passes = [(c, a, b) for c in range(KC) for a, b in SPLITS]
                for n, (c, a, b) in enumerate(passes):
                    mm = nc.tensor.matmul(out[:], left[:, a, c], w[:, bass.ds(par, 1), k, b, c].squeeze(1),
                                          start=(n == 0), stop=(n == len(passes) - 1))
                return mm

            def down(i):
                e = pe.value_load(pick(G["expert"], i), min_val=0, max_val=E_ - 1)
                par = pe.value_load(pick(G["parity"], i), min_val=0, max_val=1)
                pe.wait_ge(W["hi"], 3 * e + 3)
                pe.wait_ge(W["lo"], 3 * e + 3)
                pe.wait_ge(hT_lo, i + 1)
                if not is_at(i, 0):
                    pe.wait_ge(y_biased, i)
                products(ps_y, hT, par, DOWN).then_inc(y_made, 1)

            pe.wait_ge(W["small_loaded"][0], 16)
            pe.wait_ge(W["small_loaded"][1], 32)
            turn_x(0, 0)

            def body(i, j):
                e = pe.value_load(pick(G["expert"], i), min_val=0, max_val=E_ - 1)
                par = pe.value_load(pick(G["parity"], i), min_val=0, max_val=1)
                pe.wait_ge(W["hi"], 3 * e + 2)
                pe.wait_ge(W["lo"], 3 * e + 2)
                pe.wait_ge(W["small_loaded"][0], e // 2 * 16 + 16)
                pe.wait_ge(W["small_loaded"][1], (e + 1) // 2 * 16 + 16)
                pe.wait_ge(xT_lo, i + 1)
                if not is_at(i, 0):
                    pe.wait_ge(g_kept, i)
                products(ps_g, xT[:, j % 2], par, GATE).then_inc(g_made, 1)
                if not is_at(i, 0):
                    turn_h(i - 1)
                    pe.wait_ge(u_kept, i)
                products(ps_u, xT[:, j % 2], par, UP).then_inc(u_made, 1)
                if not is_at(i, TILES - 1):
                    turn_x(i + 1, (j + 1) % U)
                if not is_at(i, 0):
                    down(i - 1)

            def end(i):
                turn_h(i)
                down(i)

            loop(pe, body, end)


def last_norm(nc, S, out):
    with ExitStack() as ctx:
        def sb(name, shape, dt=F32):
            return ctx.enter_context(nc.sbuf_tensor(name, shape, dt))

        def sem(name):
            return ctx.enter_context(nc.semaphore(name))

        G4 = 2
        NG = NT // G4
        acc = sb("acc_sb", [P, NT, D])
        res = sb("res_sb", [P, NT, D])
        stats = sb("stats5", [P, NT, 6])
        mean_var = sb("mean_var5", [P, NT, 2])
        rstd = sb("rstd5", [P, NT])
        minus_half = sb("minus_half5", [P, NT])
        loaded = [sem(f"acc_loaded{i}") for i in range(NG)]
        stats_made, moments, var_eps, rstd_made, normed, stored, half_set = (
            sem("stats5_made"), sem("moments5"), sem("var_eps"), sem("rstd5_made"), sem("normed"), sem("stored"),
            sem("half5_set"))
        block = ctx.enter_context(nc.Block())

        @block.sync
        def _(sp):
            for g in range(NG):
                sp.dma_start(acc[:, G4 * g:G4 * g + G4], S["acc"][G4 * g * P:G4 * (g + 1) * P, :].rearrange(
                    "(t p) d -> p t d", p=P)).then_inc(loaded[g], 16)
            for g in range(NG):
                sp.wait_ge(normed, G4 * (g + 1))
                sp.dma_start(out[G4 * g * P:G4 * (g + 1) * P, :].rearrange("(t p) d -> p t d", p=P),
                             res[:, G4 * g:G4 * g + G4]).then_inc(stored, 16)
            sp.wait_ge(stored, 16 * NG)

        @block.gpsimd
        def _(pool):
            nc.gpsimd.memset(minus_half[:], -0.5).then_inc(half_set, 1)
            pool.wait_ge(half_set, 1)
            for g in range(NG):
                ts = slice(G4 * g, G4 * g + G4)
                pool.wait_ge(var_eps, g + 1)
                nc.gpsimd.tensor_tensor(rstd[:, ts], mean_var[:, ts, 1], minus_half[:, ts], ALU.pow).then_inc(
                    rstd_made, 1)

        @block.vector
        def _(dve):
            def moments_of(g):
                dve.wait_ge(loaded[g], 16)
                for t in range(G4 * g, G4 * g + G4):
                    nc.vector.bn_stats(stats[:, t], acc[:, t]).then_inc(stats_made, 1)
                dve.wait_ge(stats_made, G4 * (g + 1))
                for t in range(G4 * g, G4 * g + G4):
                    nc.vector.bn_aggr(mean_var[:, t], stats[:, t]).then_inc(moments, 1)
                dve.wait_ge(moments, G4 * (g + 1))
                ts = slice(G4 * g, G4 * g + G4)
                nc.vector.tensor_scalar(mean_var[:, ts, 1], mean_var[:, ts, 1], LN_EPS, None, ALU.add).then_inc(
                    var_eps, 1)

            def apply(g):
                dve.wait_ge(rstd_made, g + 1)
                for t in range(G4 * g, G4 * g + G4):
                    nc.vector.tensor_scalar(res[:, t], acc[:, t], mean_var[:, t, 0:1], rstd[:, t:t + 1],
                                            ALU.subtract, ALU.mult).then_inc(normed, 1)

            moments_of(0)
            for g in range(NG):
                if g + 1 < NG:
                    moments_of(g + 1)
                apply(g)


SCRATCH = {
    "parts": ([B, 2, 3, 16, 16, D], BF16),
    "rows_q": ([B, 9, D], BF16),
    "rows_k": ([B, 12, D], BF16),
    "max": ([B, 4, 3, 4 * D], BF16),
    "heads": ([B, 16, 2 * 16, D], F32),
    "inv": ([B, 16, D], F32),
    "x2": ([TOK + P, D], F32),
    "acc": ([TOK + P, D], F32),
}


def decoder_layer(nc, A, out):
    S = {name: nc.dram_tensor(f"scratch_{name}", shape, dt).ap() for name, (shape, dt) in SCRATCH.items()}
    with ExitStack() as ctx:
        def sb(name, shape, dt):
            return ctx.enter_context(nc.sbuf_tensor(name, shape, dt))

        G = {
            "token": sb("slot_token", [P, TILES], U32),
            "weight": sb("slot_weight", [P, TILES], F32),
            "expert": sb("tile_expert", [1, TILES], I32),
            "active": sb("tile_active", [1, TILES], I32),
            "new": sb("tile_new", [1, TILES], I32),
            "parity": sb("tile_parity", [1, TILES], I32),
            "last_tile": sb("expert_last", [1, E_], I32),
        }
        with ExitStack() as keep:
            x = keep.enter_context(nc.sbuf_tensor("x_keep", [P, NT, D], F32))
            R = router_buffers(nc, keep)
            ident = keep.enter_context(nc.sbuf_tensor("ident", [P, P], F32))
            with ExitStack() as early:
                stage = early.enter_context(nc.sbuf_tensor("stage", [P, 2 * KC * D], F32))
                V = attention_inputs(stage)
                consts_loaded = early.enter_context(nc.semaphore("consts2_loaded"))
                in_loaded = early.enter_context(nc.semaphore("in_loaded"))

                def prefetch(sp):
                    load_attention_inputs(sp, A, V, consts_loaded, in_loaded)

                linear_attention(nc, A, x, stage, ident, prefetch)
                cross_attention(nc, A, S, x, R, V, ident, consts_loaded, in_loaded)
            W = weight_buffers(nc, keep)
            route(nc, A, S, x, G, W, R)
            experts(nc, A, S, G, W)
        last_norm(nc, S, out)


def kernel(x, ctx_2048, mask_Bx1x2048_fk1, L0_attn_Wq, L0_attn_Wk, L0_attn_Wv, L0_attn_Wu, L0_attn_Wo,
           L0_xattn_Wq, L0_xattn_bq, L0_xattn_Wk, L0_xattn_bk, L0_xattn_Wv, L0_xattn_bv,
           L0_ffn_router_weight, L0_ffn_router_bias, L0_ffn_gate_up_proj, L0_ffn_gate_up_proj_bias,
           L0_ffn_down_proj, L0_ffn_down_proj_bias):
    import numpy as np
    import concourse.bacc as bacc
    from concourse.bass_utils import run_bass_kernel_spmd

    def rows_in(w):
        w = np.asarray(w)
        return w.reshape(-1, P, w.shape[-1]).transpose(1, 0, 2)

    tokens = np.asarray(x).reshape(TOK, D)
    mask = np.asarray(mask_Bx1x2048_fk1).reshape(B, D)
    gate_up, down = np.asarray(L0_ffn_gate_up_proj), np.asarray(L0_ffn_down_proj)
    gate_up_b = np.asarray(L0_ffn_gate_up_proj_bias)
    arrays = {
        "x": tokens,
        "xT": rows_in(tokens.T),
        "w1": np.stack([rows_in(w) for w in (L0_attn_Wq, L0_attn_Wk, L0_attn_Wv, L0_attn_Wu, L0_attn_Wo)]),
        "w2": np.stack([rows_in(np.asarray(w).T) for w in (L0_xattn_Wq, L0_xattn_Wk, L0_xattn_Wv)]),
        "bias_qk": np.stack([np.asarray(b).reshape(2, P).T for b in (L0_xattn_bq, L0_xattn_bk)], 1),
        "bias_v": np.asarray(L0_xattn_bv).reshape(1, 2 * P),
        "ctx": np.asarray(ctx_2048).reshape(B, 2, P, D).transpose(0, 2, 1, 3),
        "mask": mask,
        "mask_col": mask.reshape(B, 4, P).transpose(2, 0, 1),
        "router_w": rows_in(np.asarray(L0_ffn_router_weight).T),
        "router_b": np.asarray(L0_ffn_router_bias).reshape(1, E_),
        "w_expert": np.stack([gate_up[:, :, ::2], gate_up[:, :, 1::2], down], 1).reshape(
            E_, 3, KC, P, D).transpose(0, 3, 1, 2, 4),
        "b_expert": np.concatenate([gate_up_b[:, ::2], gate_up_b[:, 1::2], np.asarray(L0_ffn_down_proj_bias)], 1),
        "ident": np.eye(P, dtype=np.float32),
        "kv_mask": np.kron(np.eye(4), np.ones((32, 32))).astype(np.float32),
        "before": np.triu(np.ones((P, P), np.float32), 1),
        "iota_p": np.arange(P, dtype=np.float32).reshape(P, 1),
        "iota_f": np.tile(np.arange(P, dtype=np.float32), (P, 1)),
    }
    nc = bacc.Bacc("TRN2", target_bir_lowering=False, num_devices=1)
    ins, aps = {}, {}
    for name, a in arrays.items():
        ins[f"in_{name}"] = np.ascontiguousarray(a)
        aps[name] = nc.dram_tensor(f"in_{name}", a.shape, F32, kind="ExternalInput").ap()
    out = nc.dram_tensor("out", [TOK, D], F32, kind="ExternalOutput").ap()
    decoder_layer(nc, aps, out)
    r = run_bass_kernel_spmd(nc, [ins], core_ids=[0])
    return r.results[0]["out"].reshape(B, L, D)
```
